# Optimizing a Trainium2 kernel written in Bass

```python
import numpy as np
import jax
import jax.numpy as jnp

def _softmax(x, axis=-1):
    return jax.nn.softmax(x, axis=axis)

def _gelu(x):
    return jax.nn.gelu(x, approximate=True)

def _silu(x):
    return jax.nn.silu(x)

def _sigmoid(x):
    return jax.nn.sigmoid(x)

def _layernorm(x, axis=-1, eps=1e-05):
    m = jnp.mean(x, axis=axis, keepdims=True)
    v = jnp.var(x, axis=axis, keepdims=True)
    return (x - m) / jnp.sqrt(v + eps)

def _scatter_add(tgt, idx, src, axis=0):
    return tgt.at[idx].add(src)

def _segment_sum(src, seg, n):
    return jax.ops.segment_sum(src, seg, n)
kernel_name = 'mk_decoder_preln_d2_seqx_r8_73dbb5'

def setup_inputs(seed: int=0):
    np.random.seed(seed)
    _w = jnp.asarray

    def _rec_inputs():
        import jax
        import jax.numpy as jnp
        _rk = jax.random.key(seed)
        x = -0.0005207 + 1.001 * jax.random.normal(jax.random.fold_in(_rk, 1), (16, 56, 256), jnp.float32)
        _lenS = 56 - jax.random.randint(jax.random.fold_in(_rk, 7), (16,), 0, max(1, 56 // 4) + 1, jnp.int32)
        _lenS2 = 1500 - jax.random.randint(jax.random.fold_in(_rk, 8), (16,), 0, max(1, 1500 // 4) + 1, jnp.int32)
        _ctx_2048P = jax.random.normal(jax.random.fold_in(_rk, 12), (16, 16, 256), jnp.float32)
        _ctx_2048c = jax.random.dirichlet(jax.random.fold_in(_rk, 512), 0.3 * jnp.ones((16,), jnp.float32), (16, 1500))
        _ctx_2048t = jnp.einsum('bsk,bkd->bsd', _ctx_2048c, _ctx_2048P)
        _ctx_2048t = _ctx_2048t * jax.lax.rsqrt(jnp.mean(jnp.square(_ctx_2048t)) + 1e-12) * 0.953939
        ctx_2048 = -5.72187e-05 + 0.999849 * (_ctx_2048t + 0.3 * jax.random.normal(jax.random.fold_in(_rk, 612), (16, 1500, 256), jnp.float32))
        _validS = jnp.arange(56)[None, :] < _lenS[:, None]
        _validS2 = jnp.arange(1500)[None, :] < _lenS2[:, None]
        _causal = jnp.tril(jnp.ones((56, 56), dtype=bool))
        mask_BxSx4224_bf0 = jnp.logical_not(jnp.ones((16, 56, 528), dtype=bool))
        return (x, ctx_2048, mask_BxSx4224_bf0)
    x, ctx_2048, mask_BxSx4224_bf0 = _rec_inputs()

    def _L0_attn_setup():
        import jax, jax.numpy as jnp
        import numpy as np
        HID = 256
        NK, DK = (16, 128)
        NV, DV = (32, 128)
        KC = 4
        P = NV // NK
        SV = P * DV
        QD = NK * DK
        VD = NV * DV
        QKV = QD + QD + VD
        B, T = (2, 256)
        EPS_NORM = 1e-12
        EPS_RMS = 1e-06

        def _l2norm(x):
            n = jnp.sqrt(jnp.sum(x * x, axis=-1, keepdims=True))
            return x / jnp.maximum(n, EPS_NORM)

        def _reference_tuple_inner(x, W_qkv, W_z, W_b, W_a, conv_w, dt_bias, A_log, norm_w, W_out):
            Bq, Tq, _ = x.shape
            qkv = jnp.einsum('btc,dc->btd', x, W_qkv)
            z = jnp.einsum('btc,dc->btd', x, W_z)
            beta = jax.nn.sigmoid(jnp.einsum('btc,hc->bth', x, W_b))
            dt = jax.nn.softplus(jnp.einsum('btc,hc->bth', x, W_a) + dt_bias)
            decay = jnp.exp(-dt * jnp.exp(A_log))
            xp = jnp.pad(qkv, ((0, 0), (KC - 1, 0), (0, 0)))
            qkv_c = sum((xp[:, j:j + Tq, :] * conv_w[:, j] for j in range(KC)))
            new_conv_buf = jnp.transpose(xp[:, -(KC - 1):, :], (0, 2, 1))
            q = _l2norm(qkv_c[..., :QD].reshape(Bq, Tq, NK, DK))
            k = _l2norm(qkv_c[..., QD:2 * QD].reshape(Bq, Tq, NK, DK))
            v = qkv_c[..., 2 * QD:].reshape(Bq, Tq, NK, P, DV)
            beta_r = beta.reshape(Bq, Tq, NK, P)
            decay_r = decay.reshape(Bq, Tq, NK, P)
            qT = jnp.swapaxes(q, 0, 1)
            kT = jnp.swapaxes(k, 0, 1)
            vT = jnp.swapaxes(v, 0, 1)
            bT = jnp.swapaxes(beta_r, 0, 1)
            dT = jnp.swapaxes(decay_r, 0, 1)

            def step(S, inp):
                q_t, k_t, v_t, b_t, d_t = inp
                Sk = jnp.einsum('bhi,bhipj->bhpj', k_t, S)
                dv = b_t[..., None] * (v_t - Sk)
                upd = jnp.einsum('bhi,bhpj->bhipj', k_t, dv)
                S = S * d_t[:, :, None, :, None] + upd
                o = jnp.einsum('bhi,bhipj->bhpj', q_t, S)
                return (S, o)
            S0 = jnp.zeros((Bq, NK, DK, P, DV), x.dtype)
            S_final, outs = jax.lax.scan(step, S0, (qT, kT, vT, bT, dT))
            out = jnp.swapaxes(outs, 0, 1).reshape(Bq, Tq, NV, DV)
            rms = jax.lax.rsqrt(jnp.mean(out * out, axis=-1, keepdims=True) + EPS_RMS)
            out = out * rms * norm_w
            out = out.reshape(Bq, Tq, VD) * jax.nn.silu(z)
            y = jnp.einsum('btd,cd->btc', out, W_out)
            return (y, S_final.reshape(Bq, NK, DK, SV), new_conv_buf)
        key = jax.random.key(seed)
        ks = jax.random.split(key, 8)
        lin = lambda k, o, i: jax.random.normal(k, (o, i), jnp.float32) / np.sqrt(i).astype(np.float32)
        return {'x': jax.random.normal(ks[0], (B, T, HID), jnp.float32), 'W_qkv': lin(ks[1], QKV, HID), 'W_z': lin(ks[2], VD, HID), 'W_b': lin(ks[3], NV, HID), 'W_a': lin(ks[4], NV, HID), 'conv_w': jax.random.normal(ks[5], (QKV, KC), jnp.float32) * 0.1, 'dt_bias': jnp.zeros((NV,), jnp.float32), 'A_log': jnp.zeros((NV,), jnp.float32), 'norm_w': jnp.ones((DV,), jnp.float32), 'W_out': lin(ks[6], HID, VD)}
    _L0_attn_all = _L0_attn_setup()
    _L0_attn_in = {k: v for k, v in _L0_attn_all.items() if k in ('W_qkv', 'W_z', 'W_b', 'W_a', 'conv_w', 'dt_bias', 'A_log', 'norm_w', 'W_out')}
    del _L0_attn_all

    def _L0_xattn_setup():
        import jax, jax.numpy as jnp
        import numpy as np
        import math
        DIM = 256
        B, Q_LEN, KV_LEN = (8, 128, 512)
        key = jax.random.key(seed)
        ks = jax.random.split(key, 8)
        x = jax.random.normal(ks[0], (B, Q_LEN, DIM), dtype=jnp.float32)
        mask = jnp.zeros((B, Q_LEN, KV_LEN + Q_LEN), dtype=bool)
        k_cache = jax.random.normal(ks[1], (B, KV_LEN, DIM), dtype=jnp.float32)
        v_cache = jax.random.normal(ks[2], (B, KV_LEN, DIM), dtype=jnp.float32)
        scale = 1.0 / math.sqrt(DIM)
        wq = jax.random.normal(ks[3], (DIM, DIM), dtype=jnp.float32) * scale
        wk = jax.random.normal(ks[4], (DIM, DIM), dtype=jnp.float32) * scale
        wv = jax.random.normal(ks[5], (DIM, DIM), dtype=jnp.float32) * scale
        wo = jax.random.normal(ks[6], (DIM, DIM), dtype=jnp.float32) * scale
        return {'x': x, 'mask': mask, 'k_cache': k_cache, 'v_cache': v_cache, 'wq': wq, 'wk': wk, 'wv': wv, 'wo': wo}
    _L0_xattn_all = _L0_xattn_setup()
    _L0_xattn_in = {k: v for k, v in _L0_xattn_all.items() if k in ('wq', 'wk', 'wv', 'wo')}
    del _L0_xattn_all

    def _L0_ffn_setup():
        import jax, jax.numpy as jnp
        import numpy as np
        B, S, D = (2, 256, 256)
        F = 512
        E, K = (8, 2)
        key = jax.random.key(seed)
        k0, k1, k2, k3, k4 = jax.random.split(key, 5)
        sc_d = 1.0 / np.sqrt(D)
        sc_f = 1.0 / np.sqrt(F)
        return {'hidden_states': jax.random.normal(k0, (B, S, D), jnp.float32), 'gate_w': jax.random.normal(k1, (E, D), jnp.float32) * sc_d, 'w1': jax.random.normal(k2, (E, F, D), jnp.float32) * sc_d, 'w2': jax.random.normal(k3, (E, D, F), jnp.float32) * sc_f, 'w3': jax.random.normal(k4, (E, F, D), jnp.float32) * sc_d}
    _L0_ffn_all = _L0_ffn_setup()
    _L0_ffn_in = {k: v for k, v in _L0_ffn_all.items() if k in ('gate_w', 'w1', 'w2', 'w3')}
    del _L0_ffn_all

    def _L1_attn_setup():
        import math
        import jax, jax.numpy as jnp
        import numpy as np
        HID = 256
        H = 16
        HKV = 8
        D = HID // H
        F = D
        SEQ = 256
        BATCH = 2
        THETA = 10000.0

        def _rotate_half(x):
            x1, x2 = (x[..., :x.shape[-1] // 2], x[..., x.shape[-1] // 2:])
            return jnp.concatenate((-x2, x1), axis=-1)

        def _softmax_kernel(x, R):
            n = jnp.sqrt(jnp.sum(x * x, axis=-1, keepdims=True))
            x = x / jnp.maximum(n, 1e-06)
            p = jnp.einsum('...d,ed->...e', x, R)
            feats = jnp.concatenate([jnp.sin(p), jnp.cos(p)], axis=-1)
            return feats / math.sqrt(F)
        key = jax.random.key(seed)
        ks = jax.random.split(key, 10)
        s = lambda k, shape, scale=0.02: jax.random.normal(k, shape, dtype=jnp.float32) * scale
        return {'hidden_states': jax.random.normal(ks[0], (BATCH, SEQ, HID), dtype=jnp.float32), 'Wq': s(ks[1], (HID, HID)), 'bq': s(ks[2], (HID,)), 'Wk': s(ks[3], (HKV * D, HID)), 'bk': s(ks[4], (HKV * D,)), 'Wv': s(ks[5], (HKV * D, HID)), 'bv': s(ks[6], (HKV * D,)), 'Wo': s(ks[7], (HID, HID)), 'bo': s(ks[8], (HID,)), 'rand_matrix': jax.random.normal(ks[9], (F // 2, D), dtype=jnp.float32)}
    _L1_attn_all = _L1_attn_setup()
    _L1_attn_in = {k: v for k, v in _L1_attn_all.items() if k in ('Wq', 'bq', 'Wk', 'bk', 'Wv', 'bv', 'Wo', 'bo', 'rand_matrix')}
    del _L1_attn_all

    def _L1_xattn_setup():
        import jax, jax.numpy as jnp
        import numpy as np
        HIDDEN = 256
        N_HEADS = 16
        N_KV_HEADS = 4
        HEAD_DIM = 128
        EPS = 1e-06

        def rms_norm(x, w, eps=EPS):
            xf = x.astype(jnp.float32)
            var = jnp.mean(xf * xf, axis=-1, keepdims=True)
            return w * (xf * jax.lax.rsqrt(var + eps)).astype(x.dtype)
        key = jax.random.key(seed)
        ks = jax.random.split(key, 8)
        B, S, S_ENC = (4, 256, 128)
        inner = N_HEADS * HEAD_DIM
        kv_dim = N_KV_HEADS * HEAD_DIM
        s = 0.02
        return {'hidden_states': jax.random.normal(ks[0], (B, S, HIDDEN), jnp.float32), 'encoder_hidden_states': jax.random.normal(ks[1], (B, S_ENC, HIDDEN), jnp.float32), 'Wq': jax.random.normal(ks[2], (HIDDEN, inner), jnp.float32) * s, 'Wk': jax.random.normal(ks[3], (HIDDEN, kv_dim), jnp.float32) * s, 'Wv': jax.random.normal(ks[4], (HIDDEN, kv_dim), jnp.float32) * s, 'Wo': jax.random.normal(ks[5], (inner, HIDDEN), jnp.float32) * s, 'q_norm_w': jnp.ones((HEAD_DIM,), jnp.float32), 'k_norm_w': jnp.ones((HEAD_DIM,), jnp.float32)}
    _L1_xattn_all = _L1_xattn_setup()
    _L1_xattn_in = {k: v for k, v in _L1_xattn_all.items() if k in ('Wq', 'Wk', 'Wv', 'Wo', 'q_norm_w', 'k_norm_w')}
    del _L1_xattn_all

    def _L1_ffn_setup():
        import jax, jax.numpy as jnp
        import numpy as np
        E, R, K = (8, 8, 2)
        D, F = (256, 1024)
        B, S = (2, 256)
        SCALING = 16.0 / 8.0

        def act(x):
            return jax.nn.gelu(x, approximate=True)
        key = jax.random.key(seed)
        ks = jax.random.split(key, 12)
        return {'hidden_states': jax.random.normal(ks[0], (B, S, D), jnp.float32), 'W_r': jax.random.normal(ks[1], (E, D), jnp.float32) * 0.02, 'b_r': jnp.zeros((E,), jnp.float32), 'W1': jax.random.normal(ks[2], (F, D), jnp.float32) * 0.02, 'b1': jnp.zeros((F,), jnp.float32), 'W2': jax.random.normal(ks[3], (D, F), jnp.float32) * 0.02, 'b2': jnp.zeros((D,), jnp.float32), 'A1': jax.random.normal(ks[4], (E, R, D), jnp.float32) * 0.02, 'B1': jax.random.normal(ks[5], (F, R) * 1 + ()).reshape(1, F, R).repeat(1, 0) * 0.0 + jax.random.normal(ks[5], (E, F, R), jnp.float32) * 0.02, 'A2': jax.random.normal(ks[6], (E, R, F), jnp.float32) * 0.02, 'B2': jax.random.normal(ks[7], (E, D, R), jnp.float32) * 0.02}
    _L1_ffn_all = _L1_ffn_setup()
    _L1_ffn_in = {k: v for k, v in _L1_ffn_all.items() if k in ('W_r', 'b_r', 'W1', 'b1', 'W2', 'b2', 'A1', 'B1', 'A2', 'B2')}
    del _L1_ffn_all
    return {'x': x, 'ctx_2048': ctx_2048, 'mask_BxSx4224_bf0': mask_BxSx4224_bf0, 'L0_attn_W_qkv': _L0_attn_in['W_qkv'], 'L0_attn_W_z': _L0_attn_in['W_z'], 'L0_attn_W_b': _L0_attn_in['W_b'], 'L0_attn_W_a': _L0_attn_in['W_a'], 'L0_attn_conv_w': _L0_attn_in['conv_w'], 'L0_attn_dt_bias': _L0_attn_in['dt_bias'], 'L0_attn_A_log': _L0_attn_in['A_log'], 'L0_attn_norm_w': _L0_attn_in['norm_w'], 'L0_attn_W_out': _L0_attn_in['W_out'], 'L0_xattn_wq': _L0_xattn_in['wq'], 'L0_xattn_wk': _L0_xattn_in['wk'], 'L0_xattn_wv': _L0_xattn_in['wv'], 'L0_xattn_wo': _L0_xattn_in['wo'], 'L0_ffn_gate_w': _L0_ffn_in['gate_w'], 'L0_ffn_w1': _L0_ffn_in['w1'], 'L0_ffn_w2': _L0_ffn_in['w2'], 'L0_ffn_w3': _L0_ffn_in['w3'], 'L1_attn_Wq': _L1_attn_in['Wq'], 'L1_attn_bq': _L1_attn_in['bq'], 'L1_attn_Wk': _L1_attn_in['Wk'], 'L1_attn_bk': _L1_attn_in['bk'], 'L1_attn_Wv': _L1_attn_in['Wv'], 'L1_attn_bv': _L1_attn_in['bv'], 'L1_attn_Wo': _L1_attn_in['Wo'], 'L1_attn_bo': _L1_attn_in['bo'], 'L1_attn_rand_matrix': _L1_attn_in['rand_matrix'], 'L1_xattn_Wq': _L1_xattn_in['Wq'], 'L1_xattn_Wk': _L1_xattn_in['Wk'], 'L1_xattn_Wv': _L1_xattn_in['Wv'], 'L1_xattn_Wo': _L1_xattn_in['Wo'], 'L1_xattn_q_norm_w': _L1_xattn_in['q_norm_w'], 'L1_xattn_k_norm_w': _L1_xattn_in['k_norm_w'], 'L1_ffn_W_r': _L1_ffn_in['W_r'], 'L1_ffn_b_r': _L1_ffn_in['b_r'], 'L1_ffn_W1': _L1_ffn_in['W1'], 'L1_ffn_b1': _L1_ffn_in['b1'], 'L1_ffn_W2': _L1_ffn_in['W2'], 'L1_ffn_b2': _L1_ffn_in['b2'], 'L1_ffn_A1': _L1_ffn_in['A1'], 'L1_ffn_B1': _L1_ffn_in['B1'], 'L1_ffn_A2': _L1_ffn_in['A2'], 'L1_ffn_B2': _L1_ffn_in['B2']}

def reference(x, ctx_2048, mask_BxSx4224_bf0, L0_attn_W_qkv, L0_attn_W_z, L0_attn_W_b, L0_attn_W_a, L0_attn_conv_w, L0_attn_dt_bias, L0_attn_A_log, L0_attn_norm_w, L0_attn_W_out, L0_xattn_wq, L0_xattn_wk, L0_xattn_wv, L0_xattn_wo, L0_ffn_gate_w, L0_ffn_w1, L0_ffn_w2, L0_ffn_w3, L1_attn_Wq, L1_attn_bq, L1_attn_Wk, L1_attn_bk, L1_attn_Wv, L1_attn_bv, L1_attn_Wo, L1_attn_bo, L1_attn_rand_matrix, L1_xattn_Wq, L1_xattn_Wk, L1_xattn_Wv, L1_xattn_Wo, L1_xattn_q_norm_w, L1_xattn_k_norm_w, L1_ffn_W_r, L1_ffn_b_r, L1_ffn_W1, L1_ffn_b1, L1_ffn_W2, L1_ffn_b2, L1_ffn_A1, L1_ffn_B1, L1_ffn_A2, L1_ffn_B2):
    import jax
    import jax.numpy as jnp

    def _L0_attn_ref(x, W_qkv, W_z, W_b, W_a, conv_w, dt_bias, A_log, norm_w, W_out):
        import jax, jax.numpy as jnp
        import numpy as np
        HID = 256
        NK, DK = (16, 128)
        NV, DV = (32, 128)
        KC = 4
        P = NV // NK
        SV = P * DV
        QD = NK * DK
        VD = NV * DV
        QKV = QD + QD + VD
        B, T = (2, 256)
        EPS_NORM = 1e-12
        EPS_RMS = 1e-06

        def _l2norm(x):
            n = jnp.sqrt(jnp.sum(x * x, axis=-1, keepdims=True))
            return x / jnp.maximum(n, EPS_NORM)

        def _reference_tuple_inner(x, W_qkv, W_z, W_b, W_a, conv_w, dt_bias, A_log, norm_w, W_out):
            Bq, Tq, _ = x.shape
            qkv = jnp.einsum('btc,dc->btd', x, W_qkv)
            z = jnp.einsum('btc,dc->btd', x, W_z)
            beta = jax.nn.sigmoid(jnp.einsum('btc,hc->bth', x, W_b))
            dt = jax.nn.softplus(jnp.einsum('btc,hc->bth', x, W_a) + dt_bias)
            decay = jnp.exp(-dt * jnp.exp(A_log))
            xp = jnp.pad(qkv, ((0, 0), (KC - 1, 0), (0, 0)))
            qkv_c = sum((xp[:, j:j + Tq, :] * conv_w[:, j] for j in range(KC)))
            new_conv_buf = jnp.transpose(xp[:, -(KC - 1):, :], (0, 2, 1))
            q = _l2norm(qkv_c[..., :QD].reshape(Bq, Tq, NK, DK))
            k = _l2norm(qkv_c[..., QD:2 * QD].reshape(Bq, Tq, NK, DK))
            v = qkv_c[..., 2 * QD:].reshape(Bq, Tq, NK, P, DV)
            beta_r = beta.reshape(Bq, Tq, NK, P)
            decay_r = decay.reshape(Bq, Tq, NK, P)
            qT = jnp.swapaxes(q, 0, 1)
            kT = jnp.swapaxes(k, 0, 1)
            vT = jnp.swapaxes(v, 0, 1)
            bT = jnp.swapaxes(beta_r, 0, 1)
            dT = jnp.swapaxes(decay_r, 0, 1)

            def step(S, inp):
                q_t, k_t, v_t, b_t, d_t = inp
                Sk = jnp.einsum('bhi,bhipj->bhpj', k_t, S)
                dv = b_t[..., None] * (v_t - Sk)
                upd = jnp.einsum('bhi,bhpj->bhipj', k_t, dv)
                S = S * d_t[:, :, None, :, None] + upd
                o = jnp.einsum('bhi,bhipj->bhpj', q_t, S)
                return (S, o)
            S0 = jnp.zeros((Bq, NK, DK, P, DV), x.dtype)
            S_final, outs = jax.lax.scan(step, S0, (qT, kT, vT, bT, dT))
            out = jnp.swapaxes(outs, 0, 1).reshape(Bq, Tq, NV, DV)
            rms = jax.lax.rsqrt(jnp.mean(out * out, axis=-1, keepdims=True) + EPS_RMS)
            out = out * rms * norm_w
            out = out.reshape(Bq, Tq, VD) * jax.nn.silu(z)
            y = jnp.einsum('btd,cd->btc', out, W_out)
            return (y, S_final.reshape(Bq, NK, DK, SV), new_conv_buf)
        return _reference_tuple_inner(x, W_qkv, W_z, W_b, W_a, conv_w, dt_bias, A_log, norm_w, W_out)[0]

    def _L0_xattn_ref(x, mask, k_cache, v_cache, wq, wk, wv, wo):
        import jax, jax.numpy as jnp
        import numpy as np
        import math
        DIM = 256
        B, Q_LEN, KV_LEN = (8, 128, 512)
        q = jnp.einsum('bsd,ed->bse', x, wq)
        k_new = jnp.einsum('bsd,ed->bse', x, wk)
        v_new = jnp.einsum('bsd,ed->bse', x, wv)
        k = jnp.concatenate([k_cache, k_new], axis=1)
        v = jnp.concatenate([v_cache, v_new], axis=1)
        scale = 1.0 / math.sqrt(q.shape[-1])
        scores = jnp.einsum('bqd,bkd->bqk', q, k) * scale
        attn = jax.nn.softmax(scores, axis=-1)
        out = jnp.einsum('bqk,bkd->bqd', attn, v)
        return jnp.einsum('bqd,ed->bqe', out, wo)

    def _L0_ffn_ref(hidden_states, gate_w, w1, w2, w3):
        import jax, jax.numpy as jnp
        import numpy as np
        B, S, D = (2, 256, 256)
        F = 512
        E, K = (8, 2)
        b, s, d = hidden_states.shape
        x = hidden_states.reshape(-1, d)
        T = x.shape[0]
        logits = x @ gate_w.T
        probs = jax.nn.softmax(logits.astype(jnp.float32), axis=-1)
        top_w, top_e = jax.lax.top_k(probs, K)
        top_w = top_w / jnp.sum(top_w, axis=-1, keepdims=True)
        top_w = top_w.astype(x.dtype)
        rows = jnp.arange(T)[:, None]
        w_full = jnp.zeros((T, E), x.dtype).at[rows, top_e].set(top_w)
        y = jnp.zeros_like(x)
        for e in range(E):
            h = jax.nn.silu(x @ w1[e].T) * (x @ w3[e].T)
            y = y + w_full[:, e:e + 1] * (h @ w2[e].T)
        return y.reshape(b, s, d)

    def _L1_attn_ref(hidden_states, Wq, bq, Wk, bk, Wv, bv, Wo, bo, rand_matrix):
        import math
        import jax, jax.numpy as jnp
        import numpy as np
        HID = 256
        H = 16
        HKV = 8
        D = HID // H
        F = D
        SEQ = 256
        BATCH = 2
        THETA = 10000.0

        def _rotate_half(x):
            x1, x2 = (x[..., :x.shape[-1] // 2], x[..., x.shape[-1] // 2:])
            return jnp.concatenate((-x2, x1), axis=-1)

        def _softmax_kernel(x, R):
            n = jnp.sqrt(jnp.sum(x * x, axis=-1, keepdims=True))
            x = x / jnp.maximum(n, 1e-06)
            p = jnp.einsum('...d,ed->...e', x, R)
            feats = jnp.concatenate([jnp.sin(p), jnp.cos(p)], axis=-1)
            return feats / math.sqrt(F)
        b, s, _ = hidden_states.shape
        q = (hidden_states @ Wq.T + bq).reshape(b, s, H, D).transpose(0, 2, 1, 3)
        k = (hidden_states @ Wk.T + bk).reshape(b, s, HKV, D).transpose(0, 2, 1, 3)
        v = (hidden_states @ Wv.T + bv).reshape(b, s, HKV, D).transpose(0, 2, 1, 3)
        inv_freq = 1.0 / THETA ** (jnp.arange(0, D, 2, dtype=jnp.float32) / D)
        freqs = jnp.arange(s, dtype=jnp.float32)[:, None] * inv_freq[None, :]
        emb = jnp.concatenate((freqs, freqs), axis=-1)
        cos = jnp.cos(emb)[None, None, :, :]
        sin = jnp.sin(emb)[None, None, :, :]
        q = q * cos + _rotate_half(q) * sin
        k = k * cos + _rotate_half(k) * sin
        rep = H // HKV
        k = jnp.repeat(k, rep, axis=1)
        v = jnp.repeat(v, rep, axis=1)
        qp = _softmax_kernel(q, rand_matrix)
        kp = _softmax_kernel(k, rand_matrix)
        kv = jnp.einsum('bhsf,bhsd->bsfd', kp, v)
        out = jnp.einsum('bhsf,bsfd->bhsd', qp, kv)
        out = out.reshape(b, s, HID)
        return out @ Wo.T + bo

    def _L1_xattn_ref(hidden_states, encoder_hidden_states, Wq, Wk, Wv, Wo, q_norm_w, k_norm_w):
        import jax, jax.numpy as jnp
        import numpy as np
        HIDDEN = 256
        N_HEADS = 16
        N_KV_HEADS = 4
        HEAD_DIM = 128
        EPS = 1e-06

        def rms_norm(x, w, eps=EPS):
            xf = x.astype(jnp.float32)
            var = jnp.mean(xf * xf, axis=-1, keepdims=True)
            return w * (xf * jax.lax.rsqrt(var + eps)).astype(x.dtype)
        B, S, _ = hidden_states.shape
        S_enc = encoder_hidden_states.shape[1]
        groups = N_HEADS // N_KV_HEADS
        scale = 1.0 / HEAD_DIM ** 0.5
        q = (hidden_states @ Wq).reshape(B, S, N_HEADS, HEAD_DIM)
        k = (encoder_hidden_states @ Wk).reshape(B, S_enc, N_KV_HEADS, HEAD_DIM)
        v = (encoder_hidden_states @ Wv).reshape(B, S_enc, N_KV_HEADS, HEAD_DIM)
        q = rms_norm(q, q_norm_w)
        k = rms_norm(k, k_norm_w)
        k = jnp.repeat(k, groups, axis=2)
        v = jnp.repeat(v, groups, axis=2)
        scores = jnp.einsum('bqhd,bkhd->bhqk', q, k) * scale
        probs = jax.nn.softmax(scores, axis=-1)
        out = jnp.einsum('bhqk,bkhd->bqhd', probs, v)
        out = out.reshape(B, S, N_HEADS * HEAD_DIM)
        return out @ Wo

    def _L1_ffn_ref(hidden_states, W_r, b_r, W1, b1, W2, b2, A1, B1, A2, B2):
        import jax, jax.numpy as jnp
        import numpy as np
        E, R, K = (8, 8, 2)
        D, F = (256, 1024)
        B, S = (2, 256)
        SCALING = 16.0 / 8.0

        def act(x):
            return jax.nn.gelu(x, approximate=True)
        b, s, d = hidden_states.shape
        N = b * s
        x = hidden_states.reshape(N, d)
        probs = jax.nn.softmax(x @ W_r.T + b_r, axis=-1)
        w_topk, idx_topk = jax.lax.top_k(probs, K)
        base1 = x @ W1.T + b1
        u1 = jnp.einsum('nd,erd->ner', x, A1)
        B1_rf = B1.transpose(0, 2, 1).reshape(E * R, F)
        B2_rf = B2.transpose(0, 2, 1).reshape(E * R, d)
        res = jnp.zeros((N, d), hidden_states.dtype)
        for k in range(K):
            oh = jax.nn.one_hot(idx_topk[:, k], E, dtype=x.dtype)
            z1 = (u1 * oh[:, :, None]).reshape(N, E * R)
            h = act(base1 + z1 @ B1_rf * SCALING)
            u2 = jnp.einsum('nf,erf->ner', h, A2)
            z2 = (u2 * oh[:, :, None]).reshape(N, E * R)
            y = h @ W2.T + b2 + z2 @ B2_rf * SCALING
            res = res + w_topk[:, k:k + 1] * y
        return res.reshape(b, s, d)
    x = x + _L0_attn_ref(_layernorm(x, axis=-1), L0_attn_W_qkv, L0_attn_W_z, L0_attn_W_b, L0_attn_W_a, L0_attn_conv_w, L0_attn_dt_bias, L0_attn_A_log, L0_attn_norm_w, L0_attn_W_out)
    x = x + _L0_xattn_ref(_layernorm(x, axis=-1), mask_BxSx4224_bf0, ctx_2048, ctx_2048, L0_xattn_wq, L0_xattn_wk, L0_xattn_wv, L0_xattn_wo)
    x = x + _L0_ffn_ref(_layernorm(x, axis=-1), L0_ffn_gate_w, L0_ffn_w1, L0_ffn_w2, L0_ffn_w3)
    x = x + _L1_attn_ref(_layernorm(x, axis=-1), L1_attn_Wq, L1_attn_bq, L1_attn_Wk, L1_attn_bk, L1_attn_Wv, L1_attn_bv, L1_attn_Wo, L1_attn_bo, L1_attn_rand_matrix)
    x = x + _L1_xattn_ref(_layernorm(x, axis=-1), ctx_2048, L1_xattn_Wq, L1_xattn_Wk, L1_xattn_Wv, L1_xattn_Wo, L1_xattn_q_norm_w, L1_xattn_k_norm_w)
    x = x + _L1_ffn_ref(_layernorm(x, axis=-1), L1_ffn_W_r, L1_ffn_b_r, L1_ffn_W1, L1_ffn_b1, L1_ffn_W2, L1_ffn_b2, L1_ffn_A1, L1_ffn_B1, L1_ffn_A2, L1_ffn_B2)
    return x

_drawn_inputs = setup_inputs


def setup_inputs(seed=0):
    import zlib

    import numpy as np

    out = dict(_drawn_inputs(seed))
    spreads = {'L0_attn_dt_bias': (0.0, 0.1),
     'L0_attn_A_log': (0.0, 0.1),
     'L0_attn_norm_w': (1.0, 0.2),
     'L1_xattn_q_norm_w': (1.0, 0.6),
     'L1_xattn_k_norm_w': (1.0, 0.6),
     'L1_ffn_b_r': (0.0, 0.8),
     'L1_ffn_b1': (0.0, 0.796),
     'L1_ffn_b2': (0.0, 0.281)}
    factors = {'L0_xattn_wk': 2.952,
     'L0_xattn_wv': 2.671,
     'L1_attn_bq': 8.0,
     'L1_attn_bk': 8.0,
     'L1_attn_bv': 8.0,
     'L1_attn_bo': 4.022,
     'L1_ffn_W_r': 8.0,
     'L1_ffn_A1': 8.0,
     'L1_ffn_B1': 8.0,
     'L1_ffn_A2': 8.0,
     'L1_ffn_B2': 8.0}
    for name, (base, spread) in spreads.items():
        noise = np.random.default_rng([zlib.crc32(name.encode()), seed]).standard_normal(out[name].shape)
        drawn = base * np.exp(spread * noise) if base else spread * noise
        out[name] = jnp.asarray(drawn.astype(out[name].dtype))
    for name, factor in factors.items():
        out[name] = (out[name] * factor).astype(out[name].dtype)
    return out
```

```python
from collections import namedtuple
from contextlib import ExitStack

import numpy as np

import concourse.bass as bass
from concourse import mybir

F32 = mybir.dt.float32
ALU = mybir.AluOpType
ACT = mybir.ActivationFunctionType
AX = mybir.AxisListType

BATCH, SEQ, HID = 16, 56, 256
PAIRS = BATCH // 2
PT = 2 * SEQ
TOK = BATCH * SEQ
HALF = TOK // 2
HPAIRS = PAIRS // 2
CC = HID // 128
BANK = 512

NK, DK, NV, KC = 16, 128, 32, 4
VPK = NV // NK
GROUPS = 4
GK = NK // GROUPS
GV = GK * VPK
SYS = PAIRS * GV
BLK = SEQ // 2

CTX, KT = 1500, 125
NKT = CTX // KT
KS = 500
NKS = CTX // KS

E0, F0 = 8, 512
E1, R1, F1 = 8, 8, 1024
LSCALE = 2.0

AH, AHKV, AD = 16, 8, 16
AF = AD // 2
QKH = AH + AHKV

XH, XKV, XD = 16, 4, 128
XG = XH // XKV


class Shared:
    pass


def sb(nc, ctx, name, shape, dt=F32):
    return ctx.enter_context(nc.sbuf_tensor(f"{name}_sb", list(shape), dt))


def pb(nc, ctx, name, banks):
    return ctx.enter_context(nc.psum_tensor(name, [128, banks, BANK], F32))


def sem(nc, ctx, name):
    handle = nc.alloc_semaphore(name)
    ctx.callback(nc.clear_and_free_semaphores, [handle])
    return handle


def sems(nc, ctx, tag, names, pairs=""):
    ctx.callback(nc.all_engine_barrier)
    found = [sem(nc, ctx, f"{tag}_{n}") for n in names.split()]
    found += [[sem(nc, ctx, f"{tag}_{n}{j}") for j in range(2)] for n in pairs.split()]
    return namedtuple("Semaphores", f"{names} {pairs}")(*found)


def load_constants(nc, k, t):
    with ExitStack() as ctx:
        s = sems(nc, ctx, "init", "loaded filled")
        block = ctx.enter_context(nc.Block())

        @block.sync
        def _(sp):
            sp.dma_start(k.x[:], t["x"].rearrange("(p q) d -> q p d", q=PT)).then_inc(s.loaded, 16)
            sp.dma_start(k.ident[:], t["ident"]).then_inc(s.loaded, 16)
            sp.wait_ge(s.loaded, 32)

        @block.gpsimd
        def _(pool):
            nc.gpsimd.memset(k.ones[:], 1.0).then_inc(s.filled, 1)
            nc.gpsimd.memset(k.minus_half[:], -0.5).then_inc(s.filled, 1)
            nc.gpsimd.memset(k.half[:], 0.5).then_inc(s.filled, 1)
            nc.gpsimd.memset(k.eps6[:], 1e-6).then_inc(s.filled, 1)
            pool.wait_ge(s.filled, 4)


def store_result(nc, k, out):
    with ExitStack() as ctx:
        s = sems(nc, ctx, "end", "stored")
        block = ctx.enter_context(nc.Block())

        @block.sync
        def _(sp):
            sp.dma_start(out.rearrange("(p q) d -> q p d", q=PT), k.x[:]).then_inc(s.stored, 16)
            sp.wait_ge(s.stored, 16)


def layernorm(nc, k, tag):
    with ExitStack() as ctx:
        stats = sb(nc, ctx, f"{tag}_stats", [PT, PAIRS, 6])
        meanvar = sb(nc, ctx, f"{tag}_meanvar", [PT, PAIRS, 2])
        vareps = sb(nc, ctx, f"{tag}_vareps", [PT, PAIRS])
        rstd = sb(nc, ctx, f"{tag}_rstd", [PT, PAIRS])
        xn = sb(nc, ctx, f"{tag}_xn", [PT, PAIRS, HID])
        ps = pb(nc, ctx, f"{tag}_ps", 4)
        s = sems(nc, ctx, tag, "stats meanvar var_ready rstd_ready xn_ready turned copied")
        block = ctx.enter_context(nc.Block())

        @block.vector
        def _(dve):
            for p in range(PAIRS):
                nc.vector.bn_stats(stats[:, p, :], k.x[:, p, :]).then_inc(s.stats, 1)
            for p in range(PAIRS):
                dve.wait_ge(s.stats, p + 1)
                nc.vector.bn_aggr(meanvar[:, p, :], stats[:, p, :]).then_inc(s.meanvar, 1)
            dve.wait_ge(s.meanvar, PAIRS)
            nc.vector.tensor_scalar_add(vareps[:], meanvar[:, :, 1], 1e-5).then_inc(s.var_ready, 1)
            dve.wait_ge(s.rstd_ready, 1)
            for p in range(PAIRS):
                nc.vector.tensor_scalar(xn[:, p, :], k.x[:, p, :], meanvar[:, p, 0:1], rstd[:, p:p + 1],
                                        ALU.subtract, ALU.mult).then_inc(s.xn_ready, 1)
            for b in (1, 3):
                dve.wait_ge(s.turned, b + 1)
                nc.vector.tensor_copy(k.xnT[:, b % CC, (b // CC) * HALF:(b // CC + 1) * HALF],
                                      ps[:, b, 0:HALF]).then_inc(s.copied, 1)

        @block.gpsimd
        def _(pool):
            pool.wait_ge(s.var_ready, 1)
            nc.gpsimd.tensor_tensor(rstd[:], vareps[:], k.minus_half[0:PT, 0:PAIRS], ALU.pow)\
                .then_inc(s.rstd_ready, 1)

        @block.tensor
        def _(pe):
            for b in range(4):
                pe.wait_ge(s.xn_ready, HPAIRS * (b // CC + 1))
                for p in range(HPAIRS):
                    last = nc.tensor.transpose(ps[:, b, p * PT:(p + 1) * PT],
                                               xn[:, (b // CC) * HPAIRS + p, (b % CC) * 128:(b % CC + 1) * 128],
                                               k.ident[0:PT, 0:PT])
                last.then_inc(s.turned, 1)

        @block.scalar
        def _(act):
            for b in (0, 2):
                act.wait_ge(s.turned, b + 1)
                nc.scalar.copy(k.xnT[:, b % CC, (b // CC) * HALF:(b // CC + 1) * HALF],
                               ps[:, b, 0:HALF]).then_inc(s.copied, 1)


def overlap_view(tensor, base, count, width):
    first = tensor[:, base, 0:width]
    return bass.AP(tensor=first.tensor, offset=first.offset, ap=[list(first.ap[0]), [1, count], [1, width]])


def gdn_gates(nc, k, t):
    with ExitStack() as ctx:
        wba = sb(nc, ctx, "gg_wba", [128, CC, 2 * NV])
        rows = sb(nc, ctx, "gg_rows", [PT, 2 * NV])
        exp_b = sb(nc, ctx, "gg_exp_b", [PT, PAIRS, NV])
        onep = sb(nc, ctx, "gg_onep", [PT, PAIRS, NV])
        a = sb(nc, ctx, "gg_a", [PT, PAIRS, NV])
        absa = sb(nc, ctx, "gg_absa", [PT, PAIRS, NV])
        exp_a = sb(nc, ctx, "gg_exp_a", [PT, PAIRS, NV])
        ln_a = sb(nc, ctx, "gg_ln_a", [PT, PAIRS, NV])
        dt = sb(nc, ctx, "gg_dt", [PT, PAIRS, NV])
        rate = sb(nc, ctx, "gg_rate", [PT, NV])
        ps = pb(nc, ctx, "gg_ps", 1)
        s = sems(nc, ctx, "gg", "loaded product expb onep a_ready absa expa lna rate dt_ready done")
        block = ctx.enter_context(nc.Block())
        psv = ps[0:PT, 0, :].rearrange("q (p n) -> q p n", p=PAIRS)

        @block.sync
        def _(sp):
            sp.dma_start(wba[:], t["gdn_wba"]).then_inc(s.loaded, 16)
            sp.dma_start(rows[:], t["gdn_rows"]).then_inc(s.loaded, 16)
            sp.dma_start(k.after[:], t["gdn_after"]).then_inc(s.loaded, 16)
            sp.dma_start(k.upto[:], t["gdn_upto"]).then_inc(s.loaded, 16)
            sp.dma_start(k.kqmask[:], t["gdn_kqmask"]).then_inc(s.loaded, 16)
            sp.dma_start(k.normw[:], t["gdn_normw"]).then_inc(s.loaded, 16)

        @block.tensor
        def _(pe):
            pe.wait_ge(s.loaded, 96)
            for p in range(PAIRS):
                for c in range(CC):
                    last = nc.tensor.matmul(psv[:, p, :], k.xnT[:, c, p * PT:(p + 1) * PT], wba[:, c, :],
                                            start=(c == 0), stop=(c == CC - 1))
            last.then_inc(s.product, 1)

        @block.scalar
        def _(act):
            act.wait_ge(s.product, 1)
            nc.scalar.activation(exp_b[:], psv[:, :, 0:NV], ACT.Exp, scale=-1.0).then_inc(s.expb, 1)
            nc.scalar.activation(rate[:], rows[:, NV:2 * NV], ACT.Exp).then_inc(s.rate, 1)
            act.wait_ge(s.absa, 1)
            nc.scalar.activation(exp_a[:], absa[:], ACT.Exp, scale=-1.0).then_inc(s.expa, 1)
            act.wait_ge(s.expa, 1)
            nc.scalar.activation(ln_a[:], exp_a[:], ACT.Ln, bias=1.0).then_inc(s.lna, 1)

        @block.vector
        def _(dve):
            dve.wait_ge(s.expb, 1)
            nc.vector.tensor_tensor(a[:], psv[:, :, NV:2 * NV],
                                    rows[:, 0:NV].unsqueeze(1).broadcast_to([PT, PAIRS, NV]), ALU.add)\
                .then_inc(s.a_ready, 1)
            dve.wait_ge(s.a_ready, 1)
            nc.vector.scalar_tensor_tensor(out=absa[:], in0=a[:], scalar=-1.0, in1=a[:],
                                           op0=ALU.mult, op1=ALU.max).then_inc(s.absa, 1)
            dve.wait_ge(s.expb, 1)
            nc.vector.tensor_scalar_add(onep[:], exp_b[:], 1.0).then_inc(s.onep, 1)
            dve.wait_ge(s.onep, 1)
            nc.vector.reciprocal(k.beta[:], onep[:]).then_inc(s.done, 1)
            dve.wait_ge(s.lna, 1)
            nc.vector.scalar_tensor_tensor(out=dt[:], in0=a[:], scalar=0.0, in1=ln_a[:],
                                           op0=ALU.max, op1=ALU.add).then_inc(s.dt_ready, 1)
            dve.wait_ge(s.dt_ready, 1)
            dve.wait_ge(s.rate, 1)
            nc.vector.scalar_tensor_tensor(out=k.logdecay[:], in0=dt[:], scalar=-1.0,
                                           in1=rate[:].unsqueeze(1).broadcast_to([PT, PAIRS, NV]),
                                           op0=ALU.mult, op1=ALU.mult).then_inc(s.done, 1)
            dve.wait_ge(s.done, 2)


def gdn_project(nc, k, t, grp, s, ctx):
    w = sb(nc, ctx, "gp_w", [128, 2, 4 * CC * 128 + 4 * KC])
    raw = sb(nc, ctx, "gp_raw", [128, 4, BATCH, KC - 1 + SEQ])
    kq = sb(nc, ctx, "gp_kq", [128, 2, TOK])
    v = sb(nc, ctx, "gp_v", [128, VPK, TOK])
    sq = sb(nc, ctx, "gp_sq", [128, 2, TOK])
    nsq = sb(nc, ctx, "gp_nsq", [PT, 2, PAIRS])
    nk = sb(nc, ctx, "gp_nk", [PT, PAIRS])
    proj = pb(nc, ctx, "gp_proj", 4)
    psk = pb(nc, ctx, "gp_psk", 2)
    psv = pb(nc, ctx, "gp_psv", 2)
    block = ctx.enter_context(nc.Block())
    wt = [w[:, j, 0:4 * CC * 128].rearrange("c (i k n) -> c i k n", i=4, k=CC) for j in range(2)]
    wc = [w[:, j, 4 * CC * 128:].rearrange("c (i k) -> c i k", i=4) for j in range(2)]
    conv_out = [kq[:, 0, :], kq[:, 1, :], v[:, 0, :], v[:, 1, :]]
    STEPS = 4 * (KC - 2)

    @block.sync
    def _(sp):
        with sp.Fori(0, GK // 2) as i:
            for j in range(2):
                sp.wait_ge(s.v_turned[j], 4 * (grp * 2 + i))
                sp.dma_start(w[:, j, :], t["gdn_w"][grp * GK + i * 2 + j]).then_inc(s.w_in[j], 16)

    @block.tensor
    def _(pe):
        with pe.Fori(0, GK // 2) as i:
            for j in range(2):
                n = grp * GK + i * 2 + j
                pe.wait_ge(s.w_in[j], 16 * (grp * 2 + i) + 16)
                for q in range(8):
                    pe.wait_ge(s.evac, 8 * n + (q - 3 if q >= 4 else 0))
                    for c in range(CC):
                        last = nc.tensor.matmul(proj[:, q % 4, 0:HALF], wt[j][:, q // 2, c, :],
                                                k.xnT[:, c, (q % 2) * HALF:(q % 2 + 1) * HALF],
                                                start=(c == 0), stop=(c == CC - 1))
                    last.then_inc(s.projected, 1)
                pe.wait_ge(s.squared, 2 * n + 2)
                pe.wait_ge(s.v_done, 4 * n)
                for which in range(2):
                    for p in range(PAIRS):
                        last = nc.tensor.matmul(psv[0:PT, 1, which * PAIRS + p:which * PAIRS + p + 1],
                                                sq[:, which, p * PT:(p + 1) * PT], k.ones[:, 0:1],
                                                start=True, stop=True)
                last.then_inc(s.ssq, 1)
                for gp in range(4):
                    pe.wait_ge(s.gm_done, 4 * n + (gp - 1 if gp >= 2 else 0))
                    for e in range(2):
                        p = 2 * gp + e
                        last = nc.tensor.matmul(psk[0:PT, gp % 2, e * 2 * PT:(e + 1) * 2 * PT],
                                                kq[:, 0, p * PT:(p + 1) * PT], kq[:, :, p * PT:(p + 1) * PT],
                                                start=True, stop=True)
                    last.then_inc(s.kq_done, 1)
                for q in range(4):
                    pe.wait_ge(s.conv_done, 4 * n + 3 + q // 2)
                    if q == 1:
                        pe.wait_ge(s.nsq_ready, n + 1)
                    pe.wait_ge(s.v_done, 4 * n + (q - 1 if q >= 2 else 0))
                    for e in range(HPAIRS):
                        p = (q % 2) * HPAIRS + e
                        last = nc.tensor.transpose(psv[0:PT, q % 2, e * 128:(e + 1) * 128],
                                                   v[:, q // 2, p * PT:(p + 1) * PT], k.ident[:])
                    last.then_inc(s.v_turned[j], 1)

    @block.scalar
    def _(act):
        with act.Fori(0, GK // 2) as i:
            for j in range(2):
                n = grp * GK + i * 2 + j
                act.wait_ge(s.conv_done, 4 * n)
                act.wait_ge(s.kq_done, 4 * n)
                for q in range(8):
                    tile, half = q // 2, q % 2
                    act.wait_ge(s.projected, 8 * n + q + 1)
                    if q == 4:
                        act.wait_ge(s.v_turned[1 - j], 4 * (grp * 2 + i) + 4 * j)
                    src = proj[:, q % 4, 0:HALF]
                    nc.scalar.copy(raw[:, tile, half * PAIRS:(half + 1) * PAIRS, KC - 1:],
                                   src.rearrange("c (b t) -> c b t", t=SEQ))
                    nc.scalar.mul(conv_out[tile][:, half * HALF:(half + 1) * HALF], src,
                                  wc[j][:, tile, KC - 1:KC]).then_inc(s.evac, 1)

    @block.vector
    def _(dve):
        nc.vector.memset(raw[:, :, :, 0:KC - 1], 0.0).then_inc(s.padded, 1)
        with dve.Fori(0, GK // 2) as i:
            for j in range(2):
                dve.wait_ge(s.padded, grp + 1)
                n = grp * GK + i * 2 + j
                for tile in range(4):
                    dve.wait_ge(s.evac, 8 * n + 2 * tile + 2)
                    dst = conv_out[tile].rearrange("c (b t) -> c b t", t=SEQ)
                    for tap in range(KC - 1):
                        if tap:
                            dve.wait_ge(s.conv_step, STEPS * n + 2 * tile + tap)
                        done = s.conv_done if tap == KC - 2 else s.conv_step
                        nc.vector.scalar_tensor_tensor(out=dst, in0=raw[:, tile, :, tap:tap + SEQ],
                                                       scalar=wc[j][:, tile, tap:tap + 1], in1=dst,
                                                       op0=ALU.mult, op1=ALU.add).then_inc(done, 1)
                dve.wait_ge(s.ssq, n + 1)
                dve.wait_ge(s.roots, 2 * n)
                nc.vector.tensor_scalar_max(nsq[:], psv[0:PT, 1, 0:2 * PAIRS].rearrange("q (w p) -> q w p", w=2),
                                            1e-24).then_inc(s.nsq_ready, 1)
                dve.wait_ge(s.nsq_ready, n + 1)
                nc.vector.reciprocal(k.rnk2[:, i * 2 + j, :], nsq[:, 0, :]).then_inc(s.rnk2, 1)
                for gp in range(4):
                    dve.wait_ge(s.kq_done, 4 * n + gp + 1)
                    nc.vector.tensor_tensor(k.gmtt[:, bass.ts(i * 2 + j, PAIRS * 2 * PT)]
                                            .rearrange("q (p w) -> q p w", p=PAIRS)[:, 2 * gp:2 * gp + 2, :],
                                            psk[0:PT, gp % 2, 0:4 * PT].rearrange("q (e w) -> q e w", e=2),
                                            k.kqmask[:].unsqueeze(1).broadcast_to([PT, 2, 2 * PT]),
                                            ALU.mult).then_inc(s.gm_done, 1)
                dve.wait_ge(s.roots, 2 * n + 2)
                for q in range(4):
                    dve.wait_ge(s.v_turned[j], 4 * (grp * 2 + i) + q + 1)
                    nc.vector.tensor_tensor(k.v[:, (i * 2 + j) * VPK + q // 2, (q % 2) * HPAIRS:(q % 2 + 1) * HPAIRS, :],
                                            psv[0:PT, q % 2, :].rearrange("q (p d) -> q p d", p=HPAIRS),
                                            nk[:, (q % 2) * HPAIRS:(q % 2 + 1) * HPAIRS].unsqueeze(2)
                                            .broadcast_to([PT, HPAIRS, 128]), ALU.mult).then_inc(s.v_done, 1)

    @block.gpsimd
    def _(pool):
        with pool.Fori(0, GK // 2) as i:
            for j in range(2):
                n = grp * GK + i * 2 + j
                pool.wait_ge(s.ssq, n)
                for which in range(2):
                    pool.wait_ge(s.conv_done, 4 * n + which + 1)
                    nc.gpsimd.tensor_tensor(sq[:, which, :], kq[:, which, :], kq[:, which, :], ALU.mult)\
                        .then_inc(s.squared, 1)
                pool.wait_ge(s.nsq_ready, n + 1)
                pool.wait_ge(s.v_done, 4 * n)
                nc.gpsimd.tensor_tensor(nk[:], nsq[:, 0, :], k.half[0:PT, 0:PAIRS], ALU.pow).then_inc(s.roots, 1)
                nc.gpsimd.tensor_tensor(k.rnq[:, i * 2 + j, :], nsq[:, 1, :], k.minus_half[0:PT, 0:PAIRS],
                                        ALU.pow).then_inc(s.roots, 1)


def gdn_systems(nc, k, t, grp, s, ctx):
    cs = sb(nc, ctx, "gs_cs", [PT, PAIRS, GV])
    urhs = sb(nc, ctx, "gs_urhs", [PT, 2, 4, PT])
    dec = [sb(nc, ctx, f"gs_dec{j}", [PT, 4, PT + 1]) for j in range(2)]
    ps = pb(nc, ctx, "gs_ps", 2)
    block = ctx.enter_context(nc.Block())

    @block.gpsimd
    def _(pool):
        with pool.Fori(0, PAIRS) as p:
            for j in range(2):
                pool.wait_ge(s.emm[j], grp * PAIRS + p)
                nc.gpsimd.tensor_tensor(urhs[:, j], k.upto[:].unsqueeze(1).broadcast_to([PT, 4, PT]),
                                        k.logdecay[:, p, bass.ds(grp * GV + j * 4, 4)].unsqueeze(2)
                                        .broadcast_to([PT, 4, PT]), ALU.mult).then_inc(s.u_ready[j], 1)

    @block.tensor
    def _(pe):
        with pe.Fori(0, PAIRS) as p:
            for j in range(2):
                pe.wait_ge(s.u_ready[j], grp * PAIRS + p + 1)
                pe.wait_ge(s.dec_ready[j], grp * PAIRS + p)
                nc.tensor.matmul(ps[0:PT, j, 0:4 * PT], k.after[:], urhs[:, j], start=True, stop=True)\
                    .then_inc(s.emm[j], 1)

    @block.scalar
    def _(act):
        with act.Fori(0, PAIRS) as p:
            for j in range(2):
                act.wait_ge(s.emm[j], grp * PAIRS + p + 1)
                act.wait_ge(s.apt[j], 4 * (grp * PAIRS + p))
                nc.scalar.activation(dec[j][:, :, 1:], ps[0:PT, j, 0:4 * PT].rearrange("q (v w) -> q v w", v=4),
                                     ACT.Exp).then_inc(s.dec_ready[j], 1)

    @block.vector
    def _(dve):
        nc.vector.memset(dec[0][:, :, 0:1], 1.0).then_inc(s.lead, 1)
        nc.vector.memset(dec[1][:, :, 0:1], 1.0).then_inc(s.lead, 1)
        nc.vector.tensor_tensor(cs[:].rearrange("q p (h e) -> q p h e", e=VPK),
                                k.beta[:, :, bass.ds(grp * GV, GV)].rearrange("q p (h e) -> q p h e", e=VPK),
                                k.rnk2[:].rearrange("q h p -> q p h").unsqueeze(3)
                                .broadcast_to([PT, PAIRS, GK, VPK]), ALU.mult).then_inc(s.lead, 1)
        with dve.Fori(0, PAIRS) as p:
            for j in range(2):
                dve.wait_ge(s.lead, 3 * grp + 3)
                dve.wait_ge(s.dec_ready[j], grp * PAIRS + p + 1)
                for v in range(4):
                    vh = j * 4 + v
                    nc.vector.scalar_tensor_tensor(
                        out=k.apt[:, :, bass.ds(p * GV + vh, 1), :].rearrange("q a m w -> q a (m w)"),
                        in0=overlap_view(dec[j], v, 2, PT), scalar=cs[:, p, vh:vh + 1],
                        in1=k.gmtt[:, bass.ds((vh // VPK) * PAIRS * 2 * PT + p * 2 * PT, 2 * PT)]
                        .rearrange("q (a w) -> q a w", a=2),
                        op0=ALU.mult, op1=ALU.mult).then_inc(s.apt[j], 1)


def gdn_solve(nc, k, t, grp, s, ctx):
    asys = sb(nc, ctx, "gv_asys", [2 * SYS, 2, BLK, BLK])
    tsys = sb(nc, ctx, "gv_tsys", [2 * SYS, 2, BLK, BLK])
    prod = sb(nc, ctx, "gv_prod", [2 * SYS, 2, BLK, BLK])
    block = ctx.enter_context(nc.Block())
    flat = lambda x: x.rearrange("m b r c -> m b (r c)")

    @block.sync
    def _(sp):
        for half in range(2):
            for b in range(2):
                r0 = half * SEQ + b * BLK
                sp.dma_start(k.scratch_a[half, b].rearrange("m r c -> r m c"),
                             k.apt[r0:r0 + BLK, 0, :, r0:r0 + BLK]).then_inc(s.a_out, 16)
        sp.wait_ge(s.a_out, 64 * (grp + 1))
        for half in range(2):
            sp.dma_start(flat(asys[half * SYS:(half + 1) * SYS]),
                         k.scratch_a[half].rearrange("b m r c -> m b (r c)")).then_inc(s.a_in, 16)
        sp.wait_ge(s.solved, (BLK - 1) * (grp + 1))
        for half in range(2):
            sp.dma_start(k.scratch_t[half].rearrange("b m r c -> m b (r c)"),
                         flat(tsys[half * SYS:(half + 1) * SYS])).then_inc(s.t_out, 16)
        sp.wait_ge(s.t_out, 32 * (grp + 1))
        sp.wait_ge(s.zeroed, grp + 1)
        for half in range(2):
            for b in range(2):
                r0 = half * SEQ + b * BLK
                sp.dma_start(k.tt[r0:r0 + BLK, :, r0:r0 + BLK],
                             k.scratch_t[half, b].rearrange("m r c -> r m c")).then_inc(s.t_in, 16)

    @block.gpsimd
    def _(pool):
        nc.gpsimd.memset(tsys[:], 0.0).then_inc(s.t_zero, 1)
        pool.wait_ge(s.t_zero, 2 * grp + 1)
        ones = k.ones[0:2 * SYS, 0:2 * BLK].rearrange("m (b r) -> m b r", b=2)
        nc.gpsimd.tensor_tensor(flat(tsys[:])[:, :, 0:BLK * BLK:BLK + 1], ones, ones, ALU.mult).then_inc(s.t_zero, 1)
        nc.gpsimd.memset(k.gmtt[:], 0.0).then_inc(s.zeroed, 1)
        pool.wait_ge(s.t_in, 64 * (grp + 1))

    @block.vector
    def _(dve):
        dve.wait_ge(s.a_in, 32 * (grp + 1))
        dve.wait_ge(s.t_zero, 2 * grp + 2)
        for c in range(1, BLK):
            if c > 1:
                dve.wait_ge(s.solved, (BLK - 1) * grp + c - 1)
            nc.vector.tensor_tensor(prod[:, :, 0:c, 0:c], tsys[:, :, 0:c, 0:c],
                                    asys[:, :, 0:c, c].unsqueeze(2).broadcast_to([2 * SYS, 2, c, c]),
                                    ALU.mult).then_inc(s.prod, 1)
            dve.wait_ge(s.prod, (BLK - 1) * grp + c)
            nc.vector.tensor_reduce(tsys[:, :, 0:c, c], prod[:, :, 0:c, 0:c], AX.X, ALU.add)\
                .then_inc(s.solved, 1)


def gdn_output(nc, k, t, grp, s, ctx):
    UNITS = PAIRS * 2
    wz = sb(nc, ctx, "go_wz", [128, CC, GV * 128])
    wo = sb(nc, ctx, "go_wo", [128, GV, HID])
    rq = sb(nc, ctx, "go_rq", [PT, PAIRS, GV])
    rq2 = sb(nc, ctx, "go_rq2", [PT, PAIRS, GV])
    y = sb(nc, ctx, "go_y", [PT, 3, 512])
    d = sb(nc, ctx, "go_d", [PT, 2, 512])
    r = sb(nc, ctx, "go_r", [PT, 512])
    w = sb(nc, ctx, "go_w", [PT, 512])
    sil = sb(nc, ctx, "go_sil", [PT, 512])
    gate = sb(nc, ctx, "go_gate", [PT, 4, 512])
    osq = sb(nc, ctx, "go_osq", [PT, 512])
    ssq = sb(nc, ctx, "go_ssq", [PT, 4])
    mean = sb(nc, ctx, "go_mean", [PT, 4])
    eps = sb(nc, ctx, "go_eps", [PT, 4])
    root = sb(nc, ctx, "go_root", [PT, 4])
    fac = sb(nc, ctx, "go_fac", [PT, 4])
    og = sb(nc, ctx, "go_og", [PT, 512])
    ogn = sb(nc, ctx, "go_ogn", [PT, 512])
    ogT = sb(nc, ctx, "go_ogT", [128, 4 * PT])
    ps = pb(nc, ctx, "go_ps", 8)
    Y, R, W, O, Z, T, OUT = range(7)
    block = ctx.enter_context(nc.Block())

    def unit(u):
        return u // 2, u % 2, (u // 2) * GV + (u % 2) * 4

    def upto(u):
        return grp * UNITS + u + 1

    def quad(x):
        return x.rearrange("q (v n) -> q v n", v=4)

    @block.sync
    def _(sp):
        sp.dma_start(wz[:], t["gdn_wz"][grp]).then_inc(s.wz_in, 16)
        sp.dma_start(wo[:], t["gdn_wo"][grp]).then_inc(s.wo_in, 16)

    @block.tensor
    def _(pe):
        pe.wait_ge(s.wz_in, 16 * grp + 16)
        pe.wait_ge(s.wo_in, 16 * grp + 16)
        for i in range(UNITS + 6):
            u = i
            if u < UNITS:
                p, q, m = unit(u)
                pe.wait_ge(s.silu, upto(u - 1))
                for c in range(CC):
                    last = nc.tensor.matmul(ps[0:PT, Z, :], k.xnT[:, c, p * PT:(p + 1) * PT],
                                            wz[:, c, q * 512:(q + 1) * 512], start=(c == 0), stop=(c == CC - 1))
                last.then_inc(s.z, 1)
                pe.wait_ge(s.y_ready, upto(u - 1))
                pe.wait_ge(s.d_ready, upto(u - 1))
                for v in range(4):
                    last = nc.tensor.matmul(ps[0:PT, Y, v * 128:(v + 1) * 128], k.tt[:, m + v, :],
                                            k.v[:, q * 4 + v, p, :], start=True, stop=True)
                last.then_inc(s.y, 1)
            u = i - 1
            if 0 <= u < UNITS:
                p, q, m = unit(u)
                pe.wait_ge(s.y_ready, upto(u))
                pe.wait_ge(s.r_ready, upto(u - 1))
                for v in range(4):
                    last = nc.tensor.matmul(ps[0:PT, R, v * 128:(v + 1) * 128], k.apt[:, 0, m + v, :],
                                            y[:, u % 3, v * 128:(v + 1) * 128], start=True, stop=True)
                last.then_inc(s.r, 1)
            u = i - 2
            if 0 <= u < UNITS:
                p, q, m = unit(u)
                pe.wait_ge(s.r_ready, upto(u))
                pe.wait_ge(s.w_ready, upto(u - 1))
                for v in range(4):
                    last = nc.tensor.matmul(ps[0:PT, W, v * 128:(v + 1) * 128], k.tt[:, m + v, :],
                                            r[:, v * 128:(v + 1) * 128], start=True, stop=True)
                last.then_inc(s.w, 1)
            u = i - 3
            if 0 <= u < UNITS:
                p, q, m = unit(u)
                pe.wait_ge(s.w_ready, upto(u))
                pe.wait_ge(s.og, upto(u - 1))
                pe.wait_ge(s.osq, upto(u - 1))
                for v in range(4):
                    last = nc.tensor.matmul(ps[0:PT, O, v * 128:(v + 1) * 128], k.apt[:, 1, m + v, :],
                                            w[:, v * 128:(v + 1) * 128], start=True, stop=True)
                last.then_inc(s.o, 1)
            u = i - 5
            if 0 <= u < UNITS:
                pe.wait_ge(s.ogn, upto(u))
                pe.wait_ge(s.ogT, upto(u - 1))
                for v in range(4):
                    last = nc.tensor.transpose(ps[:, T, v * PT:(v + 1) * PT], ogn[:, v * 128:(v + 1) * 128],
                                               k.ident[0:PT, 0:PT])
                last.then_inc(s.turned, 1)
                p, q, m = unit(u)
                pe.wait_ge(s.ogT, upto(u))
                if q == 0:
                    pe.wait_ge(s.added, grp * PAIRS + p)
                for v in range(4):
                    last = nc.tensor.matmul(ps[0:PT, OUT, 0:HID], ogT[:, v * PT:(v + 1) * PT],
                                            wo[:, q * 4 + v, :], start=(q == 0 and v == 0),
                                            stop=(q == 1 and v == 3))
                last.then_inc(s.out, 1)

    @block.scalar
    def _(act):
        for i in range(UNITS + 6):
            u = i
            if u < UNITS:
                act.wait_ge(s.z, upto(u))
                act.wait_ge(s.gate, upto(u - 1))
                nc.scalar.activation(sil[:], ps[0:PT, Z, :], ACT.Silu).then_inc(s.silu, 1)
                act.wait_ge(s.y, upto(u))
                if u >= 3:
                    act.wait_ge(s.w_ready, upto(u - 3))
                nc.scalar.copy(y[:, u % 3, :], ps[0:PT, Y, :]).then_inc(s.y_ready, 1)
            u = i - 3
            if 0 <= u < UNITS:
                act.wait_ge(s.o, upto(u))
                act.wait_ge(s.ssq_o, upto(u - 1))
                nc.scalar.square(osq[:], ps[0:PT, O, :]).then_inc(s.osq, 1)
            u = i - 5
            if 0 <= u < UNITS:
                act.wait_ge(s.turned, upto(u))
                act.wait_ge(s.out, upto(u - 1))
                nc.scalar.copy(ogT[:], ps[:, T, 0:4 * PT]).then_inc(s.ogT, 1)

    @block.vector
    def _(dve):
        nc.vector.tensor_copy(rq[:].rearrange("q p (h e) -> q p h e", e=VPK),
                              k.rnq[:].rearrange("q h p -> q p h").unsqueeze(3)
                              .broadcast_to([PT, PAIRS, GK, VPK])).then_inc(s.rq, 1)
        dve.wait_ge(s.rq, 2 * grp + 1)
        nc.vector.scalar_tensor_tensor(out=rq2[:], in0=rq[:], scalar=1.0 / 128, in1=rq[:],
                                       op0=ALU.mult, op1=ALU.mult).then_inc(s.rq, 1)
        for i in range(UNITS + 6):
            u = i
            if u < UNITS:
                p, q, m = unit(u)
                dve.wait_ge(s.y_ready, upto(u))
                if u >= 2:
                    dve.wait_ge(s.r_ready, upto(u - 2))
                nc.vector.tensor_tensor(quad(d[:, u % 2, :]), k.v[:, q * 4:q * 4 + 4, p, :], quad(ps[0:PT, Y, :]),
                                        ALU.subtract).then_inc(s.d_ready, 1)
            u = i - 1
            if 0 <= u < UNITS:
                dve.wait_ge(s.r, upto(u))
                dve.wait_ge(s.d_ready, upto(u))
                dve.wait_ge(s.w, upto(u - 1))
                nc.vector.tensor_tensor(r[:], ps[0:PT, R, :], d[:, u % 2, :], ALU.add).then_inc(s.r_ready, 1)
            u = i - 2
            if 0 <= u < UNITS:
                dve.wait_ge(s.w, upto(u))
                dve.wait_ge(s.o, upto(u - 1))
                nc.vector.tensor_tensor(w[:], ps[0:PT, W, :], y[:, u % 3, :], ALU.add).then_inc(s.w_ready, 1)
            u = i - 3
            if 0 <= u < UNITS:
                dve.wait_ge(s.osq, upto(u))
                dve.wait_ge(s.mean, upto(u - 1))
                nc.vector.tensor_reduce(ssq[:], quad(osq[:]), AX.X, ALU.add).then_inc(s.ssq_o, 1)
                dve.wait_ge(s.gate, upto(u))
                dve.wait_ge(s.ogn, upto(u - 1))
                nc.vector.tensor_tensor(og[:], ps[0:PT, O, :], gate[:, u % 4, :], ALU.mult).then_inc(s.og, 1)
            u = i - 5
            if 0 <= u < UNITS and u % 2:
                p = u // 2
                dve.wait_ge(s.out, upto(u))
                nc.vector.tensor_tensor(k.x[:, p, :], k.x[:, p, :], ps[0:PT, OUT, 0:HID], ALU.add)\
                    .then_inc(s.added, 1)

    @block.gpsimd
    def _(pool):
        pool.wait_ge(s.rq, 2 * grp + 2)
        for i in range(UNITS + 6):
            u = i
            if u < UNITS:
                pool.wait_ge(s.silu, upto(u))
                if u >= 4:
                    pool.wait_ge(s.og, upto(u - 4))
                nc.gpsimd.tensor_tensor(quad(gate[:, u % 4, :]), quad(sil[:]),
                                        k.normw[:].unsqueeze(1).broadcast_to([PT, 4, 128]), ALU.mult)\
                    .then_inc(s.gate, 1)
            u = i - 3
            if 0 <= u < UNITS:
                p, q, m = unit(u)
                pool.wait_ge(s.ssq_o, upto(u))
                nc.gpsimd.tensor_tensor(mean[:], ssq[:], rq2[:, p, q * 4:q * 4 + 4], ALU.mult).then_inc(s.mean, 1)
                pool.wait_ge(s.mean, upto(u))
                nc.gpsimd.tensor_tensor(eps[:], mean[:], k.eps6[0:PT, 0:4], ALU.add).then_inc(s.eps, 1)
                pool.wait_ge(s.eps, upto(u))
                nc.gpsimd.tensor_tensor(root[:], eps[:], k.minus_half[0:PT, 0:4], ALU.pow).then_inc(s.root, 1)
                pool.wait_ge(s.root, upto(u))
                nc.gpsimd.tensor_tensor(fac[:], root[:], rq[:, p, q * 4:q * 4 + 4], ALU.mult).then_inc(s.fac, 1)
                pool.wait_ge(s.fac, upto(u))
                pool.wait_ge(s.og, upto(u))
                pool.wait_ge(s.turned, upto(u - 1))
                nc.gpsimd.tensor_tensor(quad(ogn[:]), quad(og[:]), fac[:].unsqueeze(2).broadcast_to([PT, 4, 128]),
                                        ALU.mult).then_inc(s.ogn, 1)


def gated_delta_rule(nc, k, t):
    with ExitStack() as ctx:
        k.beta = sb(nc, ctx, "beta", [PT, PAIRS, NV])
        k.logdecay = sb(nc, ctx, "logdecay", [PT, PAIRS, NV])
        k.after = sb(nc, ctx, "after", [PT, PT])
        k.upto = sb(nc, ctx, "upto", [PT, PT])
        k.kqmask = sb(nc, ctx, "kqmask", [PT, 2 * PT])
        k.normw = sb(nc, ctx, "normw", [PT, 128])
        gdn_gates(nc, k, t)
        k.v = sb(nc, ctx, "values", [PT, GV, PAIRS, 128])
        k.gmtt = sb(nc, ctx, "gmtt", [PT, GK * PAIRS * 2 * PT])
        k.tt = k.gmtt[:].rearrange("q (m w) -> q m w", w=PT)
        k.apt = sb(nc, ctx, "apt", [PT, 2, SYS, PT])
        k.rnk2 = sb(nc, ctx, "rnk2", [PT, GK, PAIRS])
        k.rnq = sb(nc, ctx, "rnq", [PT, GK, PAIRS])
        k.scratch_a = nc.dram_tensor("scratch_a", [2, 2, SYS, BLK, BLK], F32, kind="Internal").ap()
        k.scratch_t = nc.dram_tensor("scratch_t", [2, 2, SYS, BLK, BLK], F32, kind="Internal").ap()
        s = sems(nc, ctx, "gdn", "evac projected squared v_done ssq gm_done kq_done conv_done nsq_ready "
                 "conv_step padded roots rnk2 lead a_out a_in solved t_out t_in t_zero zeroed prod "
                 "wz_in wo_in silu z y_ready d_ready y r r_ready w w_ready o og osq ogn ogT turned out added "
                 "gate ssq_o mean eps root fac rq", pairs="w_in v_turned emm u_ready dec_ready apt")
        with nc.Fori(0, GROUPS) as grp:
            for part in (gdn_project, gdn_systems, gdn_solve, gdn_output):
                with ExitStack() as inner:
                    part(nc, k, t, grp, s, inner)


def context_projections(nc, k, t):
    with ExitStack() as ctx:
        wq = sb(nc, ctx, "cp_wq", [128, CC, HID])
        wk = sb(nc, ctx, "cp_wk", [128, CC, HID])
        wv = sb(nc, ctx, "cp_wv", [128, CC, HID])
        ps = pb(nc, ctx, "cp_ps", 8)
        s = sems(nc, ctx, "cp", "loaded product even odd")
        block = ctx.enter_context(nc.Block())

        @block.sync
        def _(sp):
            sp.dma_start(wq[:], t["c_wq"]).then_inc(s.loaded, 16)
            sp.dma_start(wk[:], t["c_wk"]).then_inc(s.loaded, 16)
            sp.dma_start(wv[:], t["c_wv"]).then_inc(s.loaded, 16)

        @block.tensor
        def _(pe):
            pe.wait_ge(s.loaded, 48)
            for n in range(16):
                if n >= 8:
                    pe.wait_ge((s.even, s.odd)[n % 2], (n - 8) // 2 + 1)
                if n < 8:
                    w, f, half = (wq, wk)[n // 4], n // 2 % 2, n % 2
                    for c in range(CC):
                        last = nc.tensor.matmul(ps[:, n, 0:HALF], w[:, c, f * 128:(f + 1) * 128],
                                                k.xnT[:, c, half * HALF:(half + 1) * HALF],
                                                start=(c == 0), stop=(c == CC - 1))
                else:
                    for e in range(2):
                        b = 2 * (n - 8) + e
                        for c in range(CC):
                            last = nc.tensor.matmul(ps[0:SEQ, n % 8, e * HID:(e + 1) * HID],
                                                    k.xnT[:, c, b * SEQ:(b + 1) * SEQ], wv[:, c, :],
                                                    start=(c == 0), stop=(c == CC - 1))
                last.then_inc(s.product, 1)

        def evacuate(eng, n, copy, scaled):
            eng.wait_ge(s.product, n + 1)
            done = (s.even, s.odd)[n % 2]
            if n < 8:
                dst = (k.qT, k.knT)[n // 4][:, n // 2 % 2, n % 2 * HALF:(n % 2 + 1) * HALF]
                if n < 4:
                    scaled(dst, ps[:, n, 0:HALF], 1 / 16).then_inc(done, 1)
                else:
                    copy(dst, ps[:, n, 0:HALF]).then_inc(done, 1)
            else:
                copy(k.vnew[:, 2 * (n - 8):2 * (n - 8) + 2, :].rearrange("q b d -> q (b d)"),
                     ps[0:SEQ, n % 8, :]).then_inc(done, 1)

        @block.scalar
        def _(act):
            for n in range(0, 16, 2):
                evacuate(act, n, nc.scalar.copy, nc.scalar.mul)

        @block.vector
        def _(dve):
            for n in range(1, 16, 2):
                evacuate(dve, n, nc.vector.tensor_copy, nc.vector.tensor_scalar_mul)


def context_softmax(nc, k, t):
    SLOTS = 4
    TURNS = BATCH // SLOTS
    KEYS = CTX + SEQ
    SPAN = KEYS // 4
    NT = NKT + 1
    LOW = 7
    with ExitStack() as ctx:
        kv = sb(nc, ctx, "cs_kv", [KT, SLOTS, NKT, HID])
        kvT = sb(nc, ctx, "cs_kvT", [128, 2, CC, CTX])
        qslot = sb(nc, ctx, "cs_qslot", [128, 2, CC, SEQ])
        vslot = sb(nc, ctx, "cs_vslot", [SEQ, 2, HID])
        prob = sb(nc, ctx, "cs_prob", [SEQ, KEYS])
        probn = sb(nc, ctx, "cs_probn", [SEQ, KEYS])
        pT = sb(nc, ctx, "cs_pT", [KT, NT, SEQ])
        negmax = sb(nc, ctx, "cs_negmax", [SEQ, 1])
        total = sb(nc, ctx, "cs_total", [SEQ, 1])
        rtotal = sb(nc, ctx, "cs_rtotal", [SEQ, 1])
        ps_s = pb(nc, ctx, "cs_ps_s", 4)
        ps_t = pb(nc, ctx, "cs_ps_t", 2)
        ps_o = pb(nc, ctx, "cs_ps_o", 1)
        s = sems(nc, ctx, "cs", "scored negmax exped rtotal probn stored staged")
        ctx_in = [sem(nc, ctx, f"cs_ctx_in{j}") for j in range(SLOTS)]
        pv_done = [sem(nc, ctx, f"cs_pv_done{j}") for j in range(SLOTS)]
        turned = [sem(nc, ctx, f"cs_turned{j}") for j in range(2)]
        copied = [sem(nc, ctx, f"cs_copied{j}") for j in range(2)]
        block = ctx.enter_context(nc.Block())
        FIRST = NKT // 4
        EACH = FIRST + 1

        def turns(body, eng):
            with eng.Fori(0, TURNS - 1) as it:
                for j in range(SLOTS):
                    body(it, j, False)
            for j in range(SLOTS):
                body(TURNS - 1, j, j == SLOTS - 1)

        @block.sync
        def _(sp):
            with sp.Fori(0, TURNS) as it:
                for j in range(SLOTS):
                    sp.wait_ge(pv_done[j], it)
                    sp.dma_start(kv[:, j], t["context"][it * SLOTS + j].rearrange("(i q) d -> q i d", q=KT))\
                        .then_inc(ctx_in[j], 16)

        @block.tensor
        def _(pe):
            def turn_context(it, j, b, use):
                pe.wait_ge(ctx_in[j], 16 * it + 16)
                for r in range(2 * FIRST):
                    c, quad = r % 2, r // 2
                    pe.wait_ge(copied[c], use + quad)
                    for e in range(4):
                        last = nc.tensor.transpose(ps_t[:, c, e * KT:(e + 1) * KT],
                                                   kv[:, j, quad * 4 + e, c * 128:(c + 1) * 128],
                                                   k.ident[0:KT, 0:KT])
                    last.then_inc(turned[c], 1)

            def sequence(it, j, last_one):
                b = it * SLOTS + j
                use = FIRST + EACH * b
                for c in range(2):
                    pe.wait_ge(copied[c], use)
                pe.wait_ge(s.staged, 2 * b + 2)
                pe.wait_ge(s.exped, b)
                for i in range(4):
                    lo, hi = i * SPAN, min((i + 1) * SPAN, CTX)
                    for c in range(CC):
                        nc.tensor.matmul(ps_s[0:SEQ, i, 0:hi - lo], qslot[:, j % 2, c, :],
                                         kvT[:, j % 2, c, lo:hi], start=(c == 0), stop=(c == CC - 1))
                for c in range(CC):
                    last = nc.tensor.matmul(ps_s[0:SEQ, 3, SPAN - SEQ:SPAN], qslot[:, j % 2, c, :],
                                            k.knT[:, c, bass.ts(b, SEQ)], start=(c == 0), stop=(c == CC - 1))
                last.then_inc(s.scored, 1)
                if not last_one:
                    nj = (j + 1) % SLOTS
                    turn_context(it + (j + 1) // SLOTS, nj, b + 1, use)
                    use = use + FIRST
                pe.wait_ge(s.probn, b + 1)
                for bank in range(2):
                    pe.wait_ge(copied[bank], use)
                nc.tensor.nop(nofuse=True)
                for bank, tiles in ((0, range(LOW)), (1, range(LOW, NT))):
                    for i in tiles:
                        n = KT if i < NKT else SEQ
                        last = nc.tensor.transpose(ps_t[0:n, bank, (i - tiles[0]) * SEQ:(i - tiles[0] + 1) * SEQ],
                                                   probn[:, i * KT:i * KT + n], k.ident[0:SEQ, 0:SEQ])
                    last.then_inc(turned[bank], 1)
                for bank in range(2):
                    pe.wait_ge(copied[bank], use + 1)
                pe.wait_ge(s.stored, b)
                for d in range(CC):
                    for i in range(NT):
                        n = KT if i < NKT else SEQ
                        v = kv[:, j, i, d * 128:(d + 1) * 128] if i < NKT else vslot[:, j % 2, d * 128:(d + 1) * 128]
                        last = nc.tensor.matmul(ps_o[:, 0, d * SEQ:(d + 1) * SEQ], v, pT[0:n, i, :],
                                                start=(i == 0), stop=(i == NT - 1))
                last.then_inc(pv_done[j], 1)

            turn_context(0, 0, 0, 0)
            turns(sequence, pe)

        def copy_context(eng, copy, bank, j, b, use):
            eng.wait_ge(s.scored, b - 1 if not isinstance(b, int) else max(b - 1, 0))
            for quad in range(FIRST):
                eng.wait_ge(turned[bank], use + quad + 1)
                copy(kvT[:, j % 2, bank, quad * 500:(quad + 1) * 500], ps_t[:, bank, 0:500])\
                    .then_inc(copied[bank], 1)

        @block.scalar
        def _(act):
            def sequence(it, j, last_one):
                b = it * SLOTS + j
                use = FIRST + EACH * b
                if not last_one:
                    copy_context(act, nc.scalar.copy, 0, j + 1, b + 1, use)
                    use = use + FIRST
                act.wait_ge(s.negmax, b + 1)
                nc.scalar.activation(prob[:].rearrange("q (i n) -> q i n", i=4), ps_s[0:SEQ, :, 0:SPAN], ACT.Exp,
                                     bias=negmax[:], accum_out=total[:]).then_inc(s.exped, 1)
                act.wait_ge(turned[0], use + 1)
                nc.scalar.copy(pT[:, 0:LOW, :], ps_t[0:KT, 0, 0:LOW * SEQ].rearrange("q (i n) -> q i n", n=SEQ))\
                    .then_inc(copied[0], 1)

            for quad in range(FIRST):
                act.wait_ge(turned[0], quad + 1)
                nc.scalar.copy(kvT[:, 0, 0, quad * 500:(quad + 1) * 500], ps_t[:, 0, 0:500]).then_inc(copied[0], 1)
            turns(sequence, act)

        @block.vector
        def _(dve):
            def sequence(it, j, last_one):
                b = it * SLOTS + j
                use = FIRST + EACH * b
                dve.wait_ge(s.scored, b + 1)
                nc.vector.tensor_reduce(negmax[:], ps_s[0:SEQ, :, 0:SPAN], AX.XY, ALU.max, negate=True)\
                    .then_inc(s.negmax, 1)
                if not last_one:
                    copy_context(dve, nc.vector.tensor_copy, 1, j + 1, b + 1, use)
                    use = use + FIRST
                dve.wait_ge(s.exped, b + 1)
                nc.vector.reciprocal(rtotal[:], total[:]).then_inc(s.rtotal, 1)
                dve.wait_ge(s.rtotal, b + 1)
                nc.vector.tensor_scalar_mul(probn[:], prob[:], rtotal[:]).then_inc(s.probn, 1)
                dve.wait_ge(turned[1], use + 1)
                nc.vector.tensor_copy(pT[:, LOW:NKT, :], ps_t[0:KT, 1, 0:(NKT - LOW) * SEQ]
                                      .rearrange("q (i n) -> q i n", n=SEQ))
                nc.vector.tensor_copy(pT[0:SEQ, NKT, :], ps_t[0:SEQ, 1, (NKT - LOW) * SEQ:(NT - LOW) * SEQ])\
                    .then_inc(copied[1], 1)
                dve.wait_ge(pv_done[j], it + 1)
                nc.vector.tensor_copy(k.oT[:, :, bass.ts(b, SEQ)],
                                      ps_o[:, 0, 0:CC * SEQ].rearrange("d (c n) -> d c n", c=CC)).then_inc(s.stored, 1)

            for quad in range(FIRST):
                dve.wait_ge(turned[1], quad + 1)
                nc.vector.tensor_copy(kvT[:, 0, 1, quad * 500:(quad + 1) * 500], ps_t[:, 1, 0:500]).then_inc(copied[1], 1)
            turns(sequence, dve)

        @block.gpsimd
        def _(pool):
            with pool.Fori(0, TURNS) as it:
                for j in range(SLOTS):
                    b = it * SLOTS + j
                    pool.wait_ge(pv_done[(j - 2) % SLOTS], it + (1 if j >= 2 else 0))
                    nc.gpsimd.tensor_copy(qslot[:, j % 2], k.qT[:, :, bass.ts(b, SEQ)]).then_inc(s.staged, 1)
                    nc.gpsimd.tensor_copy(vslot[:, j % 2, :], k.vnew[:, b, :]).then_inc(s.staged, 1)


def add_projection(nc, k, tag, weight, srcT, chunks, bias=None):
    with ExitStack() as ctx:
        w = sb(nc, ctx, f"{tag}_w", [128, chunks, HID])
        ps = pb(nc, ctx, f"{tag}_ps", 8)
        s = sems(nc, ctx, tag, "loaded product biased added")
        block = ctx.enter_context(nc.Block())

        @block.sync
        def _(sp):
            sp.dma_start(w[:], weight).then_inc(s.loaded, 16)

        @block.tensor
        def _(pe):
            pe.wait_ge(s.loaded, 16)
            for p in range(PAIRS):
                for c in range(chunks):
                    last = nc.tensor.matmul(ps[0:PT, p, 0:HID], srcT[:, c, p * PT:(p + 1) * PT], w[:, c, :],
                                            start=(c == 0), stop=(c == chunks - 1))
                last.then_inc(s.product, 1)

        @block.vector
        def _(dve):
            if bias is not None:
                nc.vector.tensor_tensor(k.x[:], k.x[:], bias.unsqueeze(1).broadcast_to([PT, PAIRS, HID]),
                                        ALU.add).then_inc(s.biased, 1)
                dve.wait_ge(s.biased, 1)
            for p in range(PAIRS):
                dve.wait_ge(s.product, p + 1)
                nc.vector.tensor_tensor(k.x[:, p, :], k.x[:, p, :], ps[0:PT, p, 0:HID], ALU.add)\
                    .then_inc(s.added, 1)


def context_attention(nc, k, t):
    with ExitStack() as ctx:
        k.qT = sb(nc, ctx, "ca_qT", [128, CC, TOK])
        k.knT = sb(nc, ctx, "ca_knT", [128, CC, TOK])
        k.vnew = sb(nc, ctx, "ca_vnew", [SEQ, BATCH, HID])
        k.oT = sb(nc, ctx, "ca_oT", [128, CC, TOK])
        context_projections(nc, k, t)
        context_softmax(nc, k, t)
        add_projection(nc, k, "ca_out", t["c_wo"], k.oT, CC)


def route(nc, k, tag, weight, bias, experts=8):
    N = PAIRS * experts
    with ExitStack() as ctx:
        w = sb(nc, ctx, f"{tag}_w", [128, CC, experts])
        earlier = sb(nc, ctx, f"{tag}_earlier", [PT, experts * experts])
        brow = sb(nc, ctx, f"{tag}_brow", [PT, experts]) if bias is not None else None
        logit = sb(nc, ctx, f"{tag}_logit", [PT, PAIRS, experts])
        top = sb(nc, ctx, f"{tag}_top", [PT, PAIRS])
        shifted = sb(nc, ctx, f"{tag}_shifted", [PT, PAIRS, experts])
        ex = sb(nc, ctx, f"{tag}_ex", [PT, PAIRS, experts])
        total = sb(nc, ctx, f"{tag}_total", [PT, PAIRS])
        rtotal = sb(nc, ctx, f"{tag}_rtotal", [PT, PAIRS])
        more = sb(nc, ctx, f"{tag}_more", [PT, N, experts])
        same = sb(nc, ctx, f"{tag}_same", [PT, N, experts])
        tie = sb(nc, ctx, f"{tag}_tie", [PT, N, experts])
        before = sb(nc, ctx, f"{tag}_before", [PT, N, experts])
        ps = pb(nc, ctx, f"{tag}_ps", 1)
        s = sems(nc, ctx, tag, "loaded product ex chain")
        block = ctx.enter_context(nc.Block())
        over_j = lambda x: x[:].unsqueeze(3).broadcast_to([PT, PAIRS, experts, experts])
        over_e = lambda x: x[:].unsqueeze(2).broadcast_to([PT, PAIRS, experts, experts])
        cube = lambda x: x[:].rearrange("q (p e) j -> q p e j", p=PAIRS)

        @block.sync
        def _(sp):
            sp.dma_start(w[:], weight).then_inc(s.loaded, 16)
            sp.dma_start(earlier[:], k.t["earlier"]).then_inc(s.loaded, 16)
            if bias is not None:
                sp.dma_start(brow[:], bias).then_inc(s.loaded, 16)

        @block.tensor
        def _(pe):
            pe.wait_ge(s.loaded, 32 if bias is None else 48)
            for p in range(PAIRS):
                for c in range(CC):
                    last = nc.tensor.matmul(ps[0:PT, 0, p * experts:(p + 1) * experts],
                                            k.xnT[:, c, p * PT:(p + 1) * PT], w[:, c, :],
                                            start=(c == 0), stop=(c == CC - 1))
            last.then_inc(s.product, 1)

        @block.scalar
        def _(act):
            act.wait_ge(s.chain, 3)
            nc.scalar.activation(ex[:], shifted[:], ACT.Exp).then_inc(s.ex, 1)

        @block.vector
        def _(dve):
            count = [0]

            def wait_all():
                dve.wait_ge(s.chain, count[0])

            def step(ins):
                ins.then_inc(s.chain, 1)
                count[0] += 1

            dve.wait_ge(s.product, 1)
            raw = ps[0:PT, 0, 0:N].rearrange("q (p e) -> q p e", p=PAIRS)
            if bias is None:
                step(nc.vector.tensor_copy(logit[:], raw))
            else:
                step(nc.vector.tensor_tensor(logit[:], raw, brow[:].unsqueeze(1)
                                             .broadcast_to([PT, PAIRS, experts]), ALU.add))
            wait_all()
            step(nc.vector.tensor_reduce(top[:], logit[:], AX.X, ALU.max))
            wait_all()
            step(nc.vector.tensor_tensor(shifted[:], logit[:], top[:].unsqueeze(2)
                                         .broadcast_to([PT, PAIRS, experts]), ALU.subtract))
            dve.wait_ge(s.ex, 1)
            step(nc.vector.tensor_reduce(total[:], ex[:], AX.X, ALU.add))
            wait_all()
            step(nc.vector.reciprocal(rtotal[:], total[:]))
            wait_all()
            step(nc.vector.tensor_tensor(k.prob[:], ex[:], rtotal[:].unsqueeze(2)
                                         .broadcast_to([PT, PAIRS, experts]), ALU.mult))
            wait_all()
            step(nc.vector.tensor_tensor(cube(more), over_e(k.prob), over_j(k.prob), ALU.is_gt))
            step(nc.vector.tensor_tensor(cube(same), over_e(k.prob), over_j(k.prob), ALU.is_equal))
            wait_all()
            step(nc.vector.tensor_tensor(cube(tie), cube(same), earlier[:]
                                         .rearrange("q (e j) -> q e j", e=experts).unsqueeze(1)
                                         .broadcast_to([PT, PAIRS, experts, experts]), ALU.mult))
            wait_all()
            step(nc.vector.tensor_tensor(before[:], more[:], tie[:], ALU.add))
            wait_all()
            step(nc.vector.tensor_reduce(k.rank[:].rearrange("q p e -> q (p e)"), before[:], AX.X, ALU.add))


def expert_weights(nc, k):
    with ExitStack() as ctx:
        picked = sb(nc, ctx, "ew_picked", [PT, PAIRS, E0])
        total = sb(nc, ctx, "ew_total", [PT, PAIRS])
        rtotal = sb(nc, ctx, "ew_rtotal", [PT, PAIRS])
        s = sems(nc, ctx, "ew", "picked total rtotal done")
        block = ctx.enter_context(nc.Block())

        @block.vector
        def _(dve):
            nc.vector.scalar_tensor_tensor(out=picked[:], in0=k.rank[:], scalar=1.5, in1=k.prob[:],
                                           op0=ALU.is_lt, op1=ALU.mult).then_inc(s.picked, 1)
            dve.wait_ge(s.picked, 1)
            nc.vector.tensor_reduce(total[:], picked[:], AX.X, ALU.add).then_inc(s.total, 1)
            dve.wait_ge(s.total, 1)
            nc.vector.reciprocal(rtotal[:], total[:]).then_inc(s.rtotal, 1)
            dve.wait_ge(s.rtotal, 1)
            nc.vector.tensor_tensor(k.wfull[:], picked[:], rtotal[:].unsqueeze(2)
                                    .broadcast_to([PT, PAIRS, E0]), ALU.mult).then_inc(s.done, 1)


def swiglu_experts(nc, k, t):
    FT = F0 // 128
    W13 = CC * F0
    with ExitStack() as ctx:
        w = sb(nc, ctx, "sw_w", [128, 2, 2 * W13 + FT * HID])
        gate = sb(nc, ctx, "sw_gate", [128, 2, HALF])
        hid = sb(nc, ctx, "sw_hid", [128, 2, FT, TOK])
        up = pb(nc, ctx, "sw_up", 4)
        down = pb(nc, ctx, "sw_down", 4)
        s = sems(nc, ctx, "sw", "upped gated hidden downed added")
        w_in = [sem(nc, ctx, f"sw_w_in{j}") for j in range(2)]
        used = [sem(nc, ctx, f"sw_used{j}") for j in range(2)]
        block = ctx.enter_context(nc.Block())
        w13 = [[w[:, j, m * W13:(m + 1) * W13].rearrange("c (k n) -> c k n", k=CC) for m in range(2)]
               for j in range(2)]
        w2 = [w[:, j, 2 * W13:].rearrange("c (k n) -> c k n", k=FT) for j in range(2)]
        Q = 2 * FT

        @block.sync
        def _(sp):
            with sp.Fori(0, E0 // 2) as i:
                for j in range(2):
                    sp.wait_ge(used[j], PAIRS * i)
                    sp.dma_start(w[:, j, :], t["s_w"][i * 2 + j]).then_inc(w_in[j], 16)

        @block.tensor
        def _(pe):
            with pe.Fori(0, E0 // 2) as i:
                for j in range(2):
                    e = i * 2 + j
                    pe.wait_ge(w_in[j], 16 * i + 16)
                    for q in range(Q):
                        f, half = q // 2, q % 2
                        pe.wait_ge(s.hidden, Q * e + max(q - 1, 0))
                        for m in range(2):
                            for c in range(CC):
                                last = nc.tensor.matmul(up[:, (q % 2) * 2 + m, 0:HALF],
                                                        w13[j][m][:, c, f * 128:(f + 1) * 128],
                                                        k.xnT[:, c, half * HALF:(half + 1) * HALF],
                                                        start=(c == 0), stop=(c == CC - 1))
                        last.then_inc(s.upped, 1)
                    pe.wait_ge(s.hidden, Q * e + Q)
                    for p in range(PAIRS):
                        pe.wait_ge(s.added, PAIRS * e + max(p - 3, 0))
                        for f in range(FT):
                            last = nc.tensor.matmul(down[0:PT, p % 4, 0:HID], hid[:, j, f, p * PT:(p + 1) * PT],
                                                    w2[j][:, f, :], start=(f == 0), stop=(f == FT - 1))
                        last.then_inc(used[j], 1)

        @block.scalar
        def _(act):
            with act.Fori(0, E0 // 2) as i:
                for j in range(2):
                    e = i * 2 + j
                    for q in range(Q):
                        act.wait_ge(s.upped, Q * e + q + 1)
                        act.wait_ge(s.hidden, Q * e + max(q - 1, 0))
                        nc.scalar.activation(gate[:, q % 2, :], up[:, (q % 2) * 2, 0:HALF], ACT.Silu)\
                            .then_inc(s.gated, 1)

        @block.vector
        def _(dve):
            with dve.Fori(0, E0 // 2) as i:
                for j in range(2):
                    e = i * 2 + j
                    dve.wait_ge(used[j], PAIRS * i)
                    for q in range(Q):
                        dve.wait_ge(s.gated, Q * e + q + 1)
                        nc.vector.tensor_tensor(hid[:, j, q // 2, (q % 2) * HALF:(q % 2 + 1) * HALF],
                                                gate[:, q % 2, :], up[:, (q % 2) * 2 + 1, 0:HALF], ALU.mult)\
                            .then_inc(s.hidden, 1)
                    for p in range(PAIRS):
                        dve.wait_ge(used[j], PAIRS * i + p + 1)
                        nc.vector.scalar_tensor_tensor(out=k.x[:, p, :], in0=down[0:PT, p % 4, 0:HID],
                                                       scalar=k.wfull[:, p, bass.ds(e, 1)], in1=k.x[:, p, :],
                                                       op0=ALU.mult, op1=ALU.add).then_inc(s.added, 1)


def routed_swiglu(nc, k, t):
    with ExitStack() as ctx:
        k.t = t
        k.prob = sb(nc, ctx, "rs_prob", [PT, PAIRS, E0])
        k.rank = sb(nc, ctx, "rs_rank", [PT, PAIRS, E0])
        k.wfull = sb(nc, ctx, "rs_wfull", [PT, PAIRS, E0])
        route(nc, k, "r0", t["r0_w"], None)
        expert_weights(nc, k)
        swiglu_experts(nc, k, t)


def feature_products(nc, k, t):
    NH = PAIRS * QKH
    MAGIC = 1.5 * 2.0 ** 23
    PI = float(np.float32(np.pi))
    TWO_PI_HI = 6.28125
    TWO_PI_LO = 2 * np.pi - TWO_PI_HI
    with ExitStack() as ctx:
        w = sb(nc, ctx, "fp_w", [128, CC, 512])
        brow = sb(nc, ctx, "fp_brow", [PT, 512])
        cos = sb(nc, ctx, "fp_cos", [PT, AD])
        sin = sb(nc, ctx, "fp_sin", [PT, AD])
        rdiag = sb(nc, ctx, "fp_rdiag", [128, 64])
        qk = sb(nc, ctx, "fp_qk", [PT, NH, AD])
        turned_by = sb(nc, ctx, "fp_turned", [PT, NH, AD])
        crossed = sb(nc, ctx, "fp_crossed", [PT, NH, AD])
        rot = sb(nc, ctx, "fp_rot", [PT, NH, AD])
        sq = sb(nc, ctx, "fp_sq", [PT, NH, AD])
        ssq = sb(nc, ctx, "fp_ssq", [PT, NH])
        ssqm = sb(nc, ctx, "fp_ssqm", [PT, NH])
        rnorm = sb(nc, ctx, "fp_rnorm", [PT, NH])
        expo = sb(nc, ctx, "fp_expo", [PT, NH])
        rotn = sb(nc, ctx, "fp_rotn", [PT, NH, AD])
        rotT = sb(nc, ctx, "fp_rotT", [128, 2, 3 * PT])
        arg = sb(nc, ctx, "fp_arg", [PT, NH, AD])
        near = sb(nc, ctx, "fp_near", [PT, NH, AD])
        ps = pb(nc, ctx, "fp_ps", 8)
        s = sems(nc, ctx, "fp", "loaded product biased chain ssqm expo rnorm turned copied feat argued ready sined")
        block = ctx.enter_context(nc.Block())
        by_pair = lambda x, p: x[:, p * QKH:(p + 1) * QKH, :].rearrange("q h d -> q (h d)")

        @block.sync
        def _(sp):
            for dst, name in ((w, "f_w"), (brow, "f_b"), (cos, "f_cos"), (sin, "f_sin"), (rdiag, "f_r")):
                sp.dma_start(dst[:], t[name]).then_inc(s.loaded, 16)

        @block.tensor
        def _(pe):
            pe.wait_ge(s.loaded, 80)
            for p in range(PAIRS):
                for c in range(CC):
                    last = nc.tensor.matmul(ps[0:PT, p, :], k.xnT[:, c, p * PT:(p + 1) * PT], w[:, c, :],
                                            start=(c == 0), stop=(c == CC - 1))
                last.then_inc(s.product, 1)
            pe.wait_ge(s.biased, 2 * PAIRS)
            pe.wait_ge(s.ready, 1)
            for p in range(PAIRS):
                if p >= 2:
                    pe.wait_ge(s.copied, p - 1)
                for i in range(3):
                    last = nc.tensor.transpose(ps[:, p % 2, i * PT:(i + 1) * PT],
                                               by_pair(rotn, p)[:, i * 128:(i + 1) * 128], k.ident[0:PT, 0:PT])
                last.then_inc(s.turned, 1)
                pe.wait_ge(s.copied, p + 1)
                if p >= 4:
                    pe.wait_ge(s.argued, 2 * (p - 3))
                for i in range(3):
                    last = nc.tensor.matmul(ps[0:PT, 4 + p % 4, i * 64:(i + 1) * 64],
                                            rotT[:, p % 2, i * PT:(i + 1) * PT], rdiag[:], start=True, stop=True)
                last.then_inc(s.feat, 1)

        @block.gpsimd
        def _(pool):
            nc.gpsimd.memset(expo[:], -0.5).then_inc(s.expo, 1)
            pool.wait_ge(s.expo, 1)
            pool.wait_ge(s.ssqm, 1)
            nc.gpsimd.tensor_tensor(rnorm[:], ssqm[:], expo[:], ALU.pow).then_inc(s.rnorm, 1)

        @block.scalar
        def _(act):
            for p in range(PAIRS):
                act.wait_ge(s.turned, p + 1)
                if p >= 2:
                    act.wait_ge(s.feat, p - 1)
                nc.scalar.copy(rotT[:, p % 2, :], ps[:, p % 2, 0:3 * PT]).then_inc(s.copied, 1)
            act.wait_ge(s.ready, 2)
            nc.scalar.activation(k.feat[:], near[:], ACT.Sin).then_inc(s.sined, 1)

        @block.vector
        def _(dve):
            count = [0]

            def step(ins):
                ins.then_inc(s.chain, 1)
                count[0] += 1
                dve.wait_ge(s.chain, count[0])

            heads = lambda x: x[:].unsqueeze(1).broadcast_to([PT, NH, AD])
            for p in range(PAIRS):
                dve.wait_ge(s.product, p + 1)
                nc.vector.tensor_tensor(by_pair(qk, p), ps[0:PT, p, 0:QKH * AD], brow[:, 0:QKH * AD], ALU.add)\
                    .then_inc(s.biased, 1)
                nc.vector.tensor_tensor(k.vals[:, p, :], ps[0:PT, p, QKH * AD:], brow[:, QKH * AD:], ALU.add)\
                    .then_inc(s.biased, 1)
            dve.wait_ge(s.biased, 2 * PAIRS)
            step(nc.vector.tensor_tensor(turned_by[:], qk[:], heads(cos), ALU.mult))
            step(nc.vector.tensor_tensor(crossed[:, :, 0:AF], qk[:, :, AF:], sin[:, 0:AF].unsqueeze(1)
                                         .broadcast_to([PT, NH, AF]), ALU.mult))
            step(nc.vector.tensor_tensor(crossed[:, :, AF:], qk[:, :, 0:AF], sin[:, AF:].unsqueeze(1)
                                         .broadcast_to([PT, NH, AF]), ALU.mult))
            step(nc.vector.tensor_tensor(rot[:], turned_by[:], crossed[:], ALU.add))
            step(nc.vector.tensor_tensor(sq[:], rot[:], rot[:], ALU.mult))
            step(nc.vector.tensor_reduce(ssq[:], sq[:], AX.X, ALU.add))
            nc.vector.tensor_scalar_max(ssqm[:], ssq[:], 1e-12).then_inc(s.ssqm, 1)
            dve.wait_ge(s.rnorm, 1)
            nc.vector.tensor_tensor(rotn[:], rot[:], rnorm[:].unsqueeze(2).broadcast_to([PT, NH, AD]), ALU.mult)\
                .then_inc(s.ready, 1)
            for p in range(PAIRS):
                dve.wait_ge(s.feat, p + 1)
                prod = ps[0:PT, 4 + p % 4, 0:QKH * AF].rearrange("q (h f) -> q h f", f=AF)
                at = arg[:, p * QKH:(p + 1) * QKH, :]
                nc.vector.tensor_copy(at[:, :, 0:AF], prod).then_inc(s.argued, 1)
                nc.vector.tensor_scalar_add(at[:, :, AF:], prod, float(np.pi / 2)).then_inc(s.argued, 1)
            dve.wait_ge(s.argued, 2 * PAIRS)
            step(nc.vector.tensor_scalar(near[:], arg[:], float(1 / (2 * np.pi)), MAGIC, ALU.mult, ALU.add))
            step(nc.vector.tensor_scalar(sq[:], near[:], -MAGIC, None, ALU.add))
            step(nc.vector.scalar_tensor_tensor(out=rot[:], in0=sq[:], scalar=-TWO_PI_HI, in1=arg[:],
                                                op0=ALU.mult, op1=ALU.add))
            step(nc.vector.scalar_tensor_tensor(out=crossed[:], in0=sq[:], scalar=-TWO_PI_LO, in1=rot[:],
                                                op0=ALU.mult, op1=ALU.add))
            nc.vector.tensor_scalar(near[:], crossed[:], PI, -PI, ALU.min, ALU.max).then_inc(s.ready, 1)


def feature_mix(nc, k, t):
    QN, KN = AH * AD, AHKV * AD
    with ExitStack() as ctx:
        prod = sb(nc, ctx, "fm_prod", [PT, 2, AH, AHKV, AD])
        score = sb(nc, ctx, "fm_score", [PT, 2, AH, AHKV])
        prod2 = sb(nc, ctx, "fm_prod2", [PT, AH, AD, AHKV])
        mixed = sb(nc, ctx, "fm_mixed", [PT, PAIRS, AH, AD])
        again = sb(nc, ctx, "fm_again", [PT, PAIRS, HID])
        ps = pb(nc, ctx, "fm_ps", 4)
        s = sems(nc, ctx, "fm", "prod scored prod2 mixed out back turned copied")
        block = ctx.enter_context(nc.Block())

        @block.gpsimd
        def _(pool):
            for p in range(PAIRS):
                if p >= 2:
                    pool.wait_ge(s.scored, p - 1)
                feat = k.feat[:, p * QKH:(p + 1) * QKH, :]
                nc.gpsimd.tensor_tensor(prod[:, p % 2], feat[:, 0:AH, :].unsqueeze(2)
                                        .broadcast_to([PT, AH, AHKV, AD]),
                                        feat[:, AH:, :].unsqueeze(1).broadcast_to([PT, AH, AHKV, AD]),
                                        ALU.mult).then_inc(s.prod, 1)

        @block.vector
        def _(dve):
            for p in range(PAIRS):
                dve.wait_ge(s.prod, p + 1)
                nc.vector.tensor_reduce(score[:, p % 2], prod[:, p % 2], AX.X, ALU.add).then_inc(s.scored, 1)
                dve.wait_ge(s.scored, p + 1)
                dve.wait_ge(s.mixed, p)
                nc.vector.tensor_tensor(prod2[:], score[:, p % 2].unsqueeze(2).broadcast_to([PT, AH, AD, AHKV]),
                                        k.vals[:, p, :].rearrange("q (h d) -> q d h", d=AD).unsqueeze(1)
                                        .broadcast_to([PT, AH, AD, AHKV]), ALU.mult).then_inc(s.prod2, 1)
                dve.wait_ge(s.prod2, p + 1)
                nc.vector.tensor_reduce(mixed[:, p], prod2[:], AX.X, ALU.add).then_inc(s.mixed, 1)

        @block.sync
        def _(sp):
            for p in range(PAIRS):
                sp.wait_ge(s.mixed, p + 1)
                for e in range(2):
                    sp.dma_start(k.scratch_f[2 * p + e].rearrange("h t d -> t h d"),
                                 mixed[e * SEQ:(e + 1) * SEQ, p]).then_inc(s.out, 16)
            sp.wait_ge(s.out, 16 * BATCH)
            flat = k.scratch_f.rearrange("b h t d -> (b h t d)").rearrange("(p q n) -> q p n", q=PT, n=HID)
            sp.dma_start(again[:], flat).then_inc(s.back, 16)

        @block.tensor
        def _(pe):
            pe.wait_ge(s.back, 16)
            for b in range(4):
                for e in range(HPAIRS):
                    last = nc.tensor.transpose(ps[:, b, e * PT:(e + 1) * PT],
                                               again[:, (b // CC) * HPAIRS + e, (b % CC) * 128:(b % CC + 1) * 128],
                                               k.ident[0:PT, 0:PT])
                last.then_inc(s.turned, 1)

        @block.scalar
        def _(act):
            for b in range(4):
                act.wait_ge(s.turned, b + 1)
                nc.scalar.mul(k.oT[:, b % CC, (b // CC) * HALF:(b // CC + 1) * HALF], ps[:, b, 0:HALF],
                              2.0 / AD).then_inc(s.copied, 1)


def feature_attention(nc, k, t):
    with ExitStack() as ctx:
        k.vals = sb(nc, ctx, "fa_vals", [PT, PAIRS, AHKV * AD])
        k.feat = sb(nc, ctx, "fa_feat", [PT, PAIRS * QKH, AD])
        k.oT = sb(nc, ctx, "fa_oT", [128, CC, TOK])
        bo = sb(nc, ctx, "fa_bo", [PT, HID])
        k.scratch_f = nc.dram_tensor("scratch_f", [BATCH, AH, SEQ, AD], F32, kind="Internal").ap()
        feature_products(nc, k, t)
        feature_mix(nc, k, t)
        load_bias(nc, "fb", bo, t["f_bo"])
        add_projection(nc, k, "fa_out", t["f_wo"], k.oT, CC, bias=bo[:])


def load_bias(nc, tag, dst, src):
    with ExitStack() as ctx:
        s = sems(nc, ctx, tag, "loaded")
        block = ctx.enter_context(nc.Block())

        @block.sync
        def _(sp):
            sp.dma_start(dst[:], src).then_inc(s.loaded, 16)
            sp.wait_ge(s.loaded, 16)


def grouped_queries(nc, k, t):
    UNITS = PAIRS * XKV
    with ExitStack() as ctx:
        w = sb(nc, ctx, "gq_w", [128, CC, XH * XD])
        nw = sb(nc, ctx, "gq_nw", [128, 2])
        nws = sb(nc, ctx, "gq_nws", [128, 1])
        sq = sb(nc, ctx, "gq_sq", [PT, 512])
        ssq = sb(nc, ctx, "gq_ssq", [PT, 2, 4])
        mean = sb(nc, ctx, "gq_mean", [PT, 2, 4])
        rms = sb(nc, ctx, "gq_rms", [PT, 2, 4])
        qn = sb(nc, ctx, "gq_qn", [PT, 2, 512])
        qT = sb(nc, ctx, "gq_qT", [128, 2, 2, XH, SEQ])
        ps = pb(nc, ctx, "gq_ps", 4)
        pt = pb(nc, ctx, "gq_pt", 2)
        s = sems(nc, ctx, "gq", "loaded product squared ssq mean rms normed turned weight copied")
        out = [sem(nc, ctx, f"gq_out{j}") for j in range(2)]
        block = ctx.enter_context(nc.Block())
        quad = lambda x: x.rearrange("q (v n) -> q v n", v=4)

        @block.sync
        def _(sp):
            sp.dma_start(w[:], t["x_wq"]).then_inc(s.loaded, 16)
            sp.dma_start(nw[:], t["x_nw"]).then_inc(s.loaded, 16)
            for p in range(PAIRS):
                sp.wait_ge(s.copied, XKV * (p + 1))
                sp.dma_start(k.scratch_q[p], qT[:, p % 2]).then_inc(out[p % 2], 16)
            for j in range(2):
                sp.wait_ge(out[j], 16 * (PAIRS // 2))

        @block.tensor
        def _(pe):
            pe.wait_ge(s.loaded, 32)
            for u in range(UNITS + 2):
                if u < UNITS:
                    p, g = u // XKV, u % XKV
                    if u >= 4:
                        pe.wait_ge(s.normed, u - 3)
                    for c in range(CC):
                        last = nc.tensor.matmul(ps[0:PT, u % 4, :], k.xnT[:, c, p * PT:(p + 1) * PT],
                                                w[:, c, g * 512:(g + 1) * 512], start=(c == 0), stop=(c == CC - 1))
                    last.then_inc(s.product, 1)
                v = u - 2
                if v >= 0:
                    pe.wait_ge(s.normed, v + 1)
                    if v >= 2:
                        pe.wait_ge(s.copied, v - 1)
                    for h in range(4):
                        last = nc.tensor.transpose(pt[:, v % 2, h * PT:(h + 1) * PT],
                                                   qn[:, v % 2, h * 128:(h + 1) * 128], k.ident[0:PT, 0:PT])
                    last.then_inc(s.turned, 1)

        @block.scalar
        def _(act):
            act.wait_ge(s.weight, 1)
            for u in range(UNITS + 2):
                if u < UNITS:
                    act.wait_ge(s.product, u + 1)
                    if u >= 1:
                        act.wait_ge(s.ssq, u)
                    nc.scalar.square(sq[:], ps[0:PT, u % 4, :]).then_inc(s.squared, 1)
                v = u - 2
                if v >= 0:
                    p, g = v // XKV, v % XKV
                    act.wait_ge(s.turned, v + 1)
                    if p >= 2:
                        act.wait_ge(out[p % 2], 16 * (p // 2))
                    nc.scalar.mul(qT[:, p % 2, :, g * 4:(g + 1) * 4, :].rearrange("d j h n -> d h j n"),
                                  pt[:, v % 2, 0:4 * PT].rearrange("d (h j n) -> d h j n", h=4, j=2), nws[:]).then_inc(s.copied, 1)

        @block.gpsimd
        def _(pool):
            for u in range(UNITS):
                pool.wait_ge(s.mean, u + 1)
                if u >= 2:
                    pool.wait_ge(s.normed, u - 1)
                nc.gpsimd.tensor_tensor(rms[:, u % 2, :], mean[:, u % 2, :], k.minus_half[0:PT, 0:4], ALU.pow)\
                    .then_inc(s.rms, 1)

        @block.vector
        def _(dve):
            dve.wait_ge(s.loaded, 32)
            nc.vector.scalar_tensor_tensor(out=nws[:], in0=nw[:, 0:1], scalar=float(XD) ** -0.5, in1=nw[:, 1:2],
                                           op0=ALU.mult, op1=ALU.mult).then_inc(s.weight, 1)
            for u in range(UNITS):
                dve.wait_ge(s.squared, u + 1)
                if u >= 2:
                    dve.wait_ge(s.mean, u - 1)
                nc.vector.tensor_reduce(ssq[:, u % 2, :], quad(sq[:]), AX.X, ALU.add).then_inc(s.ssq, 1)
                dve.wait_ge(s.ssq, u + 1)
                if u >= 2:
                    dve.wait_ge(s.rms, u - 1)
                nc.vector.tensor_scalar(mean[:, u % 2, :], ssq[:, u % 2, :], 1.0 / XD, 1e-6, ALU.mult, ALU.add)\
                    .then_inc(s.mean, 1)
                dve.wait_ge(s.rms, u + 1)
                if u >= 2:
                    dve.wait_ge(s.turned, u - 1)
                nc.vector.tensor_tensor(quad(qn[:, u % 2, :]), quad(ps[0:PT, u % 4, :]),
                                        rms[:, u % 2, :].unsqueeze(2).broadcast_to([PT, 4, 128]), ALU.mult)\
                    .then_inc(s.normed, 1)


def grouped_softmax(nc, k, t):
    HP = XH // 2
    TILES = [2, 2, 2, 2, 2, 1, 1, 0]
    FIRST = [sum(TILES[:h]) for h in range(HP + 1)]
    QT = 4
    PIECES = NKT // QT
    ROUNDS = NKT // QT
    with ExitStack() as ctx:
        wkv = sb(nc, ctx, "gx_wkv", [128, CC, 2 * XKV * XD])
        wo = sb(nc, ctx, "gx_wo", [128, XH, HID])
        piece = sb(nc, ctx, "gx_piece", [128, 2, CC, KS])
        kT = sb(nc, ctx, "gx_kT", [128, 2, XKV, CTX])
        val = sb(nc, ctx, "gx_val", [KT, 2, NKT, XKV * XD])
        qT = sb(nc, ctx, "gx_qT", [128, 2, XH, SEQ])
        oT = sb(nc, ctx, "gx_oT", [128, XH, PT])
        ksq = sb(nc, ctx, "gx_ksq", [KT, 512])
        kssq = sb(nc, ctx, "gx_kssq", [KT, 4])
        kmean = sb(nc, ctx, "gx_kmean", [KT, 4])
        krms = sb(nc, ctx, "gx_krms", [KT, 4])
        kn = sb(nc, ctx, "gx_kn", [KT, 2, 512])
        prob = sb(nc, ctx, "gx_prob", [PT, 2, CTX])
        pT = sb(nc, ctx, "gx_pT", [KT, NKT, PT])
        negmax = sb(nc, ctx, "gx_negmax", [PT, 2])
        total = sb(nc, ctx, "gx_total", [PT, 2])
        rtotal = sb(nc, ctx, "gx_rtotal", [PT, 2])
        ps_s = pb(nc, ctx, "gx_ps_s", 3)
        ps_t = pb(nc, ctx, "gx_ps_t", 2)
        ps_k = pb(nc, ctx, "gx_ps_k", 1)
        ps_v = pb(nc, ctx, "gx_ps_v", 1)
        ps_o = pb(nc, ctx, "gx_ps_o", 1)
        s = sems(nc, ctx, "gx", "weights q_in scored negmax exped rtotal probn pv stored projected added "
                 "k_ps v_ps k_sq k_ssq k_mean k_rms k_normed k_turned v_copied")
        piece_in = [sem(nc, ctx, f"gx_piece_in{j}") for j in range(2)]
        turned = [sem(nc, ctx, f"gx_turned{j}") for j in range(2)]
        copied = [sem(nc, ctx, f"gx_copied{j}") for j in range(2)]
        block = ctx.enter_context(nc.Block())
        quad = lambda x: x.rearrange("q (v n) -> q v n", v=4)

        USES0 = NKT // 2
        USES = (2 * NKT + 2 * HP * ROUNDS) // 2

        def plan(last):
            tasks, n = [], 0
            for e in range(2 * HP):
                j, h = e // HP, e % HP
                make = not (last and j == 1)
                tasks.append(("scores", e, 0, None, ((n + 1) // 2, n // 2)))
                if make and h:
                    for tile in range(FIRST[h - 1], FIRST[h]):
                        tasks.append(("turn_keys", e, tile, n % 2, n // 2))
                        n += 1
                tasks.append(("exp", e, 0, None, None))
                for d in ([e - 1] if e else []):
                    for r in range(ROUNDS):
                        tasks.append(("turn_probs", d, r, n % 2, n // 2))
                        n += 1
                    tasks.append(("values", d, 0, None, ((n + 1) // 2, n // 2)))
                if make:
                    for tile in range(FIRST[h], FIRST[h + 1]):
                        tasks.append(("make", e, tile, None, None))
                tasks.append(("norm", e, 0, None, None))
            for r in range(ROUNDS):
                tasks.append(("turn_probs", e, r, n % 2, n // 2))
                n += 1
            tasks.append(("values", e, 0, None, ((n + 1) // 2, n // 2)))
            tasks.append(("project", 0, 0, None, None))
            return tasks

        def pairs(eng, task):
            def run(i, tasks):
                before = USES0 + USES * i
                for kind, e, n, bank, uses in tasks:
                    if isinstance(uses, int):
                        uses = before + uses
                    elif uses is not None:
                        uses = [before + u for u in uses]
                    task(i, kind, e, n, bank, uses)

            with eng.Fori(0, PAIRS - 1) as i:
                run(i, plan(False))
            run(PAIRS - 1, plan(True))

        def key_tile(i, e, tile):
            j = e // HP
            return (j + 1) % 2, NKT * (2 * i + j + 1) + tile

        @block.sync
        def _(sp):
            def load(slot, n):
                sp.dma_start(piece[:, slot], t["x_ctxT"][n]).then_inc(piece_in[slot], 16)

            sp.dma_start(wkv[:], t["x_wkv"]).then_inc(s.weights, 16)
            load(0, 0)
            load(1, 1)
            sp.dma_start(wo[:], t["x_wo"]).then_inc(s.weights, 16)
            sp.wait_ge(s.v_ps, QT)
            load(0, 2)

            def pair(i, sequences):
                sp.wait_ge(s.scored, 2 * HP * i)
                sp.dma_start(qT[:], k.scratch_q[i]).then_inc(s.q_in, 16)
                for q in range(PIECES, PIECES * (1 + sequences)):
                    n = 2 * PIECES * i + q
                    sp.wait_ge(s.v_ps, QT * (n - 1))
                    load(q % 2, n)

            with sp.Fori(0, PAIRS - 1) as i:
                pair(i, 2)
            pair(PAIRS - 1, 1)

        @block.tensor
        def _(pe):
            def make(slot, count, tile, uses):
                if tile % QT == 0:
                    pe.wait_ge(piece_in[slot], 16 * uses + 16)
                lo = tile % QT * KT
                for ready, free, psum, w0 in ((s.k_ps, s.k_normed, ps_k, 0), (s.v_ps, s.v_copied, ps_v, 512)):
                    pe.wait_ge(free, count)
                    for c in range(CC):
                        last = nc.tensor.matmul(psum[0:KT, 0, :], piece[:, slot, c, lo:lo + KT],
                                                wkv[:, c, w0:w0 + 512], start=(c == 0), stop=(c == CC - 1))
                    last.then_inc(ready, 1)

            def turn_keys(tile, count, bank, use):
                pe.wait_ge(s.k_normed, count + 1)
                pe.wait_ge(copied[bank], use)
                for g in range(XKV):
                    last = nc.tensor.transpose(ps_t[:, bank, g * KT:(g + 1) * KT],
                                               kn[:, tile % 2, g * 128:(g + 1) * 128], k.ident[0:KT, 0:KT])
                last.then_inc(turned[bank], 1)

            def task(i, kind, e, n, bank, use):
                j, h = e // HP, e % HP
                step = 2 * HP * i + e
                if kind == "scores":
                    if e == 0:
                        pe.wait_ge(s.q_in, 16 * i + 16)
                    if h == 0:
                        pe.wait_ge(s.v_copied, NKT * (2 * i + j + 1))
                        for b in range(2):
                            pe.wait_ge(copied[b], use[b])
                    pe.wait_ge(s.exped, step)
                    for b in range(NKS):
                        last = nc.tensor.matmul(ps_s[0:PT, b, 0:KS], qT[:, j, 2 * h:2 * h + 2, :],
                                                kT[:, j, h // 2, b * KS:(b + 1) * KS], start=True, stop=True)
                    last.then_inc(s.scored, 1)
                elif kind == "turn_keys":
                    slot, count = key_tile(i, e, n)
                    turn_keys(n, count, bank, use)
                elif kind == "make":
                    slot, count = key_tile(i, e, n)
                    pn = PIECES * (j + 1) + n // QT
                    make(pn % 2, count, n, PIECES * i + pn // 2)
                elif kind == "turn_probs":
                    if n == 0:
                        pe.wait_ge(s.probn, step + 1)
                    pe.wait_ge(copied[bank], use)
                    for x in range(QT):
                        last = nc.tensor.transpose(ps_t[0:KT, bank, x * PT:(x + 1) * PT],
                                                   prob[:, e % 2, (n * QT + x) * KT:(n * QT + x + 1) * KT],
                                                   k.ident[0:PT, 0:PT])
                    last.then_inc(turned[bank], 1)
                elif kind == "values":
                    for b in range(2):
                        pe.wait_ge(copied[b], use[b])
                    pe.wait_ge(s.stored, step)
                    if e == 0:
                        pe.wait_ge(s.added, i)
                    for x in range(NKT):
                        last = nc.tensor.matmul(ps_o[:, 0, 0:PT], val[:, j, x, h // 2 * 128:(h // 2 + 1) * 128],
                                                pT[:, x, :], start=(x == 0), stop=(x == NKT - 1))
                    last.then_inc(s.pv, 1)
                elif kind == "project":
                    pe.wait_ge(s.weights, 32)
                    pe.wait_ge(s.stored, 2 * HP * i + 2 * HP)
                    for x in range(XH):
                        last = nc.tensor.matmul(ps_o[0:PT, 0, 0:HID], oT[:, x, :], wo[:, x, :],
                                                start=(x == 0), stop=(x == XH - 1))
                    last.then_inc(s.projected, 1)

            pe.wait_ge(s.weights, 16)
            for tile in range(NKT):
                make(tile // QT % 2, tile, tile, tile // QT // 2)
                if tile:
                    turn_keys(tile - 1, tile - 1, (tile - 1) % 2, (tile - 1) // 2)
            turn_keys(NKT - 1, NKT - 1, (NKT - 1) % 2, (NKT - 1) // 2)
            pairs(pe, task)

        def copy_keys(eng, copy, slot, tile, bank, use):
            eng.wait_ge(turned[bank], use + 1)
            copy(kT[:, slot, :, tile * KT:(tile + 1) * KT],
                 ps_t[:, bank, 0:XKV * KT].rearrange("d (g n) -> d g n", g=XKV)).then_inc(copied[bank], 1)

        def copy_probs(eng, copy, r, bank, use):
            eng.wait_ge(turned[bank], use + 1)
            copy(pT[:, r * QT:(r + 1) * QT, :].rearrange("q x n -> q (x n)"), ps_t[0:KT, bank, 0:QT * PT])\
                .then_inc(copied[bank], 1)

        @block.scalar
        def _(act):
            def make(slot, tile, count):
                act.wait_ge(s.k_ps, count + 1)
                act.wait_ge(s.k_ssq, count)
                nc.scalar.square(ksq[:], ps_k[0:KT, 0, :]).then_inc(s.k_sq, 1)
                act.wait_ge(s.v_ps, count + 1)
                nc.scalar.copy(val[:, slot, tile, :], ps_v[0:KT, 0, :]).then_inc(s.v_copied, 1)

            def task(i, kind, e, n, bank, use):
                j, h = e // HP, e % HP
                step = 2 * HP * i + e
                if kind == "exp":
                    act.wait_ge(s.negmax, step + 1)
                    nc.scalar.activation(prob[:, e % 2, :].rearrange("q (b n) -> q b n", b=NKS), ps_s[0:PT, :, 0:KS],
                                         ACT.Exp, bias=negmax[:, e % 2:e % 2 + 1],
                                         accum_out=total[:, e % 2:e % 2 + 1]).then_inc(s.exped, 1)
                elif kind == "make":
                    slot, count = key_tile(i, e, n)
                    make(slot, n, count)
                elif kind == "turn_keys" and bank == 0:
                    copy_keys(act, nc.scalar.copy, key_tile(i, e, n)[0], n, bank, use)
                elif kind == "turn_probs" and bank == 0:
                    copy_probs(act, nc.scalar.copy, n, bank, use)
                elif kind == "values":
                    act.wait_ge(s.pv, step + 1)
                    if e == 0:
                        act.wait_ge(s.projected, i)
                    nc.scalar.copy(oT[:, 2 * h:2 * h + 2, j * SEQ:(j + 1) * SEQ],
                                   ps_o[:, 0, 0:PT].rearrange("d (h n) -> d h n", h=2)).then_inc(s.stored, 1)

            for tile in range(NKT):
                make(0, tile, tile)
                if tile and (tile - 1) % 2 == 0:
                    copy_keys(act, nc.scalar.copy, 0, tile - 1, 0, (tile - 1) // 2)
            pairs(act, task)

        @block.gpsimd
        def _(pool):
            def root(count):
                pool.wait_ge(s.k_mean, count + 1)
                nc.gpsimd.tensor_tensor(krms[:], kmean[:], k.minus_half[0:KT, 0:4], ALU.pow).then_inc(s.k_rms, 1)

            def task(i, kind, e, n, bank, use):
                if kind == "make":
                    root(key_tile(i, e, n)[1])

            for tile in range(NKT):
                root(tile)
            pairs(pool, task)

        @block.vector
        def _(dve):
            def make(count, tile):
                dve.wait_ge(s.k_sq, count + 1)
                nc.vector.tensor_reduce(kssq[:], quad(ksq[:]), AX.X, ALU.add).then_inc(s.k_ssq, 1)
                dve.wait_ge(s.k_ssq, count + 1)
                nc.vector.tensor_scalar(kmean[:], kssq[:], 1.0 / XD, 1e-6, ALU.mult, ALU.add).then_inc(s.k_mean, 1)
                dve.wait_ge(s.k_rms, count + 1)
                nc.vector.tensor_tensor(quad(kn[:, tile % 2, :]), quad(ps_k[0:KT, 0, :]),
                                        krms[:].unsqueeze(2).broadcast_to([KT, 4, 128]), ALU.mult)\
                    .then_inc(s.k_normed, 1)

            def task(i, kind, e, n, bank, use):
                j, h = e // HP, e % HP
                step = 2 * HP * i + e
                if kind == "scores":
                    dve.wait_ge(s.scored, step + 1)
                    nc.vector.tensor_reduce(negmax[:, e % 2:e % 2 + 1], ps_s[0:PT, :, 0:KS], AX.XY, ALU.max,
                                            negate=True).then_inc(s.negmax, 1)
                elif kind == "make":
                    slot, count = key_tile(i, e, n)
                    make(count, n)
                elif kind == "norm":
                    dve.wait_ge(s.exped, step + 1)
                    nc.vector.reciprocal(rtotal[:, e % 2:e % 2 + 1], total[:, e % 2:e % 2 + 1]).then_inc(s.rtotal, 1)
                    dve.wait_ge(s.rtotal, step + 1)
                    nc.vector.tensor_scalar_mul(prob[:, e % 2, :], prob[:, e % 2, :],
                                                rtotal[:, e % 2:e % 2 + 1]).then_inc(s.probn, 1)
                elif kind == "turn_keys" and bank == 1:
                    copy_keys(dve, nc.vector.tensor_copy, key_tile(i, e, n)[0], n, bank, use)
                elif kind == "turn_probs" and bank == 1:
                    copy_probs(dve, nc.vector.tensor_copy, n, bank, use)
                elif kind == "project":
                    dve.wait_ge(s.projected, i + 1)
                    nc.vector.tensor_tensor(k.x[:, i, :], k.x[:, i, :], ps_o[0:PT, 0, 0:HID], ALU.add)\
                        .then_inc(s.added, 1)

            for tile in range(NKT):
                make(tile, tile)
                if tile and (tile - 1) % 2 == 1:
                    copy_keys(dve, nc.vector.tensor_copy, 0, tile - 1, 1, (tile - 1) // 2)
            copy_keys(dve, nc.vector.tensor_copy, 0, NKT - 1, 1, (NKT - 1) // 2)
            pairs(dve, task)


def grouped_attention(nc, k, t):
    k.scratch_q = nc.dram_tensor("scratch_q", [PAIRS, 128, 2, XH, SEQ], F32, kind="Internal").ap()
    grouped_queries(nc, k, t)
    grouped_softmax(nc, k, t)


def lora_slots(nc, k, t):
    ER = E1 * R1
    with ExitStack() as ctx:
        a1 = sb(nc, ctx, "ls_a1", [128, CC, ER])
        chosen = sb(nc, ctx, "ls_chosen", [PT, 2, PAIRS, E1])
        z = sb(nc, ctx, "ls_z", [PT, 2, PAIRS, 128])
        ps = pb(nc, ctx, "ls_ps", 1)
        pt = pb(nc, ctx, "ls_pt", 4)
        s = sems(nc, ctx, "ls", "loaded product onehot chosen weight scaled zeroed masked turned copied summed")
        block = ctx.enter_context(nc.Block())
        psv = ps[0:PT, 0, :].rearrange("q (p n) -> q p n", p=PAIRS)

        @block.sync
        def _(sp):
            sp.dma_start(a1[:], t["l_a1"]).then_inc(s.loaded, 16)

        @block.gpsimd
        def _(pool):
            nc.gpsimd.memset(z[:], 0.0).then_inc(s.zeroed, 1)

        @block.tensor
        def _(pe):
            pe.wait_ge(s.loaded, 16)
            for p in range(PAIRS):
                for c in range(CC):
                    last = nc.tensor.matmul(psv[:, p, :], k.xnT[:, c, p * PT:(p + 1) * PT], a1[:, c, :],
                                            start=(c == 0), stop=(c == CC - 1))
            last.then_inc(s.product, 1)
            for m in range(2):
                for half in range(2):
                    pe.wait_ge(s.masked, (m + 1) * PAIRS)
                    for e in range(HPAIRS):
                        last = nc.tensor.transpose(pt[:, 2 * m + half, e * PT:(e + 1) * PT],
                                                   z[:, m, half * HPAIRS + e, :], k.ident[0:PT, 0:PT])
                    last.then_inc(s.turned, 1)

        @block.scalar
        def _(act):
            for n in range(4):
                act.wait_ge(s.turned, n + 1)
                nc.scalar.copy(k.zT[:, n // 2, (n % 2) * HALF:(n % 2 + 1) * HALF], pt[:, n, 0:HALF])\
                    .then_inc(s.copied, 1)

        @block.vector
        def _(dve):
            for m in range(2):
                nc.vector.tensor_scalar(k.onehot[:, m], k.rank[:], float(m), None, ALU.is_equal).then_inc(s.onehot, 1)
                dve.wait_ge(s.onehot, m + 1)
                nc.vector.tensor_tensor(chosen[:, m], k.onehot[:, m], k.prob[:], ALU.mult).then_inc(s.chosen, 1)
                dve.wait_ge(s.chosen, m + 1)
                nc.vector.tensor_reduce(k.wchoice[:, m, :], chosen[:, m], AX.X, ALU.add).then_inc(s.weight, 1)
                nc.vector.tensor_scalar_mul(k.onehotw[:, m], chosen[:, m], LSCALE).then_inc(s.scaled, 1)
            dve.wait_ge(s.weight, 2)
            nc.vector.tensor_tensor(k.wsum[:], k.wchoice[:, 0, :], k.wchoice[:, 1, :], ALU.add).then_inc(s.summed, 1)
            dve.wait_ge(s.product, 1)
            dve.wait_ge(s.zeroed, 1)
            for m in range(2):
                for p in range(PAIRS):
                    nc.vector.scalar_tensor_tensor(out=z[:, m, p, 0:ER].rearrange("q (e r) -> q e r", r=R1),
                                                   in0=psv[:, p, :].rearrange("q (e r) -> q e r", r=R1), scalar=LSCALE,
                                                   in1=k.onehot[:, m, p, :].unsqueeze(2).broadcast_to([PT, E1, R1]),
                                                   op0=ALU.mult, op1=ALU.mult).then_inc(s.masked, 1)


def lora_mlp(nc, k, t):
    FT = F1 // 128
    ER = E1 * R1
    with ExitStack() as ctx:
        w1 = sb(nc, ctx, "lm_w1", [128, CC, F1])
        b1x = sb(nc, ctx, "lm_b1x", [128, F1])
        b1 = sb(nc, ctx, "lm_b1", [128, FT])
        w2a2 = sb(nc, ctx, "lm_w2a2", [128, FT, HID + ER])
        b2x = sb(nc, ctx, "lm_b2x", [128, HID])
        b2 = sb(nc, ctx, "lm_b2", [PT, HID])
        hT = sb(nc, ctx, "lm_hT", [128, 2, FT, TOK])
        z2 = sb(nc, ctx, "lm_z2", [PT, PAIRS, 128])
        part = sb(nc, ctx, "lm_part", [PT, 2, ER])
        z2T = sb(nc, ctx, "lm_z2T", [128, TOK])
        up = pb(nc, ctx, "lm_up", 4)
        down = pb(nc, ctx, "lm_down", 2)
        pt = pb(nc, ctx, "lm_pt", 2)
        s = sems(nc, ctx, "lm", "loaded upped gelued downed weighed parted zeroed summed turned copied last added")
        block = ctx.enter_context(nc.Block())
        N = 4 * FT

        @block.sync
        def _(sp):
            for dst, name in ((w1, "l_w1"), (b1x, "l_b1x"), (b1, "l_b1"), (w2a2, "l_w2a2"), (b2x, "l_b2x"), (b2, "l_b2")):
                sp.dma_start(dst[:], t[name]).then_inc(s.loaded, 16)

        @block.gpsimd
        def _(pool):
            nc.gpsimd.memset(z2[:], 0.0).then_inc(s.zeroed, 1)

        @block.tensor
        def _(pe):
            pe.wait_ge(s.loaded, 96)
            for n in range(N):
                f, m, half = n // 4, n // 2 % 2, n % 2
                if n >= 4:
                    pe.wait_ge(s.gelued, n - 3)
                cols = slice(half * HALF, (half + 1) * HALF)
                for c in range(CC):
                    nc.tensor.matmul(up[:, n % 4, 0:HALF], w1[:, c, f * 128:(f + 1) * 128], k.xnT[:, c, cols],
                                     start=(c == 0), stop=False)
                nc.tensor.matmul(up[:, n % 4, 0:HALF], b1x[:, f * 128:(f + 1) * 128], k.zT[:, m, cols],
                                 start=False, stop=True).then_inc(s.upped, 1)
            pe.wait_ge(s.gelued, N)
            for n in range(2 * PAIRS):
                p, m = n // 2, n % 2
                if n >= 2:
                    pe.wait_ge(s.parted, n - 1)
                for f in range(FT):
                    last = nc.tensor.matmul(down[0:PT, m, 0:HID + ER], hT[:, m, f, p * PT:(p + 1) * PT],
                                            w2a2[:, f, :], start=(f == 0), stop=(f == FT - 1))
                last.then_inc(s.downed, 1)
            for half in range(2):
                pe.wait_ge(s.summed, (half + 1) * HPAIRS)
                for e in range(HPAIRS):
                    last = nc.tensor.transpose(pt[:, half, e * PT:(e + 1) * PT], z2[:, half * HPAIRS + e, :],
                                               k.ident[0:PT, 0:PT])
                last.then_inc(s.turned, 1)
            for p in range(PAIRS):
                pe.wait_ge(s.copied, p // HPAIRS + 1)
                if p >= 4:
                    pe.wait_ge(s.added, p - 3)
                nc.tensor.matmul(up[0:PT, p % 4, 0:HID], z2T[:, p * PT:(p + 1) * PT], b2x[:],
                                 start=True, stop=True).then_inc(s.last, 1)

        @block.scalar
        def _(act):
            act.wait_ge(s.loaded, 96)
            for n in range(N):
                f, m, half = n // 4, n // 2 % 2, n % 2
                act.wait_ge(s.upped, n + 1)
                nc.scalar.activation(hT[:, m, f, half * HALF:(half + 1) * HALF], up[:, n % 4, 0:HALF],
                                     ACT.Gelu_apprx_tanh, bias=b1[:, f:f + 1]).then_inc(s.gelued, 1)
            for half in range(2):
                act.wait_ge(s.turned, half + 1)
                nc.scalar.copy(z2T[:, half * HALF:(half + 1) * HALF], pt[:, half, 0:HALF]).then_inc(s.copied, 1)

        @block.vector
        def _(dve):
            dve.wait_ge(s.loaded, 96)
            for p in range(PAIRS):
                nc.vector.scalar_tensor_tensor(out=k.x[:, p, :], in0=b2[:], scalar=k.wsum[:, p:p + 1],
                                               in1=k.x[:, p, :], op0=ALU.mult, op1=ALU.add).then_inc(s.weighed, 1)
            dve.wait_ge(s.zeroed, 1)
            for n in range(2 * PAIRS):
                p, m = n // 2, n % 2
                dve.wait_ge(s.downed, n + 1)
                dve.wait_ge(s.weighed, PAIRS + n if m else p + 1)
                nc.vector.scalar_tensor_tensor(out=k.x[:, p, :], in0=down[0:PT, m, 0:HID],
                                               scalar=k.wchoice[:, m, p:p + 1], in1=k.x[:, p, :],
                                               op0=ALU.mult, op1=ALU.add).then_inc(s.weighed, 1)
                if n >= 2:
                    dve.wait_ge(s.summed, n // 2)
                nc.vector.tensor_tensor(part[:, m, :].rearrange("q (e r) -> q e r", r=R1),
                                        down[0:PT, m, HID:HID + ER].rearrange("q (e r) -> q e r", r=R1),
                                        k.onehotw[:, m, p, :].unsqueeze(2).broadcast_to([PT, E1, R1]), ALU.mult)\
                    .then_inc(s.parted, 1)
                if m:
                    dve.wait_ge(s.parted, n + 1)
                    nc.vector.tensor_tensor(z2[:, p, 0:ER], part[:, 0, :], part[:, 1, :], ALU.add).then_inc(s.summed, 1)
            dve.wait_ge(s.weighed, 3 * PAIRS)
            for p in range(PAIRS):
                dve.wait_ge(s.last, p + 1)
                nc.vector.tensor_tensor(k.x[:, p, :], k.x[:, p, :], up[0:PT, p % 4, 0:HID], ALU.add)\
                    .then_inc(s.added, 1)


def routed_lora(nc, k, t):
    with ExitStack() as ctx:
        k.t = t
        k.prob = sb(nc, ctx, "rl_prob", [PT, PAIRS, E1])
        k.rank = sb(nc, ctx, "rl_rank", [PT, PAIRS, E1])
        k.onehot = sb(nc, ctx, "rl_onehot", [PT, 2, PAIRS, E1])
        k.onehotw = sb(nc, ctx, "rl_onehotw", [PT, 2, PAIRS, E1])
        k.wchoice = sb(nc, ctx, "rl_wchoice", [PT, 2, PAIRS])
        k.wsum = sb(nc, ctx, "rl_wsum", [PT, PAIRS])
        k.zT = sb(nc, ctx, "rl_zT", [128, 2, TOK])
        route(nc, k, "r1", t["r1_w"], t["r1_b"])
        lora_slots(nc, k, t)
        lora_mlp(nc, k, t)


def decoder(nc, t, out, stages=range(6)):
    with ExitStack() as ctx:
        k = Shared()
        k.x = sb(nc, ctx, "x", [PT, PAIRS, HID])
        k.xnT = sb(nc, ctx, "xnT", [128, CC, TOK])
        k.ident = sb(nc, ctx, "ident", [128, 128])
        k.ones = sb(nc, ctx, "ones", [128, 128])
        k.minus_half = sb(nc, ctx, "minus_half", [128, 48])
        k.eps6 = sb(nc, ctx, "eps6", [128, 32])
        k.half = sb(nc, ctx, "half", [128, 8])
        load_constants(nc, k, t)
        sublayers = [gated_delta_rule, context_attention, routed_swiglu, feature_attention,
                     grouped_attention, routed_lora]
        for i in stages:
            layernorm(nc, k, f"ln{i}")
            sublayers[i](nc, k, t)
        store_result(nc, k, out)


def lay_out(**inputs):
    a = {n: np.asarray(v) for n, v in inputs.items()}
    f = np.ascontiguousarray

    def chunked(w):
        return f(w.T.reshape(-1, 128, w.shape[0]).transpose(1, 0, 2))

    def rows(v, n):
        return f(np.broadcast_to(v, (n, v.size)))

    o = {"x": f(a["x"].reshape(TOK, HID)), "ident": np.eye(128, dtype=np.float32)}

    w = a["L0_attn_W_qkv"]
    cw = a["L0_attn_conv_w"]
    qd = NK * DK
    per_head = []
    for h in range(NK):
        r0 = [qd + h * DK, h * DK, 2 * qd + 2 * h * DK, 2 * qd + (2 * h + 1) * DK]
        mats = np.stack([chunked(w[r:r + DK]) for r in r0], axis=1)
        taps = np.stack([cw[r:r + DK] for r in r0], axis=1)
        per_head.append(np.concatenate([mats.reshape(128, -1), taps.reshape(128, -1)], axis=1))
    o["gdn_w"] = f(np.stack(per_head))
    o["gdn_wba"] = chunked(np.concatenate([a["L0_attn_W_b"], a["L0_attn_W_a"]]))
    o["gdn_rows"] = rows(np.concatenate([a["L0_attn_dt_bias"], a["L0_attn_A_log"]]), PT)
    o["gdn_normw"] = rows(a["L0_attn_norm_w"], PT)
    o["gdn_wz"] = f(np.stack([chunked(a["L0_attn_W_z"][g * GV * 128:(g + 1) * GV * 128]) for g in range(GROUPS)]))
    o["gdn_wo"] = f(a["L0_attn_W_out"].T.reshape(GROUPS, GV, 128, HID).transpose(0, 2, 1, 3))
    r, c = np.arange(PT)[:, None], np.arange(PT)[None, :]
    same = (r // SEQ) == (c // SEQ)
    o["gdn_after"] = (same & (c < r)).astype(np.float32)
    o["gdn_upto"] = (same & (r <= c)).astype(np.float32)
    o["gdn_kqmask"] = f(np.concatenate([-(same & (r < c)).astype(np.float32),
                                        (same & (r <= c)).astype(np.float32)], axis=1))

    o["context"] = a["ctx_2048"]
    for n in "qkvo":
        o[f"c_w{n}"] = chunked(a[f"L0_xattn_w{n}"])

    o["r0_w"] = chunked(a["L0_ffn_gate_w"])
    e = np.arange(E0)
    o["earlier"] = rows((e[None, :] < e[:, None]).astype(np.float32).reshape(-1), PT)
    w1, w2, w3 = a["L0_ffn_w1"], a["L0_ffn_w2"], a["L0_ffn_w3"]
    o["s_w"] = f(np.stack([np.concatenate([chunked(w1[i]).reshape(128, -1), chunked(w3[i]).reshape(128, -1),
                                           chunked(w2[i]).reshape(128, -1)], axis=1) for i in range(E0)]))

    o["f_w"] = chunked(np.concatenate([a["L1_attn_Wq"], a["L1_attn_Wk"], a["L1_attn_Wv"]]))
    o["f_b"] = rows(np.concatenate([a["L1_attn_bq"], a["L1_attn_bk"], a["L1_attn_bv"]]), PT)
    o["f_wo"] = chunked(a["L1_attn_Wo"])
    o["f_bo"] = rows(a["L1_attn_bo"], PT)
    inv = (1.0 / np.float32(10000.0) ** (np.arange(0, AD, 2, dtype=np.float32) / AD)).astype(np.float32)
    ang = np.arange(SEQ, dtype=np.float32)[:, None] * inv[None, :]
    ang = np.concatenate([ang, ang], axis=1)
    sign = np.where(np.arange(AD) < AF, -1.0, 1.0).astype(np.float32)
    o["f_cos"] = f(np.tile(np.cos(ang), (2, 1)))
    o["f_sin"] = f(np.tile(np.sin(ang) * sign, (2, 1)))
    diag = np.zeros((128 // AD, AD, 128 // AD, AF), np.float32)
    for i in range(128 // AD):
        diag[i, :, i, :] = a["L1_attn_rand_matrix"].T
    o["f_r"] = f(diag.reshape(128, -1))

    o["x_wq"] = chunked(a["L1_xattn_Wq"].T)
    o["x_nw"] = f(np.stack([a["L1_xattn_q_norm_w"], a["L1_xattn_k_norm_w"]], axis=1))
    o["x_wkv"] = chunked(np.concatenate([a["L1_xattn_Wk"], a["L1_xattn_Wv"]], axis=1).T)
    o["x_wo"] = chunked(a["L1_xattn_Wo"].T)
    o["x_ctxT"] = f(a["ctx_2048"].reshape(BATCH * NKS, KS, CC, 128).transpose(0, 3, 2, 1))

    o["r1_w"] = chunked(a["L1_ffn_W_r"])
    o["r1_b"] = rows(a["L1_ffn_b_r"], PT)
    o["l_a1"] = chunked(a["L1_ffn_A1"].reshape(E1 * R1, HID))
    o["l_w1"] = chunked(a["L1_ffn_W1"])
    pad = np.zeros((128 - E1 * R1, F1), np.float32)
    o["l_b1x"] = f(np.concatenate([a["L1_ffn_B1"].transpose(0, 2, 1).reshape(E1 * R1, F1), pad]))
    o["l_b1"] = f(a["L1_ffn_b1"].reshape(F1 // 128, 128).T)
    o["l_w2a2"] = chunked(np.concatenate([a["L1_ffn_W2"], a["L1_ffn_A2"].reshape(E1 * R1, F1)]))
    o["l_b2x"] = f(np.concatenate([a["L1_ffn_B2"].transpose(0, 2, 1).reshape(E1 * R1, HID), pad[:, 0:HID]]))
    o["l_b2"] = rows(a["L1_ffn_b2"], PT)
    return o


def kernel(**inputs):
    import concourse.bacc as _bacc
    from concourse.bass_utils import run_bass_kernel_spmd as _run

    arrays = lay_out(**inputs)
    nc = _bacc.Bacc("TRN2", target_bir_lowering=False, num_devices=1)
    t = {n: nc.dram_tensor(n, v.shape, mybir.dt.from_np(v.dtype), kind="ExternalInput").ap()
         for n, v in arrays.items()}
    out = nc.dram_tensor("out", (TOK, HID), F32, kind="ExternalOutput").ap()
    decoder(nc, t, out)
    r = _run(nc, [arrays], core_ids=[0])
    return r.results[0]["out"].reshape(BATCH, SEQ, HID)
```

```python
from collections import namedtuple
from contextlib import ExitStack

import numpy as np

import concourse.bass as bass
from concourse import mybir

F32 = mybir.dt.float32
F32R = mybir.dt.float32r
ALU = mybir.AluOpType
ACT = mybir.ActivationFunctionType
AX = mybir.AxisListType

BATCH, SEQ, HID = 16, 56, 256
PAIRS = BATCH // 2
PT = 2 * SEQ
TOK = BATCH * SEQ
HALF = TOK // 2
HPAIRS = PAIRS // 2
CC = HID // 128
BANK = 512

SPLIT_TERMS = ((0, 0), (0, 1), (1, 0))

NK, DK, NV, KC = 16, 128, 32, 4
VPK = NV // NK
GROUPS = 4
GK = NK // GROUPS
GV = GK * VPK
SYS = PAIRS * GV
UNITS = PAIRS * GV // 4
BLK = SEQ // 2

CTX, KT = 1500, 125
NKT = CTX // KT
KS = 500
NKS = CTX // KS

E0, F0 = 8, 512
E1, R1, F1 = 8, 8, 1024
LSCALE = 2.0

AH, AHKV, AD = 16, 8, 16
AF = AD // 2
QKH = AH + AHKV

XH, XKV, XD = 16, 4, 128
XG = XH // XKV


class Shared:
    pass


def sb(nc, ctx, name, shape, dt=F32):
    return ctx.enter_context(nc.sbuf_tensor(f"{name}_sb", list(shape), dt))


def pb(nc, ctx, name, banks):
    return ctx.enter_context(nc.psum_tensor(name, [128, banks, BANK], F32))


def sem(nc, ctx, name):
    handle = nc.alloc_semaphore(name)
    ctx.callback(nc.clear_and_free_semaphores, [handle])
    return handle


def sems(nc, ctx, tag, names, pairs=""):
    ctx.callback(nc.all_engine_barrier)
    found = [sem(nc, ctx, f"{tag}_{n}") for n in names.split()]
    found += [[sem(nc, ctx, f"{tag}_{n}{j}") for j in range(2)] for n in pairs.split()]
    return namedtuple("Semaphores", f"{names} {pairs}")(*found)


def load_constants(nc, k, t):
    with ExitStack() as ctx:
        s = sems(nc, ctx, "init", "loaded filled")
        block = ctx.enter_context(nc.Block())

        @block.sync
        def _(sp):
            sp.dma_start(k.x[:], t["x"].rearrange("(p q) d -> q p d", q=PT)).then_inc(s.loaded, 16)
            sp.dma_start(k.ident[:], t["ident"]).then_inc(s.loaded, 16)
            sp.wait_ge(s.loaded, 32)

        @block.gpsimd
        def _(pool):
            nc.gpsimd.memset(k.ones[:], 1.0).then_inc(s.filled, 1)
            nc.gpsimd.memset(k.minus_half[:], -0.5).then_inc(s.filled, 1)
            nc.gpsimd.memset(k.half[:], 0.5).then_inc(s.filled, 1)
            nc.gpsimd.memset(k.eps6[:], 1e-6).then_inc(s.filled, 1)
            pool.wait_ge(s.filled, 4)


def store_result(nc, k, out):
    with ExitStack() as ctx:
        s = sems(nc, ctx, "end", "stored")
        block = ctx.enter_context(nc.Block())

        @block.sync
        def _(sp):
            sp.dma_start(out.rearrange("(p q) d -> q p d", q=PT), k.x[:]).then_inc(s.stored, 16)
            sp.wait_ge(s.stored, 16)


def layernorm(nc, k, tag):
    with ExitStack() as ctx:
        stats = sb(nc, ctx, f"{tag}_stats", [PT, PAIRS, 6])
        meanvar = sb(nc, ctx, f"{tag}_meanvar", [PT, PAIRS, 2])
        vareps = sb(nc, ctx, f"{tag}_vareps", [PT, PAIRS])
        rstd = sb(nc, ctx, f"{tag}_rstd", [PT, PAIRS])
        xn = sb(nc, ctx, f"{tag}_xn", [PT, PAIRS, HID])
        ps = pb(nc, ctx, f"{tag}_ps", 4)
        s = sems(nc, ctx, tag, "stats meanvar var_ready rstd_ready xn_ready turned copied")
        block = ctx.enter_context(nc.Block())

        @block.vector
        def _(dve):
            for p in range(PAIRS):
                nc.vector.bn_stats(stats[:, p, :], k.x[:, p, :]).then_inc(s.stats, 1)
            for p in range(PAIRS):
                dve.wait_ge(s.stats, p + 1)
                nc.vector.bn_aggr(meanvar[:, p, :], stats[:, p, :]).then_inc(s.meanvar, 1)
            dve.wait_ge(s.meanvar, PAIRS)
            nc.vector.tensor_scalar_add(vareps[:], meanvar[:, :, 1], 1e-5).then_inc(s.var_ready, 1)
            dve.wait_ge(s.rstd_ready, 1)
            for p in range(PAIRS):
                nc.vector.tensor_scalar(xn[:, p, :], k.x[:, p, :], meanvar[:, p, 0:1], rstd[:, p:p + 1],
                                        ALU.subtract, ALU.mult).then_inc(s.xn_ready, 1)
            for b in (1, 3):
                dve.wait_ge(s.turned, b + 1)
                nc.vector.tensor_copy(k.xnT[:, b % CC, (b // CC) * HALF:(b // CC + 1) * HALF],
                                      ps[:, b, 0:HALF]).then_inc(s.copied, 1)

        @block.gpsimd
        def _(pool):
            pool.wait_ge(s.var_ready, 1)
            nc.gpsimd.tensor_tensor(rstd[:], vareps[:], k.minus_half[0:PT, 0:PAIRS], ALU.pow)\
                .then_inc(s.rstd_ready, 1)

        @block.tensor
        def _(pe):
            for b in range(4):
                pe.wait_ge(s.xn_ready, HPAIRS * (b // CC + 1))
                for p in range(HPAIRS):
                    last = nc.tensor.transpose(ps[:, b, p * PT:(p + 1) * PT],
                                               xn[:, (b // CC) * HPAIRS + p, (b % CC) * 128:(b % CC + 1) * 128],
                                               k.ident[0:PT, 0:PT])
                last.then_inc(s.turned, 1)

        @block.scalar
        def _(act):
            for b in (0, 2):
                act.wait_ge(s.turned, b + 1)
                nc.scalar.copy(k.xnT[:, b % CC, (b // CC) * HALF:(b // CC + 1) * HALF],
                               ps[:, b, 0:HALF]).then_inc(s.copied, 1)


def overlap_view(tensor, base, count, width):
    first = tensor[:, base, 0:width]
    return bass.AP(tensor=first.tensor, offset=first.offset, ap=[list(first.ap[0]), [1, count], [1, width]])


def gdn_gates(nc, k, t):
    with ExitStack() as ctx:
        wba = sb(nc, ctx, "gg_wba", [128, CC, 2 * NV])
        rows = sb(nc, ctx, "gg_rows", [PT, 2 * NV])
        exp_b = sb(nc, ctx, "gg_exp_b", [PT, PAIRS, NV])
        onep = sb(nc, ctx, "gg_onep", [PT, PAIRS, NV])
        a = sb(nc, ctx, "gg_a", [PT, PAIRS, NV])
        absa = sb(nc, ctx, "gg_absa", [PT, PAIRS, NV])
        exp_a = sb(nc, ctx, "gg_exp_a", [PT, PAIRS, NV])
        ln_a = sb(nc, ctx, "gg_ln_a", [PT, PAIRS, NV])
        dt = sb(nc, ctx, "gg_dt", [PT, PAIRS, NV])
        rate = sb(nc, ctx, "gg_rate", [PT, NV])
        ps = pb(nc, ctx, "gg_ps", 1)
        s = sems(nc, ctx, "gg", "loaded product expb onep a_ready absa expa lna rate dt_ready done")
        block = ctx.enter_context(nc.Block())
        psv = ps[0:PT, 0, :].rearrange("q (p n) -> q p n", p=PAIRS)

        @block.sync
        def _(sp):
            sp.dma_start(wba[:], t["gdn_wba"]).then_inc(s.loaded, 16)
            sp.dma_start(rows[:], t["gdn_rows"]).then_inc(s.loaded, 16)
            sp.dma_start(k.after[:], t["gdn_after"]).then_inc(s.loaded, 16)
            sp.dma_start(k.upto[:], t["gdn_upto"]).then_inc(s.loaded, 16)
            sp.dma_start(k.kqmask[:], t["gdn_kqmask"]).then_inc(s.loaded, 16)
            sp.dma_start(k.normw[:], t["gdn_normw"]).then_inc(s.loaded, 16)

        @block.tensor
        def _(pe):
            pe.wait_ge(s.loaded, 96)
            for p in range(PAIRS):
                for c in range(CC):
                    last = nc.tensor.matmul(psv[:, p, :], k.xnT[:, c, p * PT:(p + 1) * PT], wba[:, c, :],
                                            start=(c == 0), stop=(c == CC - 1))
            last.then_inc(s.product, 1)

        @block.scalar
        def _(act):
            act.wait_ge(s.product, 1)
            nc.scalar.activation(exp_b[:], psv[:, :, 0:NV], ACT.Exp, scale=-1.0).then_inc(s.expb, 1)
            nc.scalar.activation(rate[:], rows[:, NV:2 * NV], ACT.Exp).then_inc(s.rate, 1)
            act.wait_ge(s.absa, 1)
            nc.scalar.activation(exp_a[:], absa[:], ACT.Exp, scale=-1.0).then_inc(s.expa, 1)
            act.wait_ge(s.expa, 1)
            nc.scalar.activation(ln_a[:], exp_a[:], ACT.Ln, bias=1.0).then_inc(s.lna, 1)

        @block.vector
        def _(dve):
            dve.wait_ge(s.expb, 1)
            nc.vector.tensor_tensor(a[:], psv[:, :, NV:2 * NV],
                                    rows[:, 0:NV].unsqueeze(1).broadcast_to([PT, PAIRS, NV]), ALU.add)\
                .then_inc(s.a_ready, 1)
            dve.wait_ge(s.a_ready, 1)
            nc.vector.scalar_tensor_tensor(out=absa[:], in0=a[:], scalar=-1.0, in1=a[:],
                                           op0=ALU.mult, op1=ALU.max).then_inc(s.absa, 1)
            dve.wait_ge(s.expb, 1)
            nc.vector.tensor_scalar_add(onep[:], exp_b[:], 1.0).then_inc(s.onep, 1)
            dve.wait_ge(s.onep, 1)
            nc.vector.reciprocal(k.beta[:], onep[:]).then_inc(s.done, 1)
            dve.wait_ge(s.lna, 1)
            nc.vector.scalar_tensor_tensor(out=dt[:], in0=a[:], scalar=0.0, in1=ln_a[:],
                                           op0=ALU.max, op1=ALU.add).then_inc(s.dt_ready, 1)
            dve.wait_ge(s.dt_ready, 1)
            dve.wait_ge(s.rate, 1)
            nc.vector.scalar_tensor_tensor(out=k.logdecay[:], in0=dt[:], scalar=-1.0,
                                           in1=rate[:].unsqueeze(1).broadcast_to([PT, PAIRS, NV]),
                                           op0=ALU.mult, op1=ALU.mult).then_inc(s.done, 1)
            dve.wait_ge(s.done, 2)


def gdn_project(nc, k, t, grp, s, ctx):
    w = sb(nc, ctx, "gp_w", [128, 2, 4 * CC * 128 + 4 * KC])
    raw = sb(nc, ctx, "gp_raw", [128, 4, BATCH, KC - 1 + SEQ])
    conv = sb(nc, ctx, "gp_conv", [128, 2, 4, TOK])
    sq = sb(nc, ctx, "gp_sq", [128, 2, TOK])
    nsq = sb(nc, ctx, "gp_nsq", [PT, 2, PAIRS])
    nk = sb(nc, ctx, "gp_nk", [PT, PAIRS])
    proj = pb(nc, ctx, "gp_proj", 4)
    psk = pb(nc, ctx, "gp_psk", 2)
    psv = pb(nc, ctx, "gp_psv", 2)
    block = ctx.enter_context(nc.Block())
    wt = [w[:, j, 0:4 * CC * 128].rearrange("c (i k n) -> c i k n", i=4, k=CC) for j in range(2)]
    wc = [w[:, j, 4 * CC * 128:].rearrange("c (i k) -> c i k", i=4) for j in range(2)]
    STEPS = 4 * (KC - 2)

    def heads():
        for h in range(GK + 1):
            yield (h if h < GK else None), (h - 1 if h else None), grp * GK + h

    @block.sync
    def _(sp):
        for h in range(GK):
            if h >= 2:
                sp.wait_ge(s.conv_done, 4 * (grp * GK + h - 1))
            sp.dma_start(w[:, h % 2, :], t["gdn_w"][grp * GK + h]).then_inc(s.w_in[h % 2], 16)

    @block.tensor
    def _(pe):
        def project(h, n, q):
            if q == 0:
                pe.wait_ge(s.w_in[h % 2], 16 * (grp * 2 + h // 2) + 16)
            pe.wait_ge(s.evac, 8 * n + (q - 3 if q >= 4 else 0))
            for c in range(CC):
                last = nc.tensor.matmul(proj[:, q % 4, 0:HALF], wt[h % 2][:, q // 2, c, :],
                                        k.xnT[:, c, (q % 2) * HALF:(q % 2 + 1) * HALF],
                                        start=(c == 0), stop=(c == CC - 1))
            last.then_inc(s.projected, 1)

        def norms(h, n, which):
            pe.wait_ge(s.squared, 2 * n + which + 1)
            pe.wait_ge(s.v_done, 4 * n)
            for p in range(PAIRS):
                last = nc.tensor.matmul(psv[0:PT, 1, which * PAIRS + p:which * PAIRS + p + 1],
                                        sq[:, which, p * PT:(p + 1) * PT], k.ones[:, 0:1],
                                        start=True, stop=True)
            if which == 1:
                last.then_inc(s.ssq, 1)

        def products(h, n, quads):
            for gp in quads:
                pe.wait_ge(s.gm_done, 4 * n + (gp - 1 if gp >= 2 else 0))
                for e in range(2):
                    p = 2 * gp + e
                    last = nc.tensor.matmul(psk[0:PT, gp % 2, e * 2 * PT:(e + 1) * 2 * PT],
                                            conv[:, h % 2, 0, p * PT:(p + 1) * PT],
                                            conv[:, h % 2, 0:2, p * PT:(p + 1) * PT], start=True, stop=True)
                last.then_inc(s.kq_done, 1)

        def turn_values(h, n, tiles):
            for q in tiles:
                pe.wait_ge(s.conv_done, 4 * n + 3 + q // 2)
                if q == 1:
                    pe.wait_ge(s.nsq_ready, n + 1)
                pe.wait_ge(s.v_done, 4 * n + (q - 1 if q >= 2 else 0))
                for e in range(HPAIRS):
                    p = (q % 2) * HPAIRS + e
                    last = nc.tensor.transpose(psv[0:PT, q % 2, e * 128:(e + 1) * 128],
                                               conv[:, h % 2, 2 + q // 2, p * PT:(p + 1) * PT], k.ident[:])
                last.then_inc(s.v_turned[h % 2], 1)

        for new, old, n in heads():
            for part in range(4):
                for e in range(2):
                    if new is not None:
                        project(new, n, 2 * part + e)
                    if old is not None and part == 0:
                        norms(old, n - 1, e)
                if old is not None:
                    if part < 2:
                        products(old, n - 1, (2 * part, 2 * part + 1))
                    else:
                        turn_values(old, n - 1, (2 * part - 4, 2 * part - 3))

    @block.scalar
    def _(act):
        for h in range(GK):
            n = grp * GK + h
            if h >= 2:
                act.wait_ge(s.kq_done, 4 * (n - 1))
            for q in range(8):
                tile, half = q // 2, q % 2
                act.wait_ge(s.projected, 8 * n + q + 1)
                if h:
                    act.wait_ge(s.conv_done, 4 * (n - 1) + tile + 1)
                if q == 4 and h >= 2:
                    act.wait_ge(s.v_turned[h % 2], 4 * (grp * 2 + h // 2))
                src = proj[:, q % 4, 0:HALF]
                nc.scalar.copy(raw[:, tile, half * PAIRS:(half + 1) * PAIRS, KC - 1:],
                               src.rearrange("c (b t) -> c b t", t=SEQ))
                nc.scalar.mul(conv[:, h % 2, tile, half * HALF:(half + 1) * HALF], src,
                              wc[h % 2][:, tile, KC - 1:KC]).then_inc(s.evac, 1)

    @block.vector
    def _(dve):
        def convolve(h, n, tile):
            dve.wait_ge(s.evac, 8 * n + 2 * tile + 2)
            dst = conv[:, h % 2, tile, :].rearrange("c (b t) -> c b t", t=SEQ)
            for tap in range(KC - 1):
                if tap:
                    dve.wait_ge(s.conv_step, STEPS * n + 2 * tile + tap)
                done = s.conv_done if tap == KC - 2 else s.conv_step
                nc.vector.scalar_tensor_tensor(out=dst, in0=raw[:, tile, :, tap:tap + SEQ],
                                               scalar=wc[h % 2][:, tile, tap:tap + 1], in1=dst,
                                               op0=ALU.mult, op1=ALU.add).then_inc(done, 1)

        def norms(h, n):
            dve.wait_ge(s.ssq, n + 1)
            dve.wait_ge(s.roots, 2 * n)
            nc.vector.tensor_scalar_max(nsq[:], psv[0:PT, 1, 0:2 * PAIRS].rearrange("q (w p) -> q w p", w=2),
                                        1e-24).then_inc(s.nsq_ready, 1)
            dve.wait_ge(s.nsq_ready, n + 1)
            nc.vector.reciprocal(k.rnk2[:, h, :], nsq[:, 0, :]).then_inc(s.rnk2, 1)

        def mask(h, n, quads):
            for gp in quads:
                dve.wait_ge(s.kq_done, 4 * n + gp + 1)
                nc.vector.tensor_tensor(k.gmtt[:, h * PAIRS * 2 * PT:(h + 1) * PAIRS * 2 * PT]
                                        .rearrange("q (p w) -> q p w", p=PAIRS)[:, 2 * gp:2 * gp + 2, :],
                                        psk[0:PT, gp % 2, 0:4 * PT].rearrange("q (e w) -> q e w", e=2),
                                        k.kqmask[:].unsqueeze(1).broadcast_to([PT, 2, 2 * PT]),
                                        ALU.mult).then_inc(s.gm_done, 1)

        def values(h, n, tiles):
            dve.wait_ge(s.roots, 2 * n + 2)
            for q in tiles:
                dve.wait_ge(s.v_turned[h % 2], 4 * (grp * 2 + h // 2) + q + 1)
                nc.vector.tensor_tensor(k.v[:, h * VPK + q // 2, (q % 2) * HPAIRS:(q % 2 + 1) * HPAIRS, :],
                                        psv[0:PT, q % 2, :].rearrange("q (p d) -> q p d", p=HPAIRS),
                                        nk[:, (q % 2) * HPAIRS:(q % 2 + 1) * HPAIRS].unsqueeze(2)
                                        .broadcast_to([PT, HPAIRS, 128]), ALU.mult).then_inc(s.v_done, 1)

        nc.vector.memset(raw[:, :, :, 0:KC - 1], 0.0).then_inc(s.padded, 1)
        dve.wait_ge(s.padded, grp + 1)
        for new, old, n in heads():
            for part in range(4):
                if old is not None:
                    if part == 0:
                        norms(old, n - 1)
                    if part < 2:
                        mask(old, n - 1, (2 * part, 2 * part + 1))
                    else:
                        values(old, n - 1, (2 * part - 4, 2 * part - 3))
                if new is not None:
                    convolve(new, n, part)

    @block.gpsimd
    def _(pool):
        for new, old, n in heads():
            if old is not None:
                pool.wait_ge(s.nsq_ready, n)
                pool.wait_ge(s.v_done, 4 * (n - 1))
                nc.gpsimd.tensor_tensor(nk[:], nsq[:, 0, :], k.half[0:PT, 0:PAIRS], ALU.pow).then_inc(s.roots, 1)
                nc.gpsimd.tensor_tensor(k.rnq[:, old, :], nsq[:, 1, :], k.minus_half[0:PT, 0:PAIRS],
                                        ALU.pow).then_inc(s.roots, 1)
            if new is not None:
                pool.wait_ge(s.ssq, n)
                for which in range(2):
                    pool.wait_ge(s.conv_done, 4 * n + which + 1)
                    nc.gpsimd.tensor_tensor(sq[:, which, :], conv[:, new % 2, which, :], conv[:, new % 2, which, :],
                                            ALU.mult).then_inc(s.squared, 1)


def gdn_systems(nc, k, t, grp, s, ctx):
    cs = sb(nc, ctx, "gs_cs", [PT, PAIRS, GV])
    urhs = sb(nc, ctx, "gs_urhs", [PT, 2, 4, PT])
    dec = [sb(nc, ctx, f"gs_dec{j}", [PT, 4, PT + 1]) for j in range(2)]
    ps = pb(nc, ctx, "gs_ps", 2)
    block = ctx.enter_context(nc.Block())

    @block.gpsimd
    def _(pool):
        with pool.Fori(0, PAIRS) as p:
            for j in range(2):
                pool.wait_ge(s.emm[j], grp * PAIRS + p)
                nc.gpsimd.tensor_tensor(urhs[:, j], k.upto[:].unsqueeze(1).broadcast_to([PT, 4, PT]),
                                        k.logdecay[:, p, bass.ds(grp * GV + j * 4, 4)].unsqueeze(2)
                                        .broadcast_to([PT, 4, PT]), ALU.mult).then_inc(s.u_ready[j], 1)

    @block.tensor
    def _(pe):
        with pe.Fori(0, PAIRS) as p:
            for j in range(2):
                pe.wait_ge(s.u_ready[j], grp * PAIRS + p + 1)
                pe.wait_ge(s.dec_ready[j], grp * PAIRS + p)
                nc.tensor.matmul(ps[0:PT, j, 0:4 * PT], k.after[:], urhs[:, j], start=True, stop=True)\
                    .then_inc(s.emm[j], 1)

    @block.scalar
    def _(act):
        with act.Fori(0, PAIRS) as p:
            for j in range(2):
                act.wait_ge(s.emm[j], grp * PAIRS + p + 1)
                act.wait_ge(s.apt[j], 4 * (grp * PAIRS + p))
                nc.scalar.activation(dec[j][:, :, 1:], ps[0:PT, j, 0:4 * PT].rearrange("q (v w) -> q v w", v=4),
                                     ACT.Exp).then_inc(s.dec_ready[j], 1)

    @block.vector
    def _(dve):
        nc.vector.memset(dec[0][:, :, 0:1], 1.0).then_inc(s.lead, 1)
        nc.vector.memset(dec[1][:, :, 0:1], 1.0).then_inc(s.lead, 1)
        nc.vector.tensor_tensor(cs[:].rearrange("q p (h e) -> q p h e", e=VPK),
                                k.beta[:, :, bass.ds(grp * GV, GV)].rearrange("q p (h e) -> q p h e", e=VPK),
                                k.rnk2[:].rearrange("q h p -> q p h").unsqueeze(3)
                                .broadcast_to([PT, PAIRS, GK, VPK]), ALU.mult).then_inc(s.lead, 1)
        with dve.Fori(0, PAIRS) as p:
            for j in range(2):
                dve.wait_ge(s.lead, 3 * grp + 3)
                dve.wait_ge(s.dec_ready[j], grp * PAIRS + p + 1)
                for v in range(4):
                    vh = j * 4 + v
                    nc.vector.scalar_tensor_tensor(
                        out=k.apt[:, :, bass.ds(p * GV + vh, 1), :].rearrange("q a m w -> q a (m w)"),
                        in0=overlap_view(dec[j], v, 2, PT), scalar=cs[:, p, vh:vh + 1],
                        in1=k.gmtt[:, bass.ds((vh // VPK) * PAIRS * 2 * PT + p * 2 * PT, 2 * PT)]
                        .rearrange("q (a w) -> q a w", a=2),
                        op0=ALU.mult, op1=ALU.mult).then_inc(s.apt[j], 1)


def gdn_solve(nc, k, t, grp, s, ctx):
    wz = sb(nc, ctx, "gv_wz", [128, CC, GV * 128])
    sil = sb(nc, ctx, "gv_sil", [PT, 2, 512])
    ps = pb(nc, ctx, "gv_ps", 4)
    asys = sb(nc, ctx, "gv_asys", [2 * SYS, 2, BLK, BLK])
    tsys = sb(nc, ctx, "gv_tsys", [2 * SYS, 2, BLK, BLK])
    prod = sb(nc, ctx, "gv_prod", [2 * SYS, 2, BLK, BLK])
    block = ctx.enter_context(nc.Block())
    flat = lambda x: x.rearrange("m b r c -> m b (r c)")

    def upto(u):
        return grp * UNITS + u + 1

    @block.tensor
    def _(pe):
        pe.wait_ge(s.wz_in, 16 * grp + 16)
        for u in range(UNITS):
            p, q = u // 2, u % 2
            if u >= 4:
                pe.wait_ge(s.silu, upto(u - 4))
            for c in range(CC):
                last = nc.tensor.matmul(ps[0:PT, u % 4, :], k.xnT[:, c, p * PT:(p + 1) * PT],
                                        wz[:, c, q * 512:(q + 1) * 512], start=(c == 0), stop=(c == CC - 1))
            last.then_inc(s.z, 1)

    @block.scalar
    def _(act):
        for u in range(UNITS):
            act.wait_ge(s.z, upto(u))
            if u >= 2:
                act.wait_ge(s.gate, upto(u - 2))
            nc.scalar.activation(sil[:, u % 2, :], ps[0:PT, u % 4, :], ACT.Silu).then_inc(s.silu, 1)

    @block.sync
    def _(sp):
        for half in range(2):
            for b in range(2):
                r0 = half * SEQ + b * BLK
                sp.dma_start(k.scratch_a[half, b].rearrange("m r c -> r m c"),
                             k.apt[r0:r0 + BLK, 0, :, r0:r0 + BLK]).then_inc(s.a_out, 16)
        sp.dma_start(wz[:], t["gdn_wz"][grp]).then_inc(s.wz_in, 16)
        sp.dma_start(k.wo[:], t["gdn_wo"][grp]).then_inc(s.wo_in, 16)
        sp.wait_ge(s.a_out, 64 * (grp + 1))
        for half in range(2):
            sp.dma_start(flat(asys[half * SYS:(half + 1) * SYS]),
                         k.scratch_a[half].rearrange("b m r c -> m b (r c)")).then_inc(s.a_in, 16)
        sp.wait_ge(s.solved, (BLK - 1) * (grp + 1))
        for half in range(2):
            sp.dma_start(k.scratch_t[half].rearrange("b m r c -> m b (r c)"),
                         flat(tsys[half * SYS:(half + 1) * SYS])).then_inc(s.t_out, 16)
        sp.wait_ge(s.t_out, 32 * (grp + 1))
        sp.wait_ge(s.zeroed, grp + 1)
        for half in range(2):
            for b in range(2):
                r0 = half * SEQ + b * BLK
                sp.dma_start(k.tt[r0:r0 + BLK, :, r0:r0 + BLK],
                             k.scratch_t[half, b].rearrange("m r c -> r m c")).then_inc(s.t_in, 16)

    @block.gpsimd
    def _(pool):
        nc.gpsimd.memset(tsys[:], 0.0).then_inc(s.t_zero, 1)
        pool.wait_ge(s.t_zero, 2 * grp + 1)
        ones = k.ones[0:2 * SYS, 0:2 * BLK].rearrange("m (b r) -> m b r", b=2)
        nc.gpsimd.tensor_tensor(flat(tsys[:])[:, :, 0:BLK * BLK:BLK + 1], ones, ones, ALU.mult).then_inc(s.t_zero, 1)
        nc.gpsimd.memset(k.gmtt[:], 0.0).then_inc(s.zeroed, 1)
        for u in range(UNITS):
            pool.wait_ge(s.silu, upto(u))
            nc.gpsimd.tensor_tensor(k.gate[:, u, :].rearrange("q (v n) -> q v n", v=4),
                                    sil[:, u % 2, :].rearrange("q (v n) -> q v n", v=4),
                                    k.normw[:].unsqueeze(1).broadcast_to([PT, 4, 128]), ALU.mult)\
                .then_inc(s.gate, 1)
        pool.wait_ge(s.t_in, 64 * (grp + 1))

    @block.vector
    def _(dve):
        dve.wait_ge(s.a_in, 32 * (grp + 1))
        dve.wait_ge(s.t_zero, 2 * grp + 2)
        for c in range(1, BLK):
            if c > 1:
                dve.wait_ge(s.solved, (BLK - 1) * grp + c - 1)
            nc.vector.tensor_tensor(prod[:, :, 0:c, 0:c], tsys[:, :, 0:c, 0:c],
                                    asys[:, :, 0:c, c].unsqueeze(2).broadcast_to([2 * SYS, 2, c, c]),
                                    ALU.mult).then_inc(s.prod, 1)
            dve.wait_ge(s.prod, (BLK - 1) * grp + c)
            nc.vector.tensor_reduce(tsys[:, :, 0:c, c], prod[:, :, 0:c, 0:c], AX.X, ALU.add)\
                .then_inc(s.solved, 1)


def gdn_output(nc, k, t, grp, s, ctx):
    rq = sb(nc, ctx, "go_rq", [PT, PAIRS, GV])
    rq2 = sb(nc, ctx, "go_rq2", [PT, PAIRS, GV])
    y = sb(nc, ctx, "go_y", [PT, 3, 512])
    d = sb(nc, ctx, "go_d", [PT, 2, 512])
    r = sb(nc, ctx, "go_r", [PT, 512])
    w = sb(nc, ctx, "go_w", [PT, 512])
    osq = sb(nc, ctx, "go_osq", [PT, 512])
    ssq = sb(nc, ctx, "go_ssq", [PT, 4])
    mean = sb(nc, ctx, "go_mean", [PT, 4])
    eps = sb(nc, ctx, "go_eps", [PT, 4])
    root = sb(nc, ctx, "go_root", [PT, 4])
    fac = sb(nc, ctx, "go_fac", [PT, 4])
    og = sb(nc, ctx, "go_og", [PT, 512])
    ogn = sb(nc, ctx, "go_ogn", [PT, 512])
    ogT = sb(nc, ctx, "go_ogT", [128, 4 * PT])
    ps = pb(nc, ctx, "go_ps", 8)
    Y, R, W, O, T, OUT = range(6)
    block = ctx.enter_context(nc.Block())

    def unit(u):
        return u // 2, u % 2, (u // 2) * GV + (u % 2) * 4

    def upto(u):
        return grp * UNITS + u + 1

    def quad(x):
        return x.rearrange("q (v n) -> q v n", v=4)

    @block.tensor
    def _(pe):
        pe.wait_ge(s.wo_in, 16 * grp + 16)
        for i in range(UNITS + 6):
            u = i
            if u < UNITS:
                p, q, m = unit(u)
                pe.wait_ge(s.y_ready, upto(u - 1))
                pe.wait_ge(s.d_ready, upto(u - 1))
                for v in range(4):
                    last = nc.tensor.matmul(ps[0:PT, Y, v * 128:(v + 1) * 128], k.tt[:, m + v, :],
                                            k.v[:, q * 4 + v, p, :], start=True, stop=True)
                last.then_inc(s.y, 1)
            u = i - 1
            if 0 <= u < UNITS:
                p, q, m = unit(u)
                pe.wait_ge(s.y_ready, upto(u))
                pe.wait_ge(s.r_ready, upto(u - 1))
                for v in range(4):
                    last = nc.tensor.matmul(ps[0:PT, R, v * 128:(v + 1) * 128], k.apt[:, 0, m + v, :],
                                            y[:, u % 3, v * 128:(v + 1) * 128], start=True, stop=True)
                last.then_inc(s.r, 1)
            u = i - 2
            if 0 <= u < UNITS:
                p, q, m = unit(u)
                pe.wait_ge(s.r_ready, upto(u))
                pe.wait_ge(s.w_ready, upto(u - 1))
                for v in range(4):
                    last = nc.tensor.matmul(ps[0:PT, W, v * 128:(v + 1) * 128], k.tt[:, m + v, :],
                                            r[:, v * 128:(v + 1) * 128], start=True, stop=True)
                last.then_inc(s.w, 1)
            u = i - 3
            if 0 <= u < UNITS:
                p, q, m = unit(u)
                pe.wait_ge(s.w_ready, upto(u))
                pe.wait_ge(s.og, upto(u - 1))
                pe.wait_ge(s.osq, upto(u - 1))
                for v in range(4):
                    last = nc.tensor.matmul(ps[0:PT, O, v * 128:(v + 1) * 128], k.apt[:, 1, m + v, :],
                                            w[:, v * 128:(v + 1) * 128], start=True, stop=True)
                last.then_inc(s.o, 1)
            u = i - 5
            if 0 <= u < UNITS:
                pe.wait_ge(s.ogn, upto(u))
                pe.wait_ge(s.ogT, upto(u - 1))
                for v in range(4):
                    last = nc.tensor.transpose(ps[:, T, v * PT:(v + 1) * PT], ogn[:, v * 128:(v + 1) * 128],
                                               k.ident[0:PT, 0:PT])
                last.then_inc(s.turned, 1)
                p, q, m = unit(u)
                pe.wait_ge(s.ogT, upto(u))
                if q == 0:
                    pe.wait_ge(s.added, grp * PAIRS + p)
                for v in range(4):
                    last = nc.tensor.matmul(ps[0:PT, OUT, 0:HID], ogT[:, v * PT:(v + 1) * PT],
                                            k.wo[:, q * 4 + v, :], start=(q == 0 and v == 0),
                                            stop=(q == 1 and v == 3))
                last.then_inc(s.out, 1)

    @block.scalar
    def _(act):
        for i in range(UNITS + 6):
            u = i
            if u < UNITS:
                act.wait_ge(s.y, upto(u))
                if u >= 3:
                    act.wait_ge(s.w_ready, upto(u - 3))
                nc.scalar.copy(y[:, u % 3, :], ps[0:PT, Y, :]).then_inc(s.y_ready, 1)
            u = i - 3
            if 0 <= u < UNITS:
                act.wait_ge(s.o, upto(u))
                act.wait_ge(s.ssq_o, upto(u - 1))
                nc.scalar.square(osq[:], ps[0:PT, O, :]).then_inc(s.osq, 1)
            u = i - 5
            if 0 <= u < UNITS:
                act.wait_ge(s.turned, upto(u))
                act.wait_ge(s.out, upto(u - 1))
                nc.scalar.copy(ogT[:], ps[:, T, 0:4 * PT]).then_inc(s.ogT, 1)

    @block.vector
    def _(dve):
        nc.vector.tensor_copy(rq[:].rearrange("q p (h e) -> q p h e", e=VPK),
                              k.rnq[:].rearrange("q h p -> q p h").unsqueeze(3)
                              .broadcast_to([PT, PAIRS, GK, VPK])).then_inc(s.rq, 1)
        dve.wait_ge(s.rq, 2 * grp + 1)
        nc.vector.scalar_tensor_tensor(out=rq2[:], in0=rq[:], scalar=1.0 / 128, in1=rq[:],
                                       op0=ALU.mult, op1=ALU.mult).then_inc(s.rq, 1)
        for i in range(UNITS + 6):
            u = i
            if u < UNITS:
                p, q, m = unit(u)
                dve.wait_ge(s.y_ready, upto(u))
                if u >= 2:
                    dve.wait_ge(s.r_ready, upto(u - 2))
                nc.vector.tensor_tensor(quad(d[:, u % 2, :]), k.v[:, q * 4:q * 4 + 4, p, :], quad(ps[0:PT, Y, :]),
                                        ALU.subtract).then_inc(s.d_ready, 1)
            u = i - 1
            if 0 <= u < UNITS:
                dve.wait_ge(s.r, upto(u))
                dve.wait_ge(s.d_ready, upto(u))
                dve.wait_ge(s.w, upto(u - 1))
                nc.vector.tensor_tensor(r[:], ps[0:PT, R, :], d[:, u % 2, :], ALU.add).then_inc(s.r_ready, 1)
            u = i - 2
            if 0 <= u < UNITS:
                dve.wait_ge(s.w, upto(u))
                dve.wait_ge(s.o, upto(u - 1))
                nc.vector.tensor_tensor(w[:], ps[0:PT, W, :], y[:, u % 3, :], ALU.add).then_inc(s.w_ready, 1)
            u = i - 3
            if 0 <= u < UNITS:
                dve.wait_ge(s.osq, upto(u))
                dve.wait_ge(s.mean, upto(u - 1))
                nc.vector.tensor_reduce(ssq[:], quad(osq[:]), AX.X, ALU.add).then_inc(s.ssq_o, 1)
                dve.wait_ge(s.ogn, upto(u - 1))
                nc.vector.tensor_tensor(og[:], ps[0:PT, O, :], k.gate[:, u, :], ALU.mult).then_inc(s.og, 1)
            u = i - 5
            if 0 <= u < UNITS and u % 2:
                p = u // 2
                dve.wait_ge(s.out, upto(u))
                nc.vector.tensor_tensor(k.x[:, p, :], k.x[:, p, :], ps[0:PT, OUT, 0:HID], ALU.add)\
                    .then_inc(s.added, 1)

    @block.gpsimd
    def _(pool):
        pool.wait_ge(s.rq, 2 * grp + 2)
        for i in range(UNITS + 6):
            u = i - 3
            if 0 <= u < UNITS:
                p, q, m = unit(u)
                pool.wait_ge(s.ssq_o, upto(u))
                nc.gpsimd.tensor_tensor(mean[:], ssq[:], rq2[:, p, q * 4:q * 4 + 4], ALU.mult).then_inc(s.mean, 1)
                pool.wait_ge(s.mean, upto(u))
                nc.gpsimd.tensor_tensor(eps[:], mean[:], k.eps6[0:PT, 0:4], ALU.add).then_inc(s.eps, 1)
                pool.wait_ge(s.eps, upto(u))
                nc.gpsimd.tensor_tensor(root[:], eps[:], k.minus_half[0:PT, 0:4], ALU.pow).then_inc(s.root, 1)
                pool.wait_ge(s.root, upto(u))
                nc.gpsimd.tensor_tensor(fac[:], root[:], rq[:, p, q * 4:q * 4 + 4], ALU.mult).then_inc(s.fac, 1)
                pool.wait_ge(s.fac, upto(u))
                pool.wait_ge(s.og, upto(u))
                pool.wait_ge(s.turned, upto(u - 1))
                nc.gpsimd.tensor_tensor(quad(ogn[:]), quad(og[:]), fac[:].unsqueeze(2).broadcast_to([PT, 4, 128]),
                                        ALU.mult).then_inc(s.ogn, 1)


def gated_delta_rule(nc, k, t):
    with ExitStack() as ctx:
        k.beta = sb(nc, ctx, "beta", [PT, PAIRS, NV])
        k.logdecay = sb(nc, ctx, "logdecay", [PT, PAIRS, NV])
        k.after = sb(nc, ctx, "after", [PT, PT])
        k.upto = sb(nc, ctx, "upto", [PT, PT])
        k.kqmask = sb(nc, ctx, "kqmask", [PT, 2 * PT])
        k.normw = sb(nc, ctx, "normw", [PT, 128])
        gdn_gates(nc, k, t)
        k.v = sb(nc, ctx, "values", [PT, GV, PAIRS, 128])
        k.gmtt = sb(nc, ctx, "gmtt", [PT, GK * PAIRS * 2 * PT])
        k.tt = k.gmtt[:].rearrange("q (m w) -> q m w", w=PT)
        k.apt = sb(nc, ctx, "apt", [PT, 2, SYS, PT])
        k.rnk2 = sb(nc, ctx, "rnk2", [PT, GK, PAIRS])
        k.rnq = sb(nc, ctx, "rnq", [PT, GK, PAIRS])
        k.scratch_a = nc.dram_tensor("scratch_a", [2, 2, SYS, BLK, BLK], F32, kind="Internal").ap()
        k.scratch_t = nc.dram_tensor("scratch_t", [2, 2, SYS, BLK, BLK], F32, kind="Internal").ap()
        s = sems(nc, ctx, "gdn", "evac projected squared v_done ssq gm_done kq_done conv_done nsq_ready "
                 "conv_step padded roots rnk2 lead a_out a_in solved t_out t_in t_zero zeroed prod "
                 "wz_in wo_in silu z y_ready d_ready y r r_ready w w_ready o og osq ogn ogT turned out added "
                 "gate ssq_o mean eps root fac rq", pairs="w_in v_turned emm u_ready dec_ready apt")
        with nc.Fori(0, GROUPS) as grp:
            for part in (gdn_project, gdn_systems):
                with ExitStack() as inner:
                    part(nc, k, t, grp, s, inner)
            with ExitStack() as both:
                k.gate = sb(nc, both, "gates", [PT, UNITS, 512])
                k.wo = sb(nc, both, "gdn_wo", [128, GV, HID])
                for part in (gdn_solve, gdn_output):
                    with ExitStack() as inner:
                        part(nc, k, t, grp, s, inner)


def context_projections(nc, k, t):
    with ExitStack() as ctx:
        wq = sb(nc, ctx, "cp_wq", [128, CC, HID])
        wk = sb(nc, ctx, "cp_wk", [128, CC, HID])
        wv = sb(nc, ctx, "cp_wv", [128, CC, HID])
        ps = pb(nc, ctx, "cp_ps", 8)
        s = sems(nc, ctx, "cp", "loaded product even odd")
        block = ctx.enter_context(nc.Block())

        @block.sync
        def _(sp):
            sp.dma_start(wq[:], t["c_wq"]).then_inc(s.loaded, 16)
            sp.dma_start(wk[:], t["c_wk"]).then_inc(s.loaded, 16)
            sp.dma_start(wv[:], t["c_wv"]).then_inc(s.loaded, 16)

        @block.tensor
        def _(pe):
            pe.wait_ge(s.loaded, 48)
            for n in range(16):
                if n >= 8:
                    pe.wait_ge((s.even, s.odd)[n % 2], (n - 8) // 2 + 1)
                if n < 8:
                    w, f, half = (wq, wk)[n // 4], n // 2 % 2, n % 2
                    for c in range(CC):
                        last = nc.tensor.matmul(ps[:, n, 0:HALF], w[:, c, f * 128:(f + 1) * 128],
                                                k.xnT[:, c, half * HALF:(half + 1) * HALF],
                                                start=(c == 0), stop=(c == CC - 1))
                else:
                    for e in range(2):
                        b = 2 * (n - 8) + e
                        for c in range(CC):
                            last = nc.tensor.matmul(ps[0:SEQ, n % 8, e * HID:(e + 1) * HID],
                                                    k.xnT[:, c, b * SEQ:(b + 1) * SEQ], wv[:, c, :],
                                                    start=(c == 0), stop=(c == CC - 1))
                last.then_inc(s.product, 1)

        def evacuate(eng, n, copy, scaled):
            eng.wait_ge(s.product, n + 1)
            done = (s.even, s.odd)[n % 2]
            if n < 8:
                dst = (k.qT, k.knT)[n // 4][:, n // 2 % 2, n % 2 * HALF:(n % 2 + 1) * HALF]
                if n < 4:
                    scaled(dst, ps[:, n, 0:HALF], 1 / 16).then_inc(done, 1)
                else:
                    copy(dst, ps[:, n, 0:HALF]).then_inc(done, 1)
            else:
                copy(k.vnew[:, 2 * (n - 8):2 * (n - 8) + 2, :].rearrange("q b d -> q (b d)"),
                     ps[0:SEQ, n % 8, :]).then_inc(done, 1)

        @block.scalar
        def _(act):
            for n in range(0, 16, 2):
                evacuate(act, n, nc.scalar.copy, nc.scalar.mul)

        @block.vector
        def _(dve):
            for n in range(1, 16, 2):
                evacuate(dve, n, nc.vector.tensor_copy, nc.vector.tensor_scalar_mul)


def context_softmax(nc, k, t):
    SLOTS = 4
    TURNS = BATCH // SLOTS
    KEYS = CTX + SEQ
    SPAN = KEYS // 4
    NT = NKT + 1
    LOW = 7
    with ExitStack() as ctx:
        kv = sb(nc, ctx, "cs_kv", [KT, SLOTS, NKT, HID])
        kvT = sb(nc, ctx, "cs_kvT", [128, 2, CC, CTX])
        qslot = sb(nc, ctx, "cs_qslot", [128, 2, CC, SEQ])
        vslot = sb(nc, ctx, "cs_vslot", [SEQ, 2, HID])
        prob = sb(nc, ctx, "cs_prob", [SEQ, KEYS])
        probn = sb(nc, ctx, "cs_probn", [SEQ, KEYS])
        pT = sb(nc, ctx, "cs_pT", [KT, NT, SEQ])
        negmax = sb(nc, ctx, "cs_negmax", [SEQ, 1])
        total = sb(nc, ctx, "cs_total", [SEQ, 1])
        rtotal = sb(nc, ctx, "cs_rtotal", [SEQ, 1])
        ps_s = pb(nc, ctx, "cs_ps_s", 4)
        ps_t = pb(nc, ctx, "cs_ps_t", 2)
        ps_o = pb(nc, ctx, "cs_ps_o", 1)
        s = sems(nc, ctx, "cs", "scored negmax exped rtotal probn stored q_staged v_staged")
        ctx_in = [sem(nc, ctx, f"cs_ctx_in{j}") for j in range(SLOTS)]
        pv_done = [sem(nc, ctx, f"cs_pv_done{j}") for j in range(SLOTS)]
        turned = [sem(nc, ctx, f"cs_turned{j}") for j in range(2)]
        copied = [sem(nc, ctx, f"cs_copied{j}") for j in range(2)]
        block = ctx.enter_context(nc.Block())
        ROUNDS = NKT // 4

        def uses(b):
            return ROUNDS if isinstance(b, int) and b == 0 else (ROUNDS + 1) * b + ROUNDS - 1

        def steps(body, eng):
            for j in range(SLOTS):
                body(0, j, j == 0, False)
            with eng.Fori(0, TURNS - 2) as it:
                for j in range(SLOTS):
                    body(it + 1, j, False, False)
            for j in range(SLOTS):
                body(TURNS - 1, j, False, j == SLOTS - 1)

        @block.sync
        def _(sp):
            with sp.Fori(0, TURNS) as it:
                for j in range(SLOTS):
                    sp.wait_ge(pv_done[j], it)
                    sp.dma_start(kv[:, j], t["context"][it * SLOTS + j].rearrange("(i q) d -> q i d", q=KT))\
                        .then_inc(ctx_in[j], 16)

        @block.tensor
        def _(pe):
            def turn_context(it, j, use, rounds):
                for r in rounds:
                    if r == 0:
                        pe.wait_ge(ctx_in[j], 16 * it + 16)
                    c, quad = r % 2, r // 2
                    pe.wait_ge(copied[c], use + quad)
                    for e in range(4):
                        last = nc.tensor.transpose(ps_t[:, c, e * KT:(e + 1) * KT],
                                                   kv[:, j, quad * 4 + e, c * 128:(c + 1) * 128],
                                                   k.ident[0:KT, 0:KT])
                    last.then_inc(turned[c], 1)

            def scores(b, j, spans):
                for i in spans:
                    lo, hi = i * SPAN, min((i + 1) * SPAN, CTX)
                    for c in range(CC):
                        nc.tensor.matmul(ps_s[0:SEQ, i, 0:hi - lo], qslot[:, j % 2, c, :],
                                         kvT[:, j % 2, c, lo:hi], start=(c == 0), stop=(c == CC - 1))
                if 3 in spans:
                    for c in range(CC):
                        last = nc.tensor.matmul(ps_s[0:SEQ, 3, SPAN - SEQ:SPAN], qslot[:, j % 2, c, :],
                                                k.knT[:, c, bass.ts(b, SEQ)], start=(c == 0), stop=(c == CC - 1))
                    last.then_inc(s.scored, 1)

            def turn_probs(b, use):
                pe.wait_ge(s.probn, b + 1)
                for bank in range(2):
                    pe.wait_ge(copied[bank], use)
                nc.tensor.nop(nofuse=True)
                for bank, tiles in ((0, range(LOW)), (1, range(LOW, NT))):
                    for i in tiles:
                        n = KT if i < NKT else SEQ
                        last = nc.tensor.transpose(ps_t[0:n, bank, (i - tiles[0]) * SEQ:(i - tiles[0] + 1) * SEQ],
                                                   probn[:, i * KT:i * KT + n], k.ident[0:SEQ, 0:SEQ])
                    last.then_inc(turned[bank], 1)

            def values(b, j, use, d):
                if d == 0:
                    for bank in range(2):
                        pe.wait_ge(copied[bank], use)
                    pe.wait_ge(s.stored, b)
                    pe.wait_ge(s.v_staged, b + 1)
                for i in range(NT):
                    n = KT if i < NKT else SEQ
                    v = kv[:, j, i, d * 128:(d + 1) * 128] if i < NKT else vslot[:, j % 2, d * 128:(d + 1) * 128]
                    last = nc.tensor.matmul(ps_o[:, 0, d * SEQ:(d + 1) * SEQ], v, pT[0:n, i, :],
                                            start=(i == 0), stop=(i == NT - 1))
                if d == CC - 1:
                    last.then_inc(pv_done[j], 1)

            def step(it, j, first, last_one):
                b = it * SLOTS + j
                use = uses(b)
                slot, nit, nslot = (j - 1) % SLOTS, it + (j + 1) // SLOTS, (j + 1) % SLOTS
                for c in range(2):
                    pe.wait_ge(copied[c], use - 1)
                pe.wait_ge(s.q_staged, b + 1)
                pe.wait_ge(s.exped, b)
                scores(b, j, (0, 1))
                if not first:
                    turn_probs(b - 1, use)
                for c in range(2):
                    pe.wait_ge(copied[c], use)
                scores(b, j, (2, 3))
                if not first:
                    use = use + 1
                    values(b - 1, slot, use, 0)
                if not last_one:
                    turn_context(nit, nslot, use, (0, 1))
                if not first:
                    values(b - 1, slot, use, 1)
                if not last_one:
                    turn_context(nit, nslot, use, range(2, 2 * ROUNDS))

            turn_context(0, 0, 0, range(2 * ROUNDS))
            steps(step, pe)
            use = uses(BATCH) - ROUNDS
            turn_probs(BATCH - 1, use)
            for d in range(CC):
                values(BATCH - 1, SLOTS - 1, use + 1, d)

        def copy_context(eng, copy, rounds, slot, use):
            for r in rounds:
                bank, quad = r % 2, r // 2
                eng.wait_ge(turned[bank], use + quad + 1)
                copy(kvT[:, slot, bank, quad * 500:(quad + 1) * 500], ps_t[:, bank, 0:500])\
                    .then_inc(copied[bank], 1)

        @block.scalar
        def _(act):
            def copy_probs(use):
                act.wait_ge(turned[0], use + 1)
                nc.scalar.copy(pT[:, 0:LOW, :], ps_t[0:KT, 0, 0:LOW * SEQ].rearrange("q (i n) -> q i n", n=SEQ))\
                    .then_inc(copied[0], 1)
                act.wait_ge(turned[1], use + 1)
                nc.scalar.copy(pT[:, LOW:NKT, :], ps_t[0:KT, 1, 0:(NKT - LOW) * SEQ]
                               .rearrange("q (i n) -> q i n", n=SEQ))
                nc.scalar.copy(pT[0:SEQ, NKT, :], ps_t[0:SEQ, 1, (NKT - LOW) * SEQ:(NT - LOW) * SEQ])\
                    .then_inc(copied[1], 1)

            def step(it, j, first, last_one):
                b = it * SLOTS + j
                use = uses(b)
                if not first:
                    copy_probs(use)
                    use = use + 1
                act.wait_ge(s.negmax, b + 1)
                nc.scalar.activation(prob[:].rearrange("q (i n) -> q i n", i=4), ps_s[0:SEQ, :, 0:SPAN], ACT.Exp,
                                     bias=negmax[:], accum_out=total[:]).then_inc(s.exped, 1)
                if not last_one:
                    copy_context(act, nc.scalar.copy, (2, 3, 5), (j + 1) % 2, use)

            copy_context(act, nc.scalar.copy, (0, 2, 4), 0, 0)
            steps(step, act)
            copy_probs(uses(BATCH) - ROUNDS)

        @block.vector
        def _(dve):
            def store(b, j, count):
                dve.wait_ge(pv_done[j], count)
                nc.vector.tensor_copy(k.oT[:, :, bass.ts(b, SEQ)],
                                      ps_o[:, 0, 0:CC * SEQ].rearrange("d (c n) -> d c n", c=CC)).then_inc(s.stored, 1)

            def step(it, j, first, last_one):
                b = it * SLOTS + j
                use = uses(b)
                dve.wait_ge(s.scored, b + 1)
                nc.vector.tensor_reduce(negmax[:], ps_s[0:SEQ, :, 0:SPAN], AX.XY, ALU.max, negate=True)\
                    .then_inc(s.negmax, 1)
                after = use if first else use + 1
                if not last_one:
                    copy_context(dve, nc.vector.tensor_copy, (0, 1), (j + 1) % 2, after)
                dve.wait_ge(s.exped, b + 1)
                nc.vector.reciprocal(rtotal[:], total[:]).then_inc(s.rtotal, 1)
                dve.wait_ge(s.rtotal, b + 1)
                if not first:
                    dve.wait_ge(turned[1], use + 1)
                nc.vector.tensor_scalar_mul(probn[:], prob[:], rtotal[:]).then_inc(s.probn, 1)
                if not first:
                    store(b - 1, (j - 1) % SLOTS, it + (1 if j else 0))
                if not last_one:
                    copy_context(dve, nc.vector.tensor_copy, (4,), (j + 1) % 2, after)

            copy_context(dve, nc.vector.tensor_copy, (1, 3, 5), 0, 0)
            steps(step, dve)
            store(BATCH - 1, SLOTS - 1, TURNS)

        @block.gpsimd
        def _(pool):
            def queries(b, j, used):
                if used:
                    pool.wait_ge(s.scored, b - 1)
                nc.gpsimd.tensor_copy(qslot[:, j % 2], k.qT[:, :, bass.ts(b, SEQ)]).then_inc(s.q_staged, 1)

            def values(b, j, count):
                if count is not None:
                    pool.wait_ge(pv_done[(j - 2) % SLOTS], count)
                nc.gpsimd.tensor_copy(vslot[:, j % 2, :], k.vnew[:, b, :]).then_inc(s.v_staged, 1)

            for b in range(SLOTS):
                queries(b, b, b >= 2)
                values(b, b, 1 if b >= 2 else None)
            with pool.Fori(0, TURNS - 1) as it:
                for j in range(SLOTS):
                    b = (it + 1) * SLOTS + j
                    queries(b, j, True)
                    values(b, j, it + (2 if j >= 2 else 1))


def add_projection(nc, k, tag, weight, srcT, chunks, bias=None):
    with ExitStack() as ctx:
        w = sb(nc, ctx, f"{tag}_w", [128, chunks, HID])
        ps = pb(nc, ctx, f"{tag}_ps", 8)
        s = sems(nc, ctx, tag, "loaded product biased added")
        block = ctx.enter_context(nc.Block())

        @block.sync
        def _(sp):
            sp.dma_start(w[:], weight).then_inc(s.loaded, 16)

        @block.tensor
        def _(pe):
            pe.wait_ge(s.loaded, 16)
            for p in range(PAIRS):
                for c in range(chunks):
                    last = nc.tensor.matmul(ps[0:PT, p, 0:HID], srcT[:, c, p * PT:(p + 1) * PT], w[:, c, :],
                                            start=(c == 0), stop=(c == chunks - 1))
                last.then_inc(s.product, 1)

        @block.vector
        def _(dve):
            if bias is not None:
                nc.vector.tensor_tensor(k.x[:], k.x[:], bias.unsqueeze(1).broadcast_to([PT, PAIRS, HID]),
                                        ALU.add).then_inc(s.biased, 1)
                dve.wait_ge(s.biased, 1)
            for p in range(PAIRS):
                dve.wait_ge(s.product, p + 1)
                nc.vector.tensor_tensor(k.x[:, p, :], k.x[:, p, :], ps[0:PT, p, 0:HID], ALU.add)\
                    .then_inc(s.added, 1)


def context_attention(nc, k, t):
    with ExitStack() as ctx:
        k.qT = sb(nc, ctx, "ca_qT", [128, CC, TOK])
        k.knT = sb(nc, ctx, "ca_knT", [128, CC, TOK])
        k.vnew = sb(nc, ctx, "ca_vnew", [SEQ, BATCH, HID])
        k.oT = sb(nc, ctx, "ca_oT", [128, CC, TOK])
        context_projections(nc, k, t)
        context_softmax(nc, k, t)
        add_projection(nc, k, "ca_out", t["c_wo"], k.oT, CC)


def route(nc, k, tag, weight, bias, experts=8):
    N = PAIRS * experts
    with ExitStack() as ctx:
        w = sb(nc, ctx, f"{tag}_w", [128, CC, experts])
        earlier = sb(nc, ctx, f"{tag}_earlier", [PT, experts * experts])
        brow = sb(nc, ctx, f"{tag}_brow", [PT, experts]) if bias is not None else None
        logit = sb(nc, ctx, f"{tag}_logit", [PT, PAIRS, experts])
        top = sb(nc, ctx, f"{tag}_top", [PT, PAIRS])
        shifted = sb(nc, ctx, f"{tag}_shifted", [PT, PAIRS, experts])
        ex = sb(nc, ctx, f"{tag}_ex", [PT, PAIRS, experts])
        total = sb(nc, ctx, f"{tag}_total", [PT, PAIRS])
        rtotal = sb(nc, ctx, f"{tag}_rtotal", [PT, PAIRS])
        more = sb(nc, ctx, f"{tag}_more", [PT, N, experts])
        same = sb(nc, ctx, f"{tag}_same", [PT, N, experts])
        tie = sb(nc, ctx, f"{tag}_tie", [PT, N, experts])
        before = sb(nc, ctx, f"{tag}_before", [PT, N, experts])
        ps = pb(nc, ctx, f"{tag}_ps", 1)
        s = sems(nc, ctx, tag, "loaded product ex chain")
        block = ctx.enter_context(nc.Block())
        over_j = lambda x: x[:].unsqueeze(3).broadcast_to([PT, PAIRS, experts, experts])
        over_e = lambda x: x[:].unsqueeze(2).broadcast_to([PT, PAIRS, experts, experts])
        cube = lambda x: x[:].rearrange("q (p e) j -> q p e j", p=PAIRS)

        @block.sync
        def _(sp):
            sp.dma_start(w[:], weight).then_inc(s.loaded, 16)
            sp.dma_start(earlier[:], k.t["earlier"]).then_inc(s.loaded, 16)
            if bias is not None:
                sp.dma_start(brow[:], bias).then_inc(s.loaded, 16)

        @block.tensor
        def _(pe):
            pe.wait_ge(s.loaded, 32 if bias is None else 48)
            for p in range(PAIRS):
                for c in range(CC):
                    last = nc.tensor.matmul(ps[0:PT, 0, p * experts:(p + 1) * experts],
                                            k.xnT[:, c, p * PT:(p + 1) * PT], w[:, c, :],
                                            start=(c == 0), stop=(c == CC - 1))
            last.then_inc(s.product, 1)

        @block.scalar
        def _(act):
            act.wait_ge(s.chain, 3)
            nc.scalar.activation(ex[:], shifted[:], ACT.Exp).then_inc(s.ex, 1)

        @block.vector
        def _(dve):
            count = [0]

            def wait_all():
                dve.wait_ge(s.chain, count[0])

            def step(ins):
                ins.then_inc(s.chain, 1)
                count[0] += 1

            dve.wait_ge(s.product, 1)
            raw = ps[0:PT, 0, 0:N].rearrange("q (p e) -> q p e", p=PAIRS)
            if bias is None:
                step(nc.vector.tensor_copy(logit[:], raw))
            else:
                step(nc.vector.tensor_tensor(logit[:], raw, brow[:].unsqueeze(1)
                                             .broadcast_to([PT, PAIRS, experts]), ALU.add))
            wait_all()
            step(nc.vector.tensor_reduce(top[:], logit[:], AX.X, ALU.max))
            wait_all()
            step(nc.vector.tensor_tensor(shifted[:], logit[:], top[:].unsqueeze(2)
                                         .broadcast_to([PT, PAIRS, experts]), ALU.subtract))
            dve.wait_ge(s.ex, 1)
            step(nc.vector.tensor_reduce(total[:], ex[:], AX.X, ALU.add))
            wait_all()
            step(nc.vector.reciprocal(rtotal[:], total[:]))
            wait_all()
            step(nc.vector.tensor_tensor(k.prob[:], ex[:], rtotal[:].unsqueeze(2)
                                         .broadcast_to([PT, PAIRS, experts]), ALU.mult))
            wait_all()
            step(nc.vector.tensor_tensor(cube(more), over_e(k.prob), over_j(k.prob), ALU.is_gt))
            step(nc.vector.tensor_tensor(cube(same), over_e(k.prob), over_j(k.prob), ALU.is_equal))
            wait_all()
            step(nc.vector.tensor_tensor(cube(tie), cube(same), earlier[:]
                                         .rearrange("q (e j) -> q e j", e=experts).unsqueeze(1)
                                         .broadcast_to([PT, PAIRS, experts, experts]), ALU.mult))
            wait_all()
            step(nc.vector.tensor_tensor(before[:], more[:], tie[:], ALU.add))
            wait_all()
            step(nc.vector.tensor_reduce(k.rank[:].rearrange("q p e -> q (p e)"), before[:], AX.X, ALU.add))


def expert_weights(nc, k):
    with ExitStack() as ctx:
        picked = sb(nc, ctx, "ew_picked", [PT, PAIRS, E0])
        total = sb(nc, ctx, "ew_total", [PT, PAIRS])
        rtotal = sb(nc, ctx, "ew_rtotal", [PT, PAIRS])
        s = sems(nc, ctx, "ew", "picked total rtotal done")
        block = ctx.enter_context(nc.Block())

        @block.vector
        def _(dve):
            nc.vector.scalar_tensor_tensor(out=picked[:], in0=k.rank[:], scalar=1.5, in1=k.prob[:],
                                           op0=ALU.is_lt, op1=ALU.mult).then_inc(s.picked, 1)
            dve.wait_ge(s.picked, 1)
            nc.vector.tensor_reduce(total[:], picked[:], AX.X, ALU.add).then_inc(s.total, 1)
            dve.wait_ge(s.total, 1)
            nc.vector.reciprocal(rtotal[:], total[:]).then_inc(s.rtotal, 1)
            dve.wait_ge(s.rtotal, 1)
            nc.vector.tensor_tensor(k.wfull[:], picked[:], rtotal[:].unsqueeze(2)
                                    .broadcast_to([PT, PAIRS, E0]), ALU.mult).then_inc(s.done, 1)


def swiglu_experts(nc, k, t):
    FT = F0 // 128
    W13 = CC * F0
    with ExitStack() as ctx:
        w = sb(nc, ctx, "sw_w", [128, 2, 2 * W13 + FT * HID])
        gate = sb(nc, ctx, "sw_gate", [128, 2, HALF])
        hid = sb(nc, ctx, "sw_hid", [128, 2, FT, TOK])
        up = pb(nc, ctx, "sw_up", 4)
        down = pb(nc, ctx, "sw_down", 4)
        s = sems(nc, ctx, "sw", "upped gated hidden downed added")
        w_in = [sem(nc, ctx, f"sw_w_in{j}") for j in range(2)]
        used = [sem(nc, ctx, f"sw_used{j}") for j in range(2)]
        block = ctx.enter_context(nc.Block())
        w13 = [[w[:, j, m * W13:(m + 1) * W13].rearrange("c (k n) -> c k n", k=CC) for m in range(2)]
               for j in range(2)]
        w2 = [w[:, j, 2 * W13:].rearrange("c (k n) -> c k n", k=FT) for j in range(2)]
        Q = 2 * FT

        @block.sync
        def _(sp):
            with sp.Fori(0, E0 // 2) as i:
                for j in range(2):
                    sp.wait_ge(used[j], PAIRS * i)
                    sp.dma_start(w[:, j, :], t["s_w"][i * 2 + j]).then_inc(w_in[j], 16)

        @block.tensor
        def _(pe):
            with pe.Fori(0, E0 // 2) as i:
                for j in range(2):
                    e = i * 2 + j
                    pe.wait_ge(w_in[j], 16 * i + 16)
                    for q in range(Q):
                        f, half = q // 2, q % 2
                        pe.wait_ge(s.hidden, Q * e + max(q - 1, 0))
                        for m in range(2):
                            for c in range(CC):
                                last = nc.tensor.matmul(up[:, (q % 2) * 2 + m, 0:HALF],
                                                        w13[j][m][:, c, f * 128:(f + 1) * 128],
                                                        k.xnT[:, c, half * HALF:(half + 1) * HALF],
                                                        start=(c == 0), stop=(c == CC - 1))
                        last.then_inc(s.upped, 1)
                    pe.wait_ge(s.hidden, Q * e + Q)
                    for p in range(PAIRS):
                        pe.wait_ge(s.added, PAIRS * e + max(p - 3, 0))
                        for f in range(FT):
                            last = nc.tensor.matmul(down[0:PT, p % 4, 0:HID], hid[:, j, f, p * PT:(p + 1) * PT],
                                                    w2[j][:, f, :], start=(f == 0), stop=(f == FT - 1))
                        last.then_inc(used[j], 1)

        @block.scalar
        def _(act):
            with act.Fori(0, E0 // 2) as i:
                for j in range(2):
                    e = i * 2 + j
                    for q in range(Q):
                        act.wait_ge(s.upped, Q * e + q + 1)
                        act.wait_ge(s.hidden, Q * e + max(q - 1, 0))
                        nc.scalar.activation(gate[:, q % 2, :], up[:, (q % 2) * 2, 0:HALF], ACT.Silu)\
                            .then_inc(s.gated, 1)

        @block.vector
        def _(dve):
            with dve.Fori(0, E0 // 2) as i:
                for j in range(2):
                    e = i * 2 + j
                    dve.wait_ge(used[j], PAIRS * i)
                    for q in range(Q):
                        dve.wait_ge(s.gated, Q * e + q + 1)
                        nc.vector.tensor_tensor(hid[:, j, q // 2, (q % 2) * HALF:(q % 2 + 1) * HALF],
                                                gate[:, q % 2, :], up[:, (q % 2) * 2 + 1, 0:HALF], ALU.mult)\
                            .then_inc(s.hidden, 1)
                    for p in range(PAIRS):
                        dve.wait_ge(used[j], PAIRS * i + p + 1)
                        nc.vector.scalar_tensor_tensor(out=k.x[:, p, :], in0=down[0:PT, p % 4, 0:HID],
                                                       scalar=k.wfull[:, p, bass.ds(e, 1)], in1=k.x[:, p, :],
                                                       op0=ALU.mult, op1=ALU.add).then_inc(s.added, 1)


def routed_swiglu(nc, k, t):
    with ExitStack() as ctx:
        k.t = t
        k.prob = sb(nc, ctx, "rs_prob", [PT, PAIRS, E0])
        k.rank = sb(nc, ctx, "rs_rank", [PT, PAIRS, E0])
        k.wfull = sb(nc, ctx, "rs_wfull", [PT, PAIRS, E0])
        route(nc, k, "r0", t["r0_w"], None)
        expert_weights(nc, k)
        swiglu_experts(nc, k, t)


def feature_products(nc, k, t):
    NH = PAIRS * QKH
    MAGIC = 1.5 * 2.0 ** 23
    PI = float(np.float32(np.pi))
    TWO_PI_HI = 6.28125
    TWO_PI_LO = 2 * np.pi - TWO_PI_HI
    with ExitStack() as ctx:
        w = sb(nc, ctx, "fp_w", [128, CC, 512])
        brow = sb(nc, ctx, "fp_brow", [PT, 512])
        cos = sb(nc, ctx, "fp_cos", [PT, AD])
        sin = sb(nc, ctx, "fp_sin", [PT, AD])
        rdiag = sb(nc, ctx, "fp_rdiag", [128, 64])
        qk = sb(nc, ctx, "fp_qk", [PT, NH, AD])
        turned_by = sb(nc, ctx, "fp_turned", [PT, NH, AD])
        crossed = sb(nc, ctx, "fp_crossed", [PT, NH, AD])
        rot = sb(nc, ctx, "fp_rot", [PT, NH, AD])
        sq = sb(nc, ctx, "fp_sq", [PT, NH, AD])
        ssq = sb(nc, ctx, "fp_ssq", [PT, NH])
        ssqm = sb(nc, ctx, "fp_ssqm", [PT, NH])
        rnorm = sb(nc, ctx, "fp_rnorm", [PT, NH])
        expo = sb(nc, ctx, "fp_expo", [PT, NH])
        rotn = sb(nc, ctx, "fp_rotn", [PT, NH, AD])
        rotT = sb(nc, ctx, "fp_rotT", [128, 2, 3 * PT])
        arg = sb(nc, ctx, "fp_arg", [PT, NH, AD])
        near = sb(nc, ctx, "fp_near", [PT, NH, AD])
        ps = pb(nc, ctx, "fp_ps", 8)
        s = sems(nc, ctx, "fp", "loaded product biased chain ssqm expo rnorm turned copied feat argued ready sined")
        block = ctx.enter_context(nc.Block())
        by_pair = lambda x, p: x[:, p * QKH:(p + 1) * QKH, :].rearrange("q h d -> q (h d)")

        @block.sync
        def _(sp):
            for dst, name in ((w, "f_w"), (brow, "f_b"), (cos, "f_cos"), (sin, "f_sin"), (rdiag, "f_r")):
                sp.dma_start(dst[:], t[name]).then_inc(s.loaded, 16)

        @block.tensor
        def _(pe):
            pe.wait_ge(s.loaded, 80)
            for p in range(PAIRS):
                for c in range(CC):
                    last = nc.tensor.matmul(ps[0:PT, p, :], k.xnT[:, c, p * PT:(p + 1) * PT], w[:, c, :],
                                            start=(c == 0), stop=(c == CC - 1))
                last.then_inc(s.product, 1)
            pe.wait_ge(s.biased, 2 * PAIRS)
            pe.wait_ge(s.ready, 1)
            for p in range(PAIRS):
                if p >= 2:
                    pe.wait_ge(s.copied, p - 1)
                for i in range(3):
                    last = nc.tensor.transpose(ps[:, p % 2, i * PT:(i + 1) * PT],
                                               by_pair(rotn, p)[:, i * 128:(i + 1) * 128], k.ident[0:PT, 0:PT])
                last.then_inc(s.turned, 1)
                pe.wait_ge(s.copied, p + 1)
                if p >= 4:
                    pe.wait_ge(s.argued, 2 * (p - 3))
                for i in range(3):
                    last = nc.tensor.matmul(ps[0:PT, 4 + p % 4, i * 64:(i + 1) * 64],
                                            rotT[:, p % 2, i * PT:(i + 1) * PT], rdiag[:], start=True, stop=True)
                last.then_inc(s.feat, 1)

        @block.gpsimd
        def _(pool):
            nc.gpsimd.memset(expo[:], -0.5).then_inc(s.expo, 1)
            pool.wait_ge(s.expo, 1)
            pool.wait_ge(s.ssqm, 1)
            nc.gpsimd.tensor_tensor(rnorm[:], ssqm[:], expo[:], ALU.pow).then_inc(s.rnorm, 1)

        @block.scalar
        def _(act):
            for p in range(PAIRS):
                act.wait_ge(s.turned, p + 1)
                if p >= 2:
                    act.wait_ge(s.feat, p - 1)
                nc.scalar.copy(rotT[:, p % 2, :], ps[:, p % 2, 0:3 * PT]).then_inc(s.copied, 1)
            act.wait_ge(s.ready, 2)
            nc.scalar.activation(k.feat[:], near[:], ACT.Sin).then_inc(s.sined, 1)

        @block.vector
        def _(dve):
            count = [0]

            def step(ins):
                ins.then_inc(s.chain, 1)
                count[0] += 1
                dve.wait_ge(s.chain, count[0])

            heads = lambda x: x[:].unsqueeze(1).broadcast_to([PT, NH, AD])
            for p in range(PAIRS):
                dve.wait_ge(s.product, p + 1)
                nc.vector.tensor_tensor(by_pair(qk, p), ps[0:PT, p, 0:QKH * AD], brow[:, 0:QKH * AD], ALU.add)\
                    .then_inc(s.biased, 1)
                nc.vector.tensor_tensor(k.vals[:, p, :], ps[0:PT, p, QKH * AD:], brow[:, QKH * AD:], ALU.add)\
                    .then_inc(s.biased, 1)
            dve.wait_ge(s.biased, 2 * PAIRS)
            step(nc.vector.tensor_tensor(turned_by[:], qk[:], heads(cos), ALU.mult))
            step(nc.vector.tensor_tensor(crossed[:, :, 0:AF], qk[:, :, AF:], sin[:, 0:AF].unsqueeze(1)
                                         .broadcast_to([PT, NH, AF]), ALU.mult))
            step(nc.vector.tensor_tensor(crossed[:, :, AF:], qk[:, :, 0:AF], sin[:, AF:].unsqueeze(1)
                                         .broadcast_to([PT, NH, AF]), ALU.mult))
            step(nc.vector.tensor_tensor(rot[:], turned_by[:], crossed[:], ALU.add))
            step(nc.vector.tensor_tensor(sq[:], rot[:], rot[:], ALU.mult))
            step(nc.vector.tensor_reduce(ssq[:], sq[:], AX.X, ALU.add))
            nc.vector.tensor_scalar_max(ssqm[:], ssq[:], 1e-12).then_inc(s.ssqm, 1)
            dve.wait_ge(s.rnorm, 1)
            nc.vector.tensor_tensor(rotn[:], rot[:], rnorm[:].unsqueeze(2).broadcast_to([PT, NH, AD]), ALU.mult)\
                .then_inc(s.ready, 1)
            for p in range(PAIRS):
                dve.wait_ge(s.feat, p + 1)
                prod = ps[0:PT, 4 + p % 4, 0:QKH * AF].rearrange("q (h f) -> q h f", f=AF)
                at = arg[:, p * QKH:(p + 1) * QKH, :]
                nc.vector.tensor_copy(at[:, :, 0:AF], prod).then_inc(s.argued, 1)
                nc.vector.tensor_scalar_add(at[:, :, AF:], prod, float(np.pi / 2)).then_inc(s.argued, 1)
            dve.wait_ge(s.argued, 2 * PAIRS)
            step(nc.vector.tensor_scalar(near[:], arg[:], float(1 / (2 * np.pi)), MAGIC, ALU.mult, ALU.add))
            step(nc.vector.tensor_scalar(sq[:], near[:], -MAGIC, None, ALU.add))
            step(nc.vector.scalar_tensor_tensor(out=rot[:], in0=sq[:], scalar=-TWO_PI_HI, in1=arg[:],
                                                op0=ALU.mult, op1=ALU.add))
            step(nc.vector.scalar_tensor_tensor(out=crossed[:], in0=sq[:], scalar=-TWO_PI_LO, in1=rot[:],
                                                op0=ALU.mult, op1=ALU.add))
            nc.vector.tensor_scalar(near[:], crossed[:], PI, -PI, ALU.min, ALU.max).then_inc(s.ready, 1)


def feature_mix(nc, k, t):
    QN, KN = AH * AD, AHKV * AD
    with ExitStack() as ctx:
        prod = sb(nc, ctx, "fm_prod", [PT, 2, AH, AHKV, AD])
        score = sb(nc, ctx, "fm_score", [PT, 2, AH, AHKV])
        prod2 = sb(nc, ctx, "fm_prod2", [PT, AH, AD, AHKV])
        mixed = sb(nc, ctx, "fm_mixed", [PT, PAIRS, AH, AD])
        again = sb(nc, ctx, "fm_again", [PT, PAIRS, HID])
        ps = pb(nc, ctx, "fm_ps", 4)
        s = sems(nc, ctx, "fm", "prod scored prod2 mixed out back turned copied")
        block = ctx.enter_context(nc.Block())

        @block.gpsimd
        def _(pool):
            for p in range(PAIRS):
                if p >= 2:
                    pool.wait_ge(s.scored, p - 1)
                feat = k.feat[:, p * QKH:(p + 1) * QKH, :]
                nc.gpsimd.tensor_tensor(prod[:, p % 2], feat[:, 0:AH, :].unsqueeze(2)
                                        .broadcast_to([PT, AH, AHKV, AD]),
                                        feat[:, AH:, :].unsqueeze(1).broadcast_to([PT, AH, AHKV, AD]),
                                        ALU.mult).then_inc(s.prod, 1)

        @block.vector
        def _(dve):
            for p in range(PAIRS):
                dve.wait_ge(s.prod, p + 1)
                nc.vector.tensor_reduce(score[:, p % 2], prod[:, p % 2], AX.X, ALU.add).then_inc(s.scored, 1)
                dve.wait_ge(s.scored, p + 1)
                dve.wait_ge(s.mixed, p)
                nc.vector.tensor_tensor(prod2[:], score[:, p % 2].unsqueeze(2).broadcast_to([PT, AH, AD, AHKV]),
                                        k.vals[:, p, :].rearrange("q (h d) -> q d h", d=AD).unsqueeze(1)
                                        .broadcast_to([PT, AH, AD, AHKV]), ALU.mult).then_inc(s.prod2, 1)
                dve.wait_ge(s.prod2, p + 1)
                nc.vector.tensor_reduce(mixed[:, p], prod2[:], AX.X, ALU.add).then_inc(s.mixed, 1)

        @block.sync
        def _(sp):
            for p in range(PAIRS):
                sp.wait_ge(s.mixed, p + 1)
                for e in range(2):
                    sp.dma_start(k.scratch_f[2 * p + e].rearrange("h t d -> t h d"),
                                 mixed[e * SEQ:(e + 1) * SEQ, p]).then_inc(s.out, 16)
            sp.wait_ge(s.out, 16 * BATCH)
            flat = k.scratch_f.rearrange("b h t d -> (b h t d)").rearrange("(p q n) -> q p n", q=PT, n=HID)
            sp.dma_start(again[:], flat).then_inc(s.back, 16)

        @block.tensor
        def _(pe):
            pe.wait_ge(s.back, 16)
            for b in range(4):
                for e in range(HPAIRS):
                    last = nc.tensor.transpose(ps[:, b, e * PT:(e + 1) * PT],
                                               again[:, (b // CC) * HPAIRS + e, (b % CC) * 128:(b % CC + 1) * 128],
                                               k.ident[0:PT, 0:PT])
                last.then_inc(s.turned, 1)

        @block.scalar
        def _(act):
            for b in range(4):
                act.wait_ge(s.turned, b + 1)
                nc.scalar.mul(k.oT[:, b % CC, (b // CC) * HALF:(b // CC + 1) * HALF], ps[:, b, 0:HALF],
                              2.0 / AD).then_inc(s.copied, 1)


def feature_attention(nc, k, t):
    with ExitStack() as ctx:
        k.vals = sb(nc, ctx, "fa_vals", [PT, PAIRS, AHKV * AD])
        k.feat = sb(nc, ctx, "fa_feat", [PT, PAIRS * QKH, AD])
        k.oT = sb(nc, ctx, "fa_oT", [128, CC, TOK])
        bo = sb(nc, ctx, "fa_bo", [PT, HID])
        k.scratch_f = nc.dram_tensor("scratch_f", [BATCH, AH, SEQ, AD], F32, kind="Internal").ap()
        feature_products(nc, k, t)
        feature_mix(nc, k, t)
        load_bias(nc, "fb", bo, t["f_bo"])
        add_projection(nc, k, "fa_out", t["f_wo"], k.oT, CC, bias=bo[:])


def load_bias(nc, tag, dst, src):
    with ExitStack() as ctx:
        s = sems(nc, ctx, tag, "loaded")
        block = ctx.enter_context(nc.Block())

        @block.sync
        def _(sp):
            sp.dma_start(dst[:], src).then_inc(s.loaded, 16)
            sp.wait_ge(s.loaded, 16)


def grouped_queries(nc, k, t):
    QUADS = PAIRS * XKV
    with ExitStack() as ctx:
        w = sb(nc, ctx, "gq_w", [128, CC, XH * XD])
        nw = sb(nc, ctx, "gq_nw", [128, 2])
        nws = sb(nc, ctx, "gq_nws", [128, 1])
        sq = sb(nc, ctx, "gq_sq", [PT, 512])
        ssq = sb(nc, ctx, "gq_ssq", [PT, 2, 4])
        mean = sb(nc, ctx, "gq_mean", [PT, 2, 4])
        rms = sb(nc, ctx, "gq_rms", [PT, 2, 4])
        qn = sb(nc, ctx, "gq_qn", [PT, 2, 512])
        qT = sb(nc, ctx, "gq_qT", [128, 2, 2, XH, SEQ])
        ps = pb(nc, ctx, "gq_ps", 4)
        pt = pb(nc, ctx, "gq_pt", 2)
        s = sems(nc, ctx, "gq", "loaded product squared ssq mean rms normed turned weight copied")
        out = [sem(nc, ctx, f"gq_out{j}") for j in range(2)]
        block = ctx.enter_context(nc.Block())
        quad = lambda x: x.rearrange("q (v n) -> q v n", v=4)

        @block.sync
        def _(sp):
            sp.dma_start(w[:], t["x_wq"]).then_inc(s.loaded, 16)
            sp.dma_start(nw[:], t["x_nw"]).then_inc(s.loaded, 16)
            for p in range(PAIRS):
                sp.wait_ge(s.copied, XKV * (p + 1))
                sp.dma_start(k.scratch_q[p], qT[:, p % 2]).then_inc(out[p % 2], 16)
            for j in range(2):
                sp.wait_ge(out[j], 16 * (PAIRS // 2))

        @block.tensor
        def _(pe):
            pe.wait_ge(s.loaded, 32)
            for u in range(QUADS + 2):
                if u < QUADS:
                    p, g = u // XKV, u % XKV
                    if u >= 4:
                        pe.wait_ge(s.normed, u - 3)
                    for c in range(CC):
                        last = nc.tensor.matmul(ps[0:PT, u % 4, :], k.xnT[:, c, p * PT:(p + 1) * PT],
                                                w[:, c, g * 512:(g + 1) * 512], start=(c == 0), stop=(c == CC - 1))
                    last.then_inc(s.product, 1)
                v = u - 2
                if v >= 0:
                    pe.wait_ge(s.normed, v + 1)
                    if v >= 2:
                        pe.wait_ge(s.copied, v - 1)
                    for h in range(4):
                        last = nc.tensor.transpose(pt[:, v % 2, h * PT:(h + 1) * PT],
                                                   qn[:, v % 2, h * 128:(h + 1) * 128], k.ident[0:PT, 0:PT])
                    last.then_inc(s.turned, 1)

        @block.scalar
        def _(act):
            act.wait_ge(s.weight, 1)
            for u in range(QUADS + 2):
                if u < QUADS:
                    act.wait_ge(s.product, u + 1)
                    if u >= 1:
                        act.wait_ge(s.ssq, u)
                    nc.scalar.square(sq[:], ps[0:PT, u % 4, :]).then_inc(s.squared, 1)
                v = u - 2
                if v >= 0:
                    p, g = v // XKV, v % XKV
                    act.wait_ge(s.turned, v + 1)
                    if p >= 2:
                        act.wait_ge(out[p % 2], 16 * (p // 2))
                    nc.scalar.mul(qT[:, p % 2, :, g * 4:(g + 1) * 4, :].rearrange("d j h n -> d h j n"),
                                  pt[:, v % 2, 0:4 * PT].rearrange("d (h j n) -> d h j n", h=4, j=2), nws[:]).then_inc(s.copied, 1)

        @block.gpsimd
        def _(pool):
            for u in range(QUADS):
                pool.wait_ge(s.mean, u + 1)
                if u >= 2:
                    pool.wait_ge(s.normed, u - 1)
                nc.gpsimd.tensor_tensor(rms[:, u % 2, :], mean[:, u % 2, :], k.minus_half[0:PT, 0:4], ALU.pow)\
                    .then_inc(s.rms, 1)

        @block.vector
        def _(dve):
            dve.wait_ge(s.loaded, 32)
            nc.vector.scalar_tensor_tensor(out=nws[:], in0=nw[:, 0:1], scalar=float(XD) ** -0.5, in1=nw[:, 1:2],
                                           op0=ALU.mult, op1=ALU.mult).then_inc(s.weight, 1)
            for u in range(QUADS):
                dve.wait_ge(s.squared, u + 1)
                if u >= 2:
                    dve.wait_ge(s.mean, u - 1)
                nc.vector.tensor_reduce(ssq[:, u % 2, :], quad(sq[:]), AX.X, ALU.add).then_inc(s.ssq, 1)
                dve.wait_ge(s.ssq, u + 1)
                if u >= 2:
                    dve.wait_ge(s.rms, u - 1)
                nc.vector.tensor_scalar(mean[:, u % 2, :], ssq[:, u % 2, :], 1.0 / XD, 1e-6, ALU.mult, ALU.add)\
                    .then_inc(s.mean, 1)
                dve.wait_ge(s.rms, u + 1)
                if u >= 2:
                    dve.wait_ge(s.turned, u - 1)
                nc.vector.tensor_tensor(quad(qn[:, u % 2, :]), quad(ps[0:PT, u % 4, :]),
                                        rms[:, u % 2, :].unsqueeze(2).broadcast_to([PT, 4, 128]), ALU.mult)\
                    .then_inc(s.normed, 1)


def grouped_softmax(nc, k, t):
    HP = XH // 2
    TILES = [2, 1] * (HP // 2)
    FIRST = [sum(TILES[:h]) for h in range(HP + 1)]
    QT = 4
    PIECES = NKT // QT
    ROUNDS = NKT // QT
    with ExitStack() as ctx:
        wkv = sb(nc, ctx, "gx_wkv", [128, 2, CC, 2 * XKV * XD], F32R)
        wo = sb(nc, ctx, "gx_wo", [128, XH, HID])
        raw = sb(nc, ctx, "gx_raw", [128, CC, KS])
        piece = sb(nc, ctx, "gx_piece", [128, 2, 2, CC, KS], F32R)
        kT = sb(nc, ctx, "gx_kT", [128, 2, XKV, CTX])
        val = sb(nc, ctx, "gx_val", [KT, 2, NKT, XKV * XD])
        qT = sb(nc, ctx, "gx_qT", [128, 2, XH, SEQ])
        oT = sb(nc, ctx, "gx_oT", [128, XH, PT])
        ksq = sb(nc, ctx, "gx_ksq", [KT, 512])
        kssq = sb(nc, ctx, "gx_kssq", [KT, 4])
        kmean = sb(nc, ctx, "gx_kmean", [KT, 4])
        krms = sb(nc, ctx, "gx_krms", [KT, 4])
        kn = sb(nc, ctx, "gx_kn", [KT, 2, 512])
        prob = sb(nc, ctx, "gx_prob", [PT, 2, CTX])
        pT = sb(nc, ctx, "gx_pT", [KT, NKT, PT])
        negmax = sb(nc, ctx, "gx_negmax", [PT, 2])
        total = sb(nc, ctx, "gx_total", [PT, 2])
        rtotal = sb(nc, ctx, "gx_rtotal", [PT, 2])
        ps_s = pb(nc, ctx, "gx_ps_s", 3)
        ps_t = pb(nc, ctx, "gx_ps_t", 2)
        ps_k = pb(nc, ctx, "gx_ps_k", 1)
        ps_v = pb(nc, ctx, "gx_ps_v", 1)
        ps_o = pb(nc, ctx, "gx_ps_o", 1)
        s = sems(nc, ctx, "gx", "weights scored negmax exped rtotal probn pv stored projected added "
                 "k_ps v_ps k_sq k_ssq k_mean k_rms k_normed v_copied raw_in split w_high w_split wo_in", pairs="q_in")
        turned = [sem(nc, ctx, f"gx_turned{j}") for j in range(2)]
        copied = [sem(nc, ctx, f"gx_copied{j}") for j in range(2)]
        block = ctx.enter_context(nc.Block())
        quad = lambda x: x.rearrange("q (v n) -> q v n", v=4)

        TURNS = 2 * NKT + 2 * HP * ROUNDS
        LACKING = ((ROUNDS + 1) // 2, ROUNDS // 2)

        wraw = kT[:, 1, 0:CC, 0:2 * XKV * XD]

        def plan(first, last):
            tasks, n = [], 0

            def turn(kind, e, x):
                nonlocal n
                tasks.append((kind, e, x, n % 2, n // 2))
                n += 1

            def values(e):
                tasks.append(("values", e, 0, None, ((n + 1) // 2, n // 2)))

            def make_values(e, tile):
                tasks.append(("make_values", e, tile, None, None))
                if tile % QT == QT - 1 and not (last and tile // QT > 0):
                    tasks.append(("split", e, tile // QT, None, None))

            if first:
                n = ROUNDS
            for e in range(2 * HP):
                j, h = e // HP % 2, e % HP
                tiles = [] if last and j == 1 else list(range(FIRST[h], FIRST[h + 1]))
                tasks.append(("scores", e, 0, None, ((n + 1) // 2, n // 2)))
                if tiles and h:
                    for tile in range(FIRST[h - 1], FIRST[h]):
                        turn("turn_keys", e, tile)
                if e or not first:
                    for r in range(ROUNDS - 1):
                        turn("turn_probs", e - 1, r)
                tasks.append(("exp", e, 0, None, None))
                if tiles:
                    tasks.append(("make_keys", e, tiles[0], None, None))
                if e or not first:
                    turn("turn_probs", e - 1, ROUNDS - 1)
                if tiles:
                    tasks.append(("sum_keys", e, tiles[0], None, None))
                tasks.append(("norm", e, 0, None, None))
                if tiles:
                    tasks.append(("scale_keys", e, tiles[0], None, None))
                if tiles and h:
                    make_values(e, tiles[0])
                if e or not first:
                    values(e - 1)
                if tiles and not h:
                    make_values(e, tiles[0])
                if e == 0 and not first:
                    tasks.append(("project", -1, 0, None, None))
                for tile in tiles[1:]:
                    for kind in ("make_keys", "sum_keys", "scale_keys"):
                        tasks.append((kind, e, tile, None, None))
                    make_values(e, tile)
                if tiles and h == HP - 1:
                    for tile in tiles:
                        turn("turn_keys", e, tile)
            return tasks

        def ending():
            tasks = [("turn_probs", -1, r, r % 2, r // 2) for r in range(ROUNDS)]
            return tasks + [("values", -1, 0, None, ((ROUNDS + 1) // 2, ROUNDS // 2)), ("project", -1, 0, None, None)]

        def pairs(eng, task):
            def run(i, tasks, lacking=LACKING):
                before = [TURNS // 2 * i + (NKT // 2 - x) for x in lacking]
                for kind, e, n, bank, uses in tasks:
                    if bank is not None:
                        uses = before[bank] + uses
                    elif uses is not None:
                        uses = [before[b] + uses[b] for b in range(2)]
                    task(i, kind, e, n, bank, uses)

            run(0, plan(True, False))
            with eng.Fori(0, PAIRS - 2) as i:
                run(i + 1, plan(False, False))
            run(PAIRS - 1, plan(False, True))
            run(PAIRS, ending(), [x + NKT // 2 for x in LACKING])

        def dve_copies(r):
            return r == ROUNDS - 1

        def key_tile(i, e, tile):
            j = e // HP
            return (j + 1) % 2, NKT * (2 * i + j + 1) + tile

        @block.sync
        def _(sp):
            def load(n):
                if not (isinstance(n, int) and n == 0):
                    sp.wait_ge(s.split, 2 * n)
                sp.dma_start(raw[:], t["x_ctxT"][n]).then_inc(s.raw_in, 16)

            def load_q(i, j, used):
                if used is not None:
                    sp.wait_ge(s.scored, used)
                sp.dma_start(qT[:, j], k.scratch_q[i, :, j]).then_inc(s.q_in[j], 16)

            sp.dma_start(wraw, t["x_wkv"]).then_inc(s.weights, 16)
            load(0)
            load_q(0, 0, None)
            sp.dma_start(wo[:], t["x_wo"]).then_inc(s.wo_in, 16)
            for n in range(1, PIECES + 2):
                load(n)

            def pair(i, first, last):
                load_q(i, 1, None if first else 2 * HP * i)
                for q in range(PIECES + 2, PIECES + 3 if last else 3 * PIECES + 2):
                    load(2 * PIECES * i + q)
                    if q == 2 * PIECES + 2:
                        load_q(i + 1, 0, 2 * HP * i + HP)

            pair(0, True, False)
            with sp.Fori(0, PAIRS - 2) as i:
                pair(i + 1, False, False)
            pair(PAIRS - 1, False, True)

        @block.tensor
        def _(pe):
            def make_keys(slot, count, tile, pieces):
                if tile % QT == 0:
                    pe.wait_ge(s.split, 2 * pieces)
                pe.wait_ge(s.k_normed, count)
                product(ps_k, slot, tile, 0).then_inc(s.k_ps, 1)

            def make_values(slot, count, tile):
                pe.wait_ge(s.v_copied, count)
                product(ps_v, slot, tile, XKV * XD).then_inc(s.v_ps, 1)

            def product(psum, slot, tile, w0):
                lo = tile % QT * KT
                terms = [(c, a, b) for c in range(CC) for a, b in SPLIT_TERMS]
                for c, a, b in terms:
                    last = nc.tensor.matmul(psum[0:KT, 0, :], piece[:, slot, a, c, lo:lo + KT],
                                            wkv[:, b, c, w0:w0 + 512], start=((c, a, b) == terms[0]),
                                            stop=((c, a, b) == terms[-1]))
                return last

            def turn_keys(tile, count, bank, use):
                pe.wait_ge(s.k_normed, count + 1)
                pe.wait_ge(copied[bank], use)
                for g in range(XKV):
                    last = nc.tensor.transpose(ps_t[:, bank, g * KT:(g + 1) * KT],
                                               kn[:, tile % 2, g * 128:(g + 1) * 128], k.ident[0:KT, 0:KT])
                last.then_inc(turned[bank], 1)

            def task(i, kind, e, n, bank, use):
                j, h = e // HP % 2, e % HP
                step = 2 * HP * i + e
                if kind == "scores":
                    if h == 0:
                        pe.wait_ge(s.q_in[j], 16 * i + 16)
                        pe.wait_ge(s.v_copied, NKT * (2 * i + j + 1))
                        for b in range(2):
                            pe.wait_ge(copied[b], use[b])
                    pe.wait_ge(s.exped, step)
                    for b in range(NKS):
                        last = nc.tensor.matmul(ps_s[0:PT, b, 0:KS], qT[:, j, 2 * h:2 * h + 2, :],
                                                kT[:, j, h // 2, b * KS:(b + 1) * KS], start=True, stop=True)
                    last.then_inc(s.scored, 1)
                elif kind == "turn_keys":
                    slot, count = key_tile(i, e, n)
                    turn_keys(n, count, bank, use)
                elif kind == "make_keys":
                    slot, count = key_tile(i, e, n)
                    pn = PIECES * (j + 1) + n // QT
                    make_keys(pn % 2, count, n, 2 * PIECES * i + pn + 1)
                elif kind == "make_values":
                    slot, count = key_tile(i, e, n)
                    make_values((PIECES * (j + 1) + n // QT) % 2, count, n)
                elif kind == "turn_probs":
                    if n == 0:
                        pe.wait_ge(s.probn, step + 1)
                    pe.wait_ge(copied[bank], use)
                    for x in range(QT):
                        last = nc.tensor.transpose(ps_t[0:KT, bank, x * PT:(x + 1) * PT],
                                                   prob[:, e % 2, (n * QT + x) * KT:(n * QT + x + 1) * KT],
                                                   k.ident[0:PT, 0:PT])
                    last.then_inc(turned[bank], 1)
                elif kind == "values":
                    for b in range(2):
                        pe.wait_ge(copied[b], use[b])
                    pe.wait_ge(s.stored, step)
                    if e == 0:
                        pe.wait_ge(s.added, i)
                    for x in range(NKT):
                        last = nc.tensor.matmul(ps_o[:, 0, 0:PT], val[:, j, x, h // 2 * 128:(h // 2 + 1) * 128],
                                                pT[:, x, :], start=(x == 0), stop=(x == NKT - 1))
                    last.then_inc(s.pv, 1)
                elif kind == "project":
                    pe.wait_ge(s.wo_in, 16)
                    pe.wait_ge(s.stored, 2 * HP * i)
                    for x in range(XH):
                        last = nc.tensor.matmul(ps_o[0:PT, 0, 0:HID], oT[:, x, :], wo[:, x, :],
                                                start=(x == 0), stop=(x == XH - 1))
                    last.then_inc(s.projected, 1)

            pe.wait_ge(s.w_split, 1)
            for tile in range(NKT):
                make_keys(tile // QT % 2, tile, tile, tile // QT + 1)
                make_values(tile // QT % 2, tile, tile)
                if tile:
                    turn_keys(tile - 1, tile - 1, (tile - 1) % 2, (tile - 1) // 2)
            turn_keys(NKT - 1, NKT - 1, (NKT - 1) % 2, (NKT - 1) // 2)
            pairs(pe, task)

        def copy_keys(eng, copy, slot, tile, bank, use):
            eng.wait_ge(turned[bank], use + 1)
            copy(kT[:, slot, :, tile * KT:(tile + 1) * KT],
                 ps_t[:, bank, 0:XKV * KT].rearrange("d (g n) -> d g n", g=XKV)).then_inc(copied[bank], 1)

        def copy_probs(eng, copy, r, bank, use):
            eng.wait_ge(turned[bank], use + 1)
            copy(pT[:, r * QT:(r + 1) * QT, :].rearrange("q x n -> q (x n)"), ps_t[0:KT, bank, 0:QT * PT])\
                .then_inc(copied[bank], 1)

        @block.scalar
        def _(act):
            def square(count):
                act.wait_ge(s.k_ps, count + 1)
                act.wait_ge(s.k_ssq, count)
                nc.scalar.square(ksq[:], ps_k[0:KT, 0, :]).then_inc(s.k_sq, 1)

            def copy_values(slot, tile, count):
                act.wait_ge(s.v_ps, count + 1)
                nc.scalar.copy(val[:, slot, tile, :], ps_v[0:KT, 0, :]).then_inc(s.v_copied, 1)

            def task(i, kind, e, n, bank, use):
                j, h = e // HP % 2, e % HP
                step = 2 * HP * i + e
                if kind == "exp":
                    act.wait_ge(s.negmax, step + 1)
                    nc.scalar.activation(prob[:, e % 2, :].rearrange("q (b n) -> q b n", b=NKS), ps_s[0:PT, :, 0:KS],
                                         ACT.Exp, bias=negmax[:, e % 2:e % 2 + 1],
                                         accum_out=total[:, e % 2:e % 2 + 1]).then_inc(s.exped, 1)
                elif kind == "sum_keys":
                    square(key_tile(i, e, n)[1])
                elif kind == "make_values":
                    slot, count = key_tile(i, e, n)
                    copy_values(slot, n, count)
                elif kind == "turn_keys":
                    copy_keys(act, nc.scalar.copy, key_tile(i, e, n)[0], n, bank, use)
                elif kind == "turn_probs" and not dve_copies(n):
                    copy_probs(act, nc.scalar.copy, n, bank, use)
                elif kind == "values":
                    act.wait_ge(s.pv, step + 1)
                    if e == 0:
                        act.wait_ge(s.projected, i)
                    nc.scalar.copy(oT[:, 2 * h:2 * h + 2, j * SEQ:(j + 1) * SEQ],
                                   ps_o[:, 0, 0:PT].rearrange("d (h n) -> d h n", h=2)).then_inc(s.stored, 1)

            act.wait_ge(s.weights, 16)
            nc.scalar.copy(wkv[:, 0], wraw).then_inc(s.w_high, 1)
            for tile in range(NKT):
                square(tile)
                copy_values(0, tile, tile)
                if tile and (tile - 1) % 2 == 0:
                    copy_keys(act, nc.scalar.copy, 0, tile - 1, 0, (tile - 1) // 2)
            pairs(act, task)

        @block.gpsimd
        def _(pool):
            def root(count):
                pool.wait_ge(s.k_mean, count + 1)
                nc.gpsimd.tensor_tensor(krms[:], kmean[:], k.minus_half[0:KT, 0:4], ALU.pow).then_inc(s.k_rms, 1)

            def task(i, kind, e, n, bank, use):
                if kind == "scale_keys":
                    root(key_tile(i, e, n)[1])
                elif kind == "split":
                    split(2 * PIECES * i + PIECES * (e // HP + 1) + n + 2, (e // HP + 1 + n) % 2)

            def split(n, slot):
                if not (isinstance(n, int) and n < 2):
                    pool.wait_ge(s.v_ps, QT * (n - 1))
                pool.wait_ge(s.raw_in, 16 * n + 16)
                nc.gpsimd.tensor_tensor(piece[:, slot, 0], raw[:], k.ones[:, 0:1].unsqueeze(2)
                                        .broadcast_to([128, CC, KS]), ALU.mult).then_inc(s.split, 1)
                pool.wait_ge(s.split, 2 * n + 1)
                nc.gpsimd.tensor_tensor(piece[:, slot, 1], raw[:], piece[:, slot, 0], ALU.subtract)\
                    .then_inc(s.split, 1)

            split(0, 0)
            split(1, 1)
            for tile in range(NKT):
                root(tile)
                if tile % QT == QT - 1:
                    split(tile // QT + 2, tile // QT % 2)
            pairs(pool, task)

        @block.vector
        def _(dve):
            def sum_keys(count):
                dve.wait_ge(s.k_sq, count + 1)
                nc.vector.tensor_reduce(kssq[:], quad(ksq[:]), AX.X, ALU.add).then_inc(s.k_ssq, 1)
                dve.wait_ge(s.k_ssq, count + 1)
                nc.vector.tensor_scalar(kmean[:], kssq[:], 1.0 / XD, 1e-6, ALU.mult, ALU.add).then_inc(s.k_mean, 1)

            def scale_keys(count, tile):
                dve.wait_ge(s.k_rms, count + 1)
                nc.vector.tensor_tensor(quad(kn[:, tile % 2, :]), quad(ps_k[0:KT, 0, :]),
                                        krms[:].unsqueeze(2).broadcast_to([KT, 4, 128]), ALU.mult)\
                    .then_inc(s.k_normed, 1)

            def task(i, kind, e, n, bank, use):
                j, h = e // HP % 2, e % HP
                step = 2 * HP * i + e
                if kind == "scores":
                    dve.wait_ge(s.scored, step + 1)
                    nc.vector.tensor_reduce(negmax[:, e % 2:e % 2 + 1], ps_s[0:PT, :, 0:KS], AX.XY, ALU.max,
                                            negate=True).then_inc(s.negmax, 1)
                elif kind == "sum_keys":
                    sum_keys(key_tile(i, e, n)[1])
                elif kind == "scale_keys":
                    scale_keys(key_tile(i, e, n)[1], n)
                elif kind == "norm":
                    dve.wait_ge(s.exped, step + 1)
                    nc.vector.reciprocal(rtotal[:, e % 2:e % 2 + 1], total[:, e % 2:e % 2 + 1]).then_inc(s.rtotal, 1)
                    dve.wait_ge(s.rtotal, step + 1)
                    nc.vector.tensor_scalar_mul(prob[:, e % 2, :], prob[:, e % 2, :],
                                                rtotal[:, e % 2:e % 2 + 1]).then_inc(s.probn, 1)
                elif kind == "turn_probs" and dve_copies(n):
                    copy_probs(dve, nc.vector.tensor_copy, n, bank, use)
                elif kind == "project":
                    dve.wait_ge(s.projected, i)
                    nc.vector.tensor_tensor(k.x[:, i - 1, :], k.x[:, i - 1, :], ps_o[0:PT, 0, 0:HID], ALU.add)\
                        .then_inc(s.added, 1)

            dve.wait_ge(s.w_high, 1)
            nc.vector.tensor_tensor(wkv[:, 1], wraw, wkv[:, 0], ALU.subtract).then_inc(s.w_split, 1)
            for tile in range(NKT):
                sum_keys(tile)
                scale_keys(tile, tile)
                if tile and (tile - 1) % 2 == 1:
                    copy_keys(dve, nc.vector.tensor_copy, 0, tile - 1, 1, (tile - 1) // 2)
            copy_keys(dve, nc.vector.tensor_copy, 0, NKT - 1, 1, (NKT - 1) // 2)
            pairs(dve, task)


def grouped_attention(nc, k, t):
    k.scratch_q = nc.dram_tensor("scratch_q", [PAIRS, 128, 2, XH, SEQ], F32, kind="Internal").ap()
    grouped_queries(nc, k, t)
    grouped_softmax(nc, k, t)


def lora_slots(nc, k, t):
    ER = E1 * R1
    with ExitStack() as ctx:
        a1 = sb(nc, ctx, "ls_a1", [128, CC, ER])
        chosen = sb(nc, ctx, "ls_chosen", [PT, 2, PAIRS, E1])
        z = sb(nc, ctx, "ls_z", [PT, 2, PAIRS, 128])
        ps = pb(nc, ctx, "ls_ps", 1)
        pt = pb(nc, ctx, "ls_pt", 4)
        s = sems(nc, ctx, "ls", "loaded product onehot chosen weight scaled zeroed masked turned copied summed")
        block = ctx.enter_context(nc.Block())
        psv = ps[0:PT, 0, :].rearrange("q (p n) -> q p n", p=PAIRS)

        @block.sync
        def _(sp):
            sp.dma_start(a1[:], t["l_a1"]).then_inc(s.loaded, 16)

        @block.gpsimd
        def _(pool):
            nc.gpsimd.memset(z[:], 0.0).then_inc(s.zeroed, 1)

        @block.tensor
        def _(pe):
            pe.wait_ge(s.loaded, 16)
            for p in range(PAIRS):
                for c in range(CC):
                    last = nc.tensor.matmul(psv[:, p, :], k.xnT[:, c, p * PT:(p + 1) * PT], a1[:, c, :],
                                            start=(c == 0), stop=(c == CC - 1))
            last.then_inc(s.product, 1)
            for m in range(2):
                for half in range(2):
                    pe.wait_ge(s.masked, (m + 1) * PAIRS)
                    for e in range(HPAIRS):
                        last = nc.tensor.transpose(pt[:, 2 * m + half, e * PT:(e + 1) * PT],
                                                   z[:, m, half * HPAIRS + e, :], k.ident[0:PT, 0:PT])
                    last.then_inc(s.turned, 1)

        @block.scalar
        def _(act):
            for n in range(4):
                act.wait_ge(s.turned, n + 1)
                nc.scalar.copy(k.zT[:, n // 2, (n % 2) * HALF:(n % 2 + 1) * HALF], pt[:, n, 0:HALF])\
                    .then_inc(s.copied, 1)

        @block.vector
        def _(dve):
            for m in range(2):
                nc.vector.tensor_scalar(k.onehot[:, m], k.rank[:], float(m), None, ALU.is_equal).then_inc(s.onehot, 1)
                dve.wait_ge(s.onehot, m + 1)
                nc.vector.tensor_tensor(chosen[:, m], k.onehot[:, m], k.prob[:], ALU.mult).then_inc(s.chosen, 1)
                dve.wait_ge(s.chosen, m + 1)
                nc.vector.tensor_reduce(k.wchoice[:, m, :], chosen[:, m], AX.X, ALU.add).then_inc(s.weight, 1)
                nc.vector.tensor_scalar_mul(k.onehotw[:, m], chosen[:, m], LSCALE).then_inc(s.scaled, 1)
            dve.wait_ge(s.weight, 2)
            nc.vector.tensor_tensor(k.wsum[:], k.wchoice[:, 0, :], k.wchoice[:, 1, :], ALU.add).then_inc(s.summed, 1)
            dve.wait_ge(s.product, 1)
            dve.wait_ge(s.zeroed, 1)
            for m in range(2):
                for p in range(PAIRS):
                    nc.vector.scalar_tensor_tensor(out=z[:, m, p, 0:ER].rearrange("q (e r) -> q e r", r=R1),
                                                   in0=psv[:, p, :].rearrange("q (e r) -> q e r", r=R1), scalar=LSCALE,
                                                   in1=k.onehot[:, m, p, :].unsqueeze(2).broadcast_to([PT, E1, R1]),
                                                   op0=ALU.mult, op1=ALU.mult).then_inc(s.masked, 1)


def lora_mlp(nc, k, t):
    FT = F1 // 128
    ER = E1 * R1
    with ExitStack() as ctx:
        w1 = sb(nc, ctx, "lm_w1", [128, CC, F1])
        b1x = sb(nc, ctx, "lm_b1x", [128, F1])
        b1 = sb(nc, ctx, "lm_b1", [128, FT])
        w2a2 = sb(nc, ctx, "lm_w2a2", [128, FT, HID + ER])
        b2x = sb(nc, ctx, "lm_b2x", [128, HID])
        b2 = sb(nc, ctx, "lm_b2", [PT, HID])
        hT = sb(nc, ctx, "lm_hT", [128, 2, FT, TOK])
        z2 = sb(nc, ctx, "lm_z2", [PT, PAIRS, 128])
        part = sb(nc, ctx, "lm_part", [PT, 2, ER])
        z2T = sb(nc, ctx, "lm_z2T", [128, TOK])
        up = pb(nc, ctx, "lm_up", 4)
        down = pb(nc, ctx, "lm_down", 2)
        pt = pb(nc, ctx, "lm_pt", 2)
        s = sems(nc, ctx, "lm", "loaded upped gelued downed weighed parted zeroed summed turned copied last added")
        block = ctx.enter_context(nc.Block())
        N = 4 * FT

        @block.sync
        def _(sp):
            for dst, name in ((w1, "l_w1"), (b1x, "l_b1x"), (b1, "l_b1"), (w2a2, "l_w2a2"), (b2x, "l_b2x"), (b2, "l_b2")):
                sp.dma_start(dst[:], t[name]).then_inc(s.loaded, 16)

        @block.gpsimd
        def _(pool):
            nc.gpsimd.memset(z2[:], 0.0).then_inc(s.zeroed, 1)

        @block.tensor
        def _(pe):
            pe.wait_ge(s.loaded, 96)
            for n in range(N):
                f, m, half = n // 4, n // 2 % 2, n % 2
                if n >= 4:
                    pe.wait_ge(s.gelued, n - 3)
                cols = slice(half * HALF, (half + 1) * HALF)
                for c in range(CC):
                    nc.tensor.matmul(up[:, n % 4, 0:HALF], w1[:, c, f * 128:(f + 1) * 128], k.xnT[:, c, cols],
                                     start=(c == 0), stop=False)
                nc.tensor.matmul(up[:, n % 4, 0:HALF], b1x[:, f * 128:(f + 1) * 128], k.zT[:, m, cols],
                                 start=False, stop=True).then_inc(s.upped, 1)
            pe.wait_ge(s.gelued, N)
            for n in range(2 * PAIRS):
                p, m = n // 2, n % 2
                if n >= 2:
                    pe.wait_ge(s.parted, n - 1)
                for f in range(FT):
                    last = nc.tensor.matmul(down[0:PT, m, 0:HID + ER], hT[:, m, f, p * PT:(p + 1) * PT],
                                            w2a2[:, f, :], start=(f == 0), stop=(f == FT - 1))
                last.then_inc(s.downed, 1)
            for half in range(2):
                pe.wait_ge(s.summed, (half + 1) * HPAIRS)
                for e in range(HPAIRS):
                    last = nc.tensor.transpose(pt[:, half, e * PT:(e + 1) * PT], z2[:, half * HPAIRS + e, :],
                                               k.ident[0:PT, 0:PT])
                last.then_inc(s.turned, 1)
            for p in range(PAIRS):
                pe.wait_ge(s.copied, p // HPAIRS + 1)
                if p >= 4:
                    pe.wait_ge(s.added, p - 3)
                nc.tensor.matmul(up[0:PT, p % 4, 0:HID], z2T[:, p * PT:(p + 1) * PT], b2x[:],
                                 start=True, stop=True).then_inc(s.last, 1)

        @block.scalar
        def _(act):
            act.wait_ge(s.loaded, 96)
            for n in range(N):
                f, m, half = n // 4, n // 2 % 2, n % 2
                act.wait_ge(s.upped, n + 1)
                nc.scalar.activation(hT[:, m, f, half * HALF:(half + 1) * HALF], up[:, n % 4, 0:HALF],
                                     ACT.Gelu_apprx_tanh, bias=b1[:, f:f + 1]).then_inc(s.gelued, 1)
            for half in range(2):
                act.wait_ge(s.turned, half + 1)
                nc.scalar.copy(z2T[:, half * HALF:(half + 1) * HALF], pt[:, half, 0:HALF]).then_inc(s.copied, 1)

        @block.vector
        def _(dve):
            dve.wait_ge(s.loaded, 96)
            for p in range(PAIRS):
                nc.vector.scalar_tensor_tensor(out=k.x[:, p, :], in0=b2[:], scalar=k.wsum[:, p:p + 1],
                                               in1=k.x[:, p, :], op0=ALU.mult, op1=ALU.add).then_inc(s.weighed, 1)
            dve.wait_ge(s.zeroed, 1)
            for n in range(2 * PAIRS):
                p, m = n // 2, n % 2
                dve.wait_ge(s.downed, n + 1)
                dve.wait_ge(s.weighed, PAIRS + n if m else p + 1)
                nc.vector.scalar_tensor_tensor(out=k.x[:, p, :], in0=down[0:PT, m, 0:HID],
                                               scalar=k.wchoice[:, m, p:p + 1], in1=k.x[:, p, :],
                                               op0=ALU.mult, op1=ALU.add).then_inc(s.weighed, 1)
                if n >= 2:
                    dve.wait_ge(s.summed, n // 2)
                nc.vector.tensor_tensor(part[:, m, :].rearrange("q (e r) -> q e r", r=R1),
                                        down[0:PT, m, HID:HID + ER].rearrange("q (e r) -> q e r", r=R1),
                                        k.onehotw[:, m, p, :].unsqueeze(2).broadcast_to([PT, E1, R1]), ALU.mult)\
                    .then_inc(s.parted, 1)
                if m:
                    dve.wait_ge(s.parted, n + 1)
                    nc.vector.tensor_tensor(z2[:, p, 0:ER], part[:, 0, :], part[:, 1, :], ALU.add).then_inc(s.summed, 1)
            dve.wait_ge(s.weighed, 3 * PAIRS)
            for p in range(PAIRS):
                dve.wait_ge(s.last, p + 1)
                nc.vector.tensor_tensor(k.x[:, p, :], k.x[:, p, :], up[0:PT, p % 4, 0:HID], ALU.add)\
                    .then_inc(s.added, 1)


def routed_lora(nc, k, t):
    with ExitStack() as ctx:
        k.t = t
        k.prob = sb(nc, ctx, "rl_prob", [PT, PAIRS, E1])
        k.rank = sb(nc, ctx, "rl_rank", [PT, PAIRS, E1])
        k.onehot = sb(nc, ctx, "rl_onehot", [PT, 2, PAIRS, E1])
        k.onehotw = sb(nc, ctx, "rl_onehotw", [PT, 2, PAIRS, E1])
        k.wchoice = sb(nc, ctx, "rl_wchoice", [PT, 2, PAIRS])
        k.wsum = sb(nc, ctx, "rl_wsum", [PT, PAIRS])
        k.zT = sb(nc, ctx, "rl_zT", [128, 2, TOK])
        route(nc, k, "r1", t["r1_w"], t["r1_b"])
        lora_slots(nc, k, t)
        lora_mlp(nc, k, t)


def decoder(nc, t, out, stages=range(6)):
    with ExitStack() as ctx:
        k = Shared()
        k.x = sb(nc, ctx, "x", [PT, PAIRS, HID])
        k.xnT = sb(nc, ctx, "xnT", [128, CC, TOK])
        k.ident = sb(nc, ctx, "ident", [128, 128])
        k.ones = sb(nc, ctx, "ones", [128, 128])
        k.minus_half = sb(nc, ctx, "minus_half", [128, 48])
        k.eps6 = sb(nc, ctx, "eps6", [128, 32])
        k.half = sb(nc, ctx, "half", [128, 8])
        load_constants(nc, k, t)
        sublayers = [gated_delta_rule, context_attention, routed_swiglu, feature_attention,
                     grouped_attention, routed_lora]
        for i in stages:
            layernorm(nc, k, f"ln{i}")
            sublayers[i](nc, k, t)
        store_result(nc, k, out)


def lay_out(**inputs):
    a = {n: np.asarray(v) for n, v in inputs.items()}
    f = np.ascontiguousarray

    def chunked(w):
        return f(w.T.reshape(-1, 128, w.shape[0]).transpose(1, 0, 2))

    def rows(v, n):
        return f(np.broadcast_to(v, (n, v.size)))

    o = {"x": f(a["x"].reshape(TOK, HID)), "ident": np.eye(128, dtype=np.float32)}

    w = a["L0_attn_W_qkv"]
    cw = a["L0_attn_conv_w"]
    qd = NK * DK
    per_head = []
    for h in range(NK):
        r0 = [qd + h * DK, h * DK, 2 * qd + 2 * h * DK, 2 * qd + (2 * h + 1) * DK]
        mats = np.stack([chunked(w[r:r + DK]) for r in r0], axis=1)
        taps = np.stack([cw[r:r + DK] for r in r0], axis=1)
        per_head.append(np.concatenate([mats.reshape(128, -1), taps.reshape(128, -1)], axis=1))
    o["gdn_w"] = f(np.stack(per_head))
    o["gdn_wba"] = chunked(np.concatenate([a["L0_attn_W_b"], a["L0_attn_W_a"]]))
    o["gdn_rows"] = rows(np.concatenate([a["L0_attn_dt_bias"], a["L0_attn_A_log"]]), PT)
    o["gdn_normw"] = rows(a["L0_attn_norm_w"], PT)
    o["gdn_wz"] = f(np.stack([chunked(a["L0_attn_W_z"][g * GV * 128:(g + 1) * GV * 128]) for g in range(GROUPS)]))
    o["gdn_wo"] = f(a["L0_attn_W_out"].T.reshape(GROUPS, GV, 128, HID).transpose(0, 2, 1, 3))
    r, c = np.arange(PT)[:, None], np.arange(PT)[None, :]
    same = (r // SEQ) == (c // SEQ)
    o["gdn_after"] = (same & (c < r)).astype(np.float32)
    o["gdn_upto"] = (same & (r <= c)).astype(np.float32)
    o["gdn_kqmask"] = f(np.concatenate([-(same & (r < c)).astype(np.float32),
                                        (same & (r <= c)).astype(np.float32)], axis=1))

    o["context"] = a["ctx_2048"]
    for n in "qkvo":
        o[f"c_w{n}"] = chunked(a[f"L0_xattn_w{n}"])

    o["r0_w"] = chunked(a["L0_ffn_gate_w"])
    e = np.arange(E0)
    o["earlier"] = rows((e[None, :] < e[:, None]).astype(np.float32).reshape(-1), PT)
    w1, w2, w3 = a["L0_ffn_w1"], a["L0_ffn_w2"], a["L0_ffn_w3"]
    o["s_w"] = f(np.stack([np.concatenate([chunked(w1[i]).reshape(128, -1), chunked(w3[i]).reshape(128, -1),
                                           chunked(w2[i]).reshape(128, -1)], axis=1) for i in range(E0)]))

    o["f_w"] = chunked(np.concatenate([a["L1_attn_Wq"], a["L1_attn_Wk"], a["L1_attn_Wv"]]))
    o["f_b"] = rows(np.concatenate([a["L1_attn_bq"], a["L1_attn_bk"], a["L1_attn_bv"]]), PT)
    o["f_wo"] = chunked(a["L1_attn_Wo"])
    o["f_bo"] = rows(a["L1_attn_bo"], PT)
    inv = (1.0 / np.float32(10000.0) ** (np.arange(0, AD, 2, dtype=np.float32) / AD)).astype(np.float32)
    ang = np.arange(SEQ, dtype=np.float32)[:, None] * inv[None, :]
    ang = np.concatenate([ang, ang], axis=1)
    sign = np.where(np.arange(AD) < AF, -1.0, 1.0).astype(np.float32)
    o["f_cos"] = f(np.tile(np.cos(ang), (2, 1)))
    o["f_sin"] = f(np.tile(np.sin(ang) * sign, (2, 1)))
    diag = np.zeros((128 // AD, AD, 128 // AD, AF), np.float32)
    for i in range(128 // AD):
        diag[i, :, i, :] = a["L1_attn_rand_matrix"].T
    o["f_r"] = f(diag.reshape(128, -1))

    o["x_wq"] = chunked(a["L1_xattn_Wq"].T)
    o["x_nw"] = f(np.stack([a["L1_xattn_q_norm_w"], a["L1_xattn_k_norm_w"]], axis=1))
    o["x_wkv"] = chunked(np.concatenate([a["L1_xattn_Wk"], a["L1_xattn_Wv"]], axis=1).T)
    o["x_wo"] = chunked(a["L1_xattn_Wo"].T)
    o["x_ctxT"] = f(a["ctx_2048"].reshape(BATCH * NKS, KS, CC, 128).transpose(0, 3, 2, 1))

    o["r1_w"] = chunked(a["L1_ffn_W_r"])
    o["r1_b"] = rows(a["L1_ffn_b_r"], PT)
    o["l_a1"] = chunked(a["L1_ffn_A1"].reshape(E1 * R1, HID))
    o["l_w1"] = chunked(a["L1_ffn_W1"])
    pad = np.zeros((128 - E1 * R1, F1), np.float32)
    o["l_b1x"] = f(np.concatenate([a["L1_ffn_B1"].transpose(0, 2, 1).reshape(E1 * R1, F1), pad]))
    o["l_b1"] = f(a["L1_ffn_b1"].reshape(F1 // 128, 128).T)
    o["l_w2a2"] = chunked(np.concatenate([a["L1_ffn_W2"], a["L1_ffn_A2"].reshape(E1 * R1, F1)]))
    o["l_b2x"] = f(np.concatenate([a["L1_ffn_B2"].transpose(0, 2, 1).reshape(E1 * R1, HID), pad[:, 0:HID]]))
    o["l_b2"] = rows(a["L1_ffn_b2"], PT)
    return o


def kernel(**inputs):
    import concourse.bacc as _bacc
    from concourse.bass_utils import run_bass_kernel_spmd as _run

    arrays = lay_out(**inputs)
    nc = _bacc.Bacc("TRN2", target_bir_lowering=False, num_devices=1)
    t = {n: nc.dram_tensor(n, v.shape, mybir.dt.from_np(v.dtype), kind="ExternalInput").ap()
         for n, v in arrays.items()}
    out = nc.dram_tensor("out", (TOK, HID), F32, kind="ExternalOutput").ap()
    decoder(nc, t, out)
    r = _run(nc, [arrays], core_ids=[0])
    return r.results[0]["out"].reshape(BATCH, SEQ, HID)
```

```python
from collections import namedtuple
from contextlib import ExitStack

import numpy as np

import concourse.bass as bass
from concourse import mybir

F32 = mybir.dt.float32
F32R = mybir.dt.float32r
ALU = mybir.AluOpType
ACT = mybir.ActivationFunctionType
AX = mybir.AxisListType

BATCH, SEQ, HID = 16, 56, 256
PAIRS = BATCH // 2
PT = 2 * SEQ
TOK = BATCH * SEQ
HALF = TOK // 2
HPAIRS = PAIRS // 2
CC = HID // 128
BANK = 512

SPLIT_TERMS = ((0, 0), (0, 1), (1, 0))

NK, DK, NV, KC = 16, 128, 32, 4
VPK = NV // NK
GROUPS = 4
GK = NK // GROUPS
GV = GK * VPK
SYS = PAIRS * GV
UNITS = PAIRS * GV // 4
BLK = SEQ // 2

CTX, KT = 1500, 125
NKT = CTX // KT
KS = 500
NKS = CTX // KS

E0, F0 = 8, 512
E1, R1, F1 = 8, 8, 1024
LSCALE = 2.0

AH, AHKV, AD = 16, 8, 16
AF = AD // 2
QKH = AH + AHKV

XH, XKV, XD = 16, 4, 128
XG = XH // XKV


class Shared:
    pass


def sb(nc, ctx, name, shape, dt=F32):
    return ctx.enter_context(nc.sbuf_tensor(f"{name}_sb", list(shape), dt))


def pb(nc, ctx, name, banks):
    return ctx.enter_context(nc.psum_tensor(name, [128, banks, BANK], F32))


def sem(nc, ctx, name):
    handle = nc.alloc_semaphore(name)
    ctx.callback(nc.clear_and_free_semaphores, [handle])
    return handle


def sems(nc, ctx, tag, names, pairs=""):
    ctx.callback(nc.all_engine_barrier)
    found = [sem(nc, ctx, f"{tag}_{n}") for n in names.split()]
    found += [[sem(nc, ctx, f"{tag}_{n}{j}") for j in range(2)] for n in pairs.split()]
    return namedtuple("Semaphores", f"{names} {pairs}")(*found)


def load_constants(nc, k, t):
    with ExitStack() as ctx:
        s = sems(nc, ctx, "init", "loaded filled")
        block = ctx.enter_context(nc.Block())

        @block.sync
        def _(sp):
            sp.dma_start(k.x[:], t["x"].rearrange("(p q) d -> q p d", q=PT)).then_inc(s.loaded, 16)
            sp.dma_start(k.ident[:], t["ident"]).then_inc(s.loaded, 16)
            sp.wait_ge(s.loaded, 32)

        @block.gpsimd
        def _(pool):
            nc.gpsimd.memset(k.ones[:], 1.0).then_inc(s.filled, 1)
            nc.gpsimd.memset(k.minus_half[:], -0.5).then_inc(s.filled, 1)
            nc.gpsimd.memset(k.half[:], 0.5).then_inc(s.filled, 1)
            nc.gpsimd.memset(k.eps6[:], 1e-6).then_inc(s.filled, 1)
            pool.wait_ge(s.filled, 4)


def store_result(nc, k, out):
    with ExitStack() as ctx:
        s = sems(nc, ctx, "end", "stored")
        block = ctx.enter_context(nc.Block())

        @block.sync
        def _(sp):
            sp.dma_start(out.rearrange("(p q) d -> q p d", q=PT), k.x[:]).then_inc(s.stored, 16)
            sp.wait_ge(s.stored, 16)


def layernorm(nc, k, tag, loads):
    with ExitStack() as ctx:
        stats = sb(nc, ctx, f"{tag}_stats", [PT, PAIRS, 6])
        meanvar = sb(nc, ctx, f"{tag}_meanvar", [PT, PAIRS, 2])
        vareps = sb(nc, ctx, f"{tag}_vareps", [PT, PAIRS])
        rstd = sb(nc, ctx, f"{tag}_rstd", [PT, PAIRS])
        xn = sb(nc, ctx, f"{tag}_xn", [PT, PAIRS, HID])
        ps = pb(nc, ctx, f"{tag}_ps", 4)
        s = sems(nc, ctx, tag, "loaded stats meanvar var_ready rstd_ready xn_ready turned copied")
        block = ctx.enter_context(nc.Block())

        @block.sync
        def _(sp):
            for dst, src in loads:
                sp.dma_start(dst, src).then_inc(s.loaded, 16)
            sp.wait_ge(s.loaded, 16 * len(loads))

        @block.vector
        def _(dve):
            for p in range(PAIRS):
                nc.vector.bn_stats(stats[:, p, :], k.x[:, p, :]).then_inc(s.stats, 1)
            for p in range(PAIRS):
                dve.wait_ge(s.stats, p + 1)
                nc.vector.bn_aggr(meanvar[:, p, :], stats[:, p, :]).then_inc(s.meanvar, 1)
            dve.wait_ge(s.meanvar, PAIRS)
            nc.vector.tensor_scalar_add(vareps[:], meanvar[:, :, 1], 1e-5).then_inc(s.var_ready, 1)
            dve.wait_ge(s.rstd_ready, 1)
            for p in range(PAIRS):
                nc.vector.tensor_scalar(xn[:, p, :], k.x[:, p, :], meanvar[:, p, 0:1], rstd[:, p:p + 1],
                                        ALU.subtract, ALU.mult).then_inc(s.xn_ready, 1)
            for b in (1, 3):
                dve.wait_ge(s.turned, b + 1)
                nc.vector.tensor_copy(k.xnT[:, b % CC, (b // CC) * HALF:(b // CC + 1) * HALF],
                                      ps[:, b, 0:HALF]).then_inc(s.copied, 1)

        @block.gpsimd
        def _(pool):
            pool.wait_ge(s.var_ready, 1)
            nc.gpsimd.tensor_tensor(rstd[:], vareps[:], k.minus_half[0:PT, 0:PAIRS], ALU.pow)\
                .then_inc(s.rstd_ready, 1)

        @block.tensor
        def _(pe):
            for b in range(4):
                pe.wait_ge(s.xn_ready, HPAIRS * (b // CC + 1))
                for p in range(HPAIRS):
                    last = nc.tensor.transpose(ps[:, b, p * PT:(p + 1) * PT],
                                               xn[:, (b // CC) * HPAIRS + p, (b % CC) * 128:(b % CC + 1) * 128],
                                               k.ident[0:PT, 0:PT])
                last.then_inc(s.turned, 1)

        @block.scalar
        def _(act):
            for b in (0, 2):
                act.wait_ge(s.turned, b + 1)
                nc.scalar.copy(k.xnT[:, b % CC, (b // CC) * HALF:(b // CC + 1) * HALF],
                               ps[:, b, 0:HALF]).then_inc(s.copied, 1)


def overlap_view(tensor, base, count, width):
    first = tensor[:, base, 0:width]
    return bass.AP(tensor=first.tensor, offset=first.offset, ap=[list(first.ap[0]), [1, count], [1, width]])


def gdn_gates(nc, k, t):
    with ExitStack() as ctx:
        wba = sb(nc, ctx, "gg_wba", [128, CC, 2 * NV])
        rows = sb(nc, ctx, "gg_rows", [PT, 2 * NV])
        exp_b = sb(nc, ctx, "gg_exp_b", [PT, PAIRS, NV])
        onep = sb(nc, ctx, "gg_onep", [PT, PAIRS, NV])
        a = sb(nc, ctx, "gg_a", [PT, PAIRS, NV])
        absa = sb(nc, ctx, "gg_absa", [PT, PAIRS, NV])
        exp_a = sb(nc, ctx, "gg_exp_a", [PT, PAIRS, NV])
        ln_a = sb(nc, ctx, "gg_ln_a", [PT, PAIRS, NV])
        dt = sb(nc, ctx, "gg_dt", [PT, PAIRS, NV])
        rate = sb(nc, ctx, "gg_rate", [PT, NV])
        layernorm(nc, k, "ln0", [(wba[:], t["gdn_wba"]), (rows[:], t["gdn_rows"]), (k.after[:], t["gdn_after"]),
                                 (k.upto[:], t["gdn_upto"]), (k.kqmask[:], t["gdn_kqmask"]),
                                 (k.normw[:], t["gdn_normw"])])
        ps = pb(nc, ctx, "gg_ps", 1)
        s = sems(nc, ctx, "gg", "product expb onep a_ready absa expa lna rate dt_ready done")
        block = ctx.enter_context(nc.Block())
        psv = ps[0:PT, 0, :].rearrange("q (p n) -> q p n", p=PAIRS)

        @block.tensor
        def _(pe):
            for p in range(PAIRS):
                for c in range(CC):
                    last = nc.tensor.matmul(psv[:, p, :], k.xnT[:, c, p * PT:(p + 1) * PT], wba[:, c, :],
                                            start=(c == 0), stop=(c == CC - 1))
            last.then_inc(s.product, 1)

        @block.scalar
        def _(act):
            act.wait_ge(s.product, 1)
            nc.scalar.activation(exp_b[:], psv[:, :, 0:NV], ACT.Exp, scale=-1.0).then_inc(s.expb, 1)
            nc.scalar.activation(rate[:], rows[:, NV:2 * NV], ACT.Exp).then_inc(s.rate, 1)
            act.wait_ge(s.absa, 1)
            nc.scalar.activation(exp_a[:], absa[:], ACT.Exp, scale=-1.0).then_inc(s.expa, 1)
            act.wait_ge(s.expa, 1)
            nc.scalar.activation(ln_a[:], exp_a[:], ACT.Ln, bias=1.0).then_inc(s.lna, 1)

        @block.vector
        def _(dve):
            dve.wait_ge(s.expb, 1)
            nc.vector.tensor_tensor(a[:], psv[:, :, NV:2 * NV],
                                    rows[:, 0:NV].unsqueeze(1).broadcast_to([PT, PAIRS, NV]), ALU.add)\
                .then_inc(s.a_ready, 1)
            dve.wait_ge(s.a_ready, 1)
            nc.vector.scalar_tensor_tensor(out=absa[:], in0=a[:], scalar=-1.0, in1=a[:],
                                           op0=ALU.mult, op1=ALU.max).then_inc(s.absa, 1)
            dve.wait_ge(s.expb, 1)
            nc.vector.tensor_scalar_add(onep[:], exp_b[:], 1.0).then_inc(s.onep, 1)
            dve.wait_ge(s.onep, 1)
            nc.vector.reciprocal(k.beta[:], onep[:]).then_inc(s.done, 1)
            dve.wait_ge(s.lna, 1)
            nc.vector.scalar_tensor_tensor(out=dt[:], in0=a[:], scalar=0.0, in1=ln_a[:],
                                           op0=ALU.max, op1=ALU.add).then_inc(s.dt_ready, 1)
            dve.wait_ge(s.dt_ready, 1)
            dve.wait_ge(s.rate, 1)
            nc.vector.scalar_tensor_tensor(out=k.logdecay[:], in0=dt[:], scalar=-1.0,
                                           in1=rate[:].unsqueeze(1).broadcast_to([PT, PAIRS, NV]),
                                           op0=ALU.mult, op1=ALU.mult).then_inc(s.done, 1)
            dve.wait_ge(s.done, 2)


def gdn_project(nc, k, t, grp, s, ctx):
    w = sb(nc, ctx, "gp_w", [128, 2, 4 * CC * 128 + 4 * KC])
    raw = sb(nc, ctx, "gp_raw", [128, 4, BATCH, KC - 1 + SEQ])
    conv = sb(nc, ctx, "gp_conv", [128, 2, 4, TOK])
    sq = sb(nc, ctx, "gp_sq", [128, 2, TOK])
    nsq = sb(nc, ctx, "gp_nsq", [PT, 2, PAIRS])
    nk = sb(nc, ctx, "gp_nk", [PT, PAIRS])
    proj = pb(nc, ctx, "gp_proj", 4)
    psk = pb(nc, ctx, "gp_psk", 2)
    psv = pb(nc, ctx, "gp_psv", 2)
    block = ctx.enter_context(nc.Block())
    wt = [w[:, j, 0:4 * CC * 128].rearrange("c (i k n) -> c i k n", i=4, k=CC) for j in range(2)]
    wc = [w[:, j, 4 * CC * 128:].rearrange("c (i k) -> c i k", i=4) for j in range(2)]
    STEPS = 4 * (KC - 2)

    def heads():
        for h in range(GK + 1):
            yield (h if h < GK else None), (h - 1 if h else None), grp * GK + h

    @block.sync
    def _(sp):
        for h in range(GK):
            if h >= 2:
                sp.wait_ge(s.conv_done, 4 * (grp * GK + h - 1))
            sp.dma_start(w[:, h % 2, :], t["gdn_w"][grp * GK + h]).then_inc(s.w_in[h % 2], 16)

    @block.tensor
    def _(pe):
        def project(h, n, q):
            if q == 0:
                pe.wait_ge(s.w_in[h % 2], 16 * (grp * 2 + h // 2) + 16)
            pe.wait_ge(s.evac, 8 * n + (q - 3 if q >= 4 else 0))
            for c in range(CC):
                last = nc.tensor.matmul(proj[:, q % 4, 0:HALF], wt[h % 2][:, q // 2, c, :],
                                        k.xnT[:, c, (q % 2) * HALF:(q % 2 + 1) * HALF],
                                        start=(c == 0), stop=(c == CC - 1))
            last.then_inc(s.projected, 1)

        def norms(h, n, which):
            pe.wait_ge(s.squared, 2 * n + which + 1)
            pe.wait_ge(s.v_done, 4 * n)
            for p in range(PAIRS):
                last = nc.tensor.matmul(psv[0:PT, 1, which * PAIRS + p:which * PAIRS + p + 1],
                                        sq[:, which, p * PT:(p + 1) * PT], k.ones[:, 0:1],
                                        start=True, stop=True)
            if which == 1:
                last.then_inc(s.ssq, 1)

        def products(h, n, quads):
            for gp in quads:
                pe.wait_ge(s.gm_done, 4 * n + (gp - 1 if gp >= 2 else 0))
                for e in range(2):
                    p = 2 * gp + e
                    last = nc.tensor.matmul(psk[0:PT, gp % 2, e * 2 * PT:(e + 1) * 2 * PT],
                                            conv[:, h % 2, 0, p * PT:(p + 1) * PT],
                                            conv[:, h % 2, 0:2, p * PT:(p + 1) * PT], start=True, stop=True)
                last.then_inc(s.kq_done, 1)

        def turn_values(h, n, tiles):
            for q in tiles:
                pe.wait_ge(s.conv_done, 4 * n + 3 + q // 2)
                if q == 1:
                    pe.wait_ge(s.nsq_ready, n + 1)
                pe.wait_ge(s.v_done, 4 * n + (q - 1 if q >= 2 else 0))
                for e in range(HPAIRS):
                    p = (q % 2) * HPAIRS + e
                    last = nc.tensor.transpose(psv[0:PT, q % 2, e * 128:(e + 1) * 128],
                                               conv[:, h % 2, 2 + q // 2, p * PT:(p + 1) * PT], k.ident[:])
                last.then_inc(s.v_turned[h % 2], 1)

        for new, old, n in heads():
            for part in range(4):
                for e in range(2):
                    if new is not None:
                        project(new, n, 2 * part + e)
                    if old is not None and part == 0:
                        norms(old, n - 1, e)
                if old is not None:
                    if part < 2:
                        products(old, n - 1, (2 * part, 2 * part + 1))
                    else:
                        turn_values(old, n - 1, (2 * part - 4, 2 * part - 3))

    @block.scalar
    def _(act):
        for h in range(GK):
            n = grp * GK + h
            if h >= 2:
                act.wait_ge(s.kq_done, 4 * (n - 1))
            for q in range(8):
                tile, half = q // 2, q % 2
                act.wait_ge(s.projected, 8 * n + q + 1)
                if h:
                    act.wait_ge(s.conv_done, 4 * (n - 1) + tile + 1)
                if q == 4 and h >= 2:
                    act.wait_ge(s.v_turned[h % 2], 4 * (grp * 2 + h // 2))
                src = proj[:, q % 4, 0:HALF]
                nc.scalar.copy(raw[:, tile, half * PAIRS:(half + 1) * PAIRS, KC - 1:],
                               src.rearrange("c (b t) -> c b t", t=SEQ))
                nc.scalar.mul(conv[:, h % 2, tile, half * HALF:(half + 1) * HALF], src,
                              wc[h % 2][:, tile, KC - 1:KC]).then_inc(s.evac, 1)

    @block.vector
    def _(dve):
        def convolve(h, n, tile):
            dve.wait_ge(s.evac, 8 * n + 2 * tile + 2)
            dst = conv[:, h % 2, tile, :].rearrange("c (b t) -> c b t", t=SEQ)
            for tap in range(KC - 1):
                if tap:
                    dve.wait_ge(s.conv_step, STEPS * n + 2 * tile + tap)
                done = s.conv_done if tap == KC - 2 else s.conv_step
                nc.vector.scalar_tensor_tensor(out=dst, in0=raw[:, tile, :, tap:tap + SEQ],
                                               scalar=wc[h % 2][:, tile, tap:tap + 1], in1=dst,
                                               op0=ALU.mult, op1=ALU.add).then_inc(done, 1)

        def norms(h, n):
            dve.wait_ge(s.ssq, n + 1)
            dve.wait_ge(s.roots, 2 * n)
            nc.vector.tensor_scalar_max(nsq[:], psv[0:PT, 1, 0:2 * PAIRS].rearrange("q (w p) -> q w p", w=2),
                                        1e-24).then_inc(s.nsq_ready, 1)
            dve.wait_ge(s.nsq_ready, n + 1)
            nc.vector.reciprocal(k.rnk2[:, h, :], nsq[:, 0, :]).then_inc(s.rnk2, 1)

        def mask(h, n, quads):
            for gp in quads:
                dve.wait_ge(s.kq_done, 4 * n + gp + 1)
                nc.vector.tensor_tensor(k.gmtt[:, h * PAIRS * 2 * PT:(h + 1) * PAIRS * 2 * PT]
                                        .rearrange("q (p w) -> q p w", p=PAIRS)[:, 2 * gp:2 * gp + 2, :],
                                        psk[0:PT, gp % 2, 0:4 * PT].rearrange("q (e w) -> q e w", e=2),
                                        k.kqmask[:].unsqueeze(1).broadcast_to([PT, 2, 2 * PT]),
                                        ALU.mult).then_inc(s.gm_done, 1)

        def values(h, n, tiles):
            dve.wait_ge(s.roots, 2 * n + 2)
            for q in tiles:
                dve.wait_ge(s.v_turned[h % 2], 4 * (grp * 2 + h // 2) + q + 1)
                nc.vector.tensor_tensor(k.v[:, h * VPK + q // 2, (q % 2) * HPAIRS:(q % 2 + 1) * HPAIRS, :],
                                        psv[0:PT, q % 2, :].rearrange("q (p d) -> q p d", p=HPAIRS),
                                        nk[:, (q % 2) * HPAIRS:(q % 2 + 1) * HPAIRS].unsqueeze(2)
                                        .broadcast_to([PT, HPAIRS, 128]), ALU.mult).then_inc(s.v_done, 1)

        nc.vector.memset(raw[:, :, :, 0:KC - 1], 0.0).then_inc(s.padded, 1)
        dve.wait_ge(s.padded, grp + 1)
        for new, old, n in heads():
            for part in range(4):
                if old is not None:
                    if part == 0:
                        norms(old, n - 1)
                    if part < 2:
                        mask(old, n - 1, (2 * part, 2 * part + 1))
                    else:
                        values(old, n - 1, (2 * part - 4, 2 * part - 3))
                if new is not None:
                    convolve(new, n, part)

    @block.gpsimd
    def _(pool):
        for new, old, n in heads():
            if old is not None:
                pool.wait_ge(s.nsq_ready, n)
                pool.wait_ge(s.v_done, 4 * (n - 1))
                nc.gpsimd.tensor_tensor(nk[:], nsq[:, 0, :], k.half[0:PT, 0:PAIRS], ALU.pow).then_inc(s.roots, 1)
                nc.gpsimd.tensor_tensor(k.rnq[:, old, :], nsq[:, 1, :], k.minus_half[0:PT, 0:PAIRS],
                                        ALU.pow).then_inc(s.roots, 1)
            if new is not None:
                pool.wait_ge(s.ssq, n)
                for which in range(2):
                    pool.wait_ge(s.conv_done, 4 * n + which + 1)
                    nc.gpsimd.tensor_tensor(sq[:, which, :], conv[:, new % 2, which, :], conv[:, new % 2, which, :],
                                            ALU.mult).then_inc(s.squared, 1)


def gdn_systems(nc, k, t, grp, s, ctx):
    cs = sb(nc, ctx, "gs_cs", [PT, PAIRS, GV])
    urhs = sb(nc, ctx, "gs_urhs", [PT, 2, 4, PT])
    dec = [sb(nc, ctx, f"gs_dec{j}", [PT, 4, PT + 1]) for j in range(2)]
    ps = pb(nc, ctx, "gs_ps", 2)
    block = ctx.enter_context(nc.Block())

    @block.gpsimd
    def _(pool):
        with pool.Fori(0, PAIRS) as p:
            for j in range(2):
                pool.wait_ge(s.emm[j], grp * PAIRS + p)
                nc.gpsimd.tensor_tensor(urhs[:, j], k.upto[:].unsqueeze(1).broadcast_to([PT, 4, PT]),
                                        k.logdecay[:, p, bass.ds(grp * GV + j * 4, 4)].unsqueeze(2)
                                        .broadcast_to([PT, 4, PT]), ALU.mult).then_inc(s.u_ready[j], 1)

    @block.tensor
    def _(pe):
        with pe.Fori(0, PAIRS) as p:
            for j in range(2):
                pe.wait_ge(s.u_ready[j], grp * PAIRS + p + 1)
                pe.wait_ge(s.dec_ready[j], grp * PAIRS + p)
                nc.tensor.matmul(ps[0:PT, j, 0:4 * PT], k.after[:], urhs[:, j], start=True, stop=True)\
                    .then_inc(s.emm[j], 1)

    @block.scalar
    def _(act):
        with act.Fori(0, PAIRS) as p:
            for j in range(2):
                act.wait_ge(s.emm[j], grp * PAIRS + p + 1)
                act.wait_ge(s.apt[j], 4 * (grp * PAIRS + p))
                nc.scalar.activation(dec[j][:, :, 1:], ps[0:PT, j, 0:4 * PT].rearrange("q (v w) -> q v w", v=4),
                                     ACT.Exp).then_inc(s.dec_ready[j], 1)

    @block.vector
    def _(dve):
        nc.vector.memset(dec[0][:, :, 0:1], 1.0).then_inc(s.lead, 1)
        nc.vector.memset(dec[1][:, :, 0:1], 1.0).then_inc(s.lead, 1)
        nc.vector.tensor_tensor(cs[:].rearrange("q p (h e) -> q p h e", e=VPK),
                                k.beta[:, :, bass.ds(grp * GV, GV)].rearrange("q p (h e) -> q p h e", e=VPK),
                                k.rnk2[:].rearrange("q h p -> q p h").unsqueeze(3)
                                .broadcast_to([PT, PAIRS, GK, VPK]), ALU.mult).then_inc(s.lead, 1)
        with dve.Fori(0, PAIRS) as p:
            for j in range(2):
                dve.wait_ge(s.lead, 3 * grp + 3)
                dve.wait_ge(s.dec_ready[j], grp * PAIRS + p + 1)
                for v in range(4):
                    vh = j * 4 + v
                    nc.vector.scalar_tensor_tensor(
                        out=k.apt[:, :, bass.ds(p * GV + vh, 1), :].rearrange("q a m w -> q a (m w)"),
                        in0=overlap_view(dec[j], v, 2, PT), scalar=cs[:, p, vh:vh + 1],
                        in1=k.gmtt[:, bass.ds((vh // VPK) * PAIRS * 2 * PT + p * 2 * PT, 2 * PT)]
                        .rearrange("q (a w) -> q a w", a=2),
                        op0=ALU.mult, op1=ALU.mult).then_inc(s.apt[j], 1)


def gdn_solve(nc, k, t, grp, s, ctx):
    wz = sb(nc, ctx, "gv_wz", [128, CC, GV * 128])
    sil = sb(nc, ctx, "gv_sil", [PT, 2, 512])
    ps = pb(nc, ctx, "gv_ps", 4)
    asys = sb(nc, ctx, "gv_asys", [2 * SYS, 2, BLK, BLK])
    tsys = sb(nc, ctx, "gv_tsys", [2 * SYS, 2, BLK, BLK])
    prod = sb(nc, ctx, "gv_prod", [2 * SYS, 2, BLK, BLK])
    block = ctx.enter_context(nc.Block())
    flat = lambda x: x.rearrange("m b r c -> m b (r c)")

    def upto(u):
        return grp * UNITS + u + 1

    @block.tensor
    def _(pe):
        pe.wait_ge(s.wz_in, 16 * grp + 16)
        for u in range(UNITS):
            p, q = u // 2, u % 2
            if u >= 4:
                pe.wait_ge(s.silu, upto(u - 4))
            for c in range(CC):
                last = nc.tensor.matmul(ps[0:PT, u % 4, :], k.xnT[:, c, p * PT:(p + 1) * PT],
                                        wz[:, c, q * 512:(q + 1) * 512], start=(c == 0), stop=(c == CC - 1))
            last.then_inc(s.z, 1)

    @block.scalar
    def _(act):
        for u in range(UNITS):
            act.wait_ge(s.z, upto(u))
            if u >= 2:
                act.wait_ge(s.gate, upto(u - 2))
            nc.scalar.activation(sil[:, u % 2, :], ps[0:PT, u % 4, :], ACT.Silu).then_inc(s.silu, 1)

    @block.sync
    def _(sp):
        for half in range(2):
            for b in range(2):
                r0 = half * SEQ + b * BLK
                sp.dma_start(k.scratch_a[half, b].rearrange("m r c -> r m c"),
                             k.apt[r0:r0 + BLK, 0, :, r0:r0 + BLK]).then_inc(s.a_out, 16)
        sp.wait_ge(s.a_out, 64 * (grp + 1))
        for half in range(2):
            sp.dma_start(flat(asys[half * SYS:(half + 1) * SYS]),
                         k.scratch_a[half].rearrange("b m r c -> m b (r c)")).then_inc(s.a_in, 16)
        sp.dma_start(wz[:], t["gdn_wz"][grp]).then_inc(s.wz_in, 16)
        sp.dma_start(k.wo[:], t["gdn_wo"][grp]).then_inc(s.wo_in, 16)
        sp.wait_ge(s.solved, (BLK - 1) * (grp + 1))
        for half in range(2):
            sp.dma_start(k.scratch_t[half].rearrange("b m r c -> m b (r c)"),
                         flat(tsys[half * SYS:(half + 1) * SYS])).then_inc(s.t_out, 16)
        sp.wait_ge(s.t_out, 32 * (grp + 1))
        sp.wait_ge(s.zeroed, grp + 1)
        for half in range(2):
            for b in range(2):
                r0 = half * SEQ + b * BLK
                sp.dma_start(k.tt[r0:r0 + BLK, :, r0:r0 + BLK],
                             k.scratch_t[half, b].rearrange("m r c -> r m c")).then_inc(s.t_in, 16)

    @block.gpsimd
    def _(pool):
        nc.gpsimd.memset(tsys[:], 0.0).then_inc(s.t_zero, 1)
        pool.wait_ge(s.t_zero, 2 * grp + 1)
        ones = k.ones[0:2 * SYS, 0:2 * BLK].rearrange("m (b r) -> m b r", b=2)
        nc.gpsimd.tensor_tensor(flat(tsys[:])[:, :, 0:BLK * BLK:BLK + 1], ones, ones, ALU.mult).then_inc(s.t_zero, 1)
        nc.gpsimd.memset(k.gmtt[:], 0.0).then_inc(s.zeroed, 1)
        for u in range(UNITS):
            pool.wait_ge(s.silu, upto(u))
            nc.gpsimd.tensor_tensor(k.gate[:, u, :].rearrange("q (v n) -> q v n", v=4),
                                    sil[:, u % 2, :].rearrange("q (v n) -> q v n", v=4),
                                    k.normw[:].unsqueeze(1).broadcast_to([PT, 4, 128]), ALU.mult)\
                .then_inc(s.gate, 1)
        pool.wait_ge(s.t_in, 64 * (grp + 1))

    @block.vector
    def _(dve):
        dve.wait_ge(s.a_in, 32 * (grp + 1))
        dve.wait_ge(s.t_zero, 2 * grp + 2)
        for c in range(1, BLK):
            if c > 1:
                dve.wait_ge(s.solved, (BLK - 1) * grp + c - 1)
            nc.vector.tensor_tensor(prod[:, :, 0:c, 0:c], tsys[:, :, 0:c, 0:c],
                                    asys[:, :, 0:c, c].unsqueeze(2).broadcast_to([2 * SYS, 2, c, c]),
                                    ALU.mult).then_inc(s.prod, 1)
            dve.wait_ge(s.prod, (BLK - 1) * grp + c)
            nc.vector.tensor_reduce(tsys[:, :, 0:c, c], prod[:, :, 0:c, 0:c], AX.X, ALU.add)\
                .then_inc(s.solved, 1)


def gdn_output(nc, k, t, grp, s, ctx):
    rq = sb(nc, ctx, "go_rq", [PT, PAIRS, GV])
    rq2 = sb(nc, ctx, "go_rq2", [PT, PAIRS, GV])
    y = sb(nc, ctx, "go_y", [PT, 3, 512])
    d = sb(nc, ctx, "go_d", [PT, 2, 512])
    r = sb(nc, ctx, "go_r", [PT, 512])
    w = sb(nc, ctx, "go_w", [PT, 512])
    osq = sb(nc, ctx, "go_osq", [PT, 512])
    ssq = sb(nc, ctx, "go_ssq", [PT, 4])
    mean = sb(nc, ctx, "go_mean", [PT, 4])
    eps = sb(nc, ctx, "go_eps", [PT, 4])
    root = sb(nc, ctx, "go_root", [PT, 4])
    fac = sb(nc, ctx, "go_fac", [PT, 4])
    og = sb(nc, ctx, "go_og", [PT, 512])
    ogn = sb(nc, ctx, "go_ogn", [PT, 512])
    ogT = sb(nc, ctx, "go_ogT", [128, 2, 4 * PT])
    ps = pb(nc, ctx, "go_ps", 8)
    Y, R, W, O, T, OUT = (0, 1), (2, 3), 4, 5, 6, 7
    block = ctx.enter_context(nc.Block())

    def unit(u):
        return u // 2, u % 2, (u // 2) * GV + (u % 2) * 4

    def upto(u):
        return grp * UNITS + u + 1

    def quad(x):
        return x.rearrange("q (v n) -> q v n", v=4)

    @block.tensor
    def _(pe):
        pe.wait_ge(s.wo_in, 16 * grp + 16)
        for i in range(UNITS + 6):
            u = i
            if u < UNITS:
                p, q, m = unit(u)
                if u >= 2:
                    pe.wait_ge(s.y_ready, upto(u - 2))
                    pe.wait_ge(s.d_ready, upto(u - 2))
                for v in range(4):
                    last = nc.tensor.matmul(ps[0:PT, Y[u % 2], v * 128:(v + 1) * 128], k.tt[:, m + v, :],
                                            k.v[:, q * 4 + v, p, :], start=True, stop=True)
                last.then_inc(s.y, 1)
            u = i - 1
            if 0 <= u < UNITS:
                p, q, m = unit(u)
                pe.wait_ge(s.y_ready, upto(u))
                if u >= 2:
                    pe.wait_ge(s.r_ready, upto(u - 2))
                for v in range(4):
                    last = nc.tensor.matmul(ps[0:PT, R[u % 2], v * 128:(v + 1) * 128], k.apt[:, 0, m + v, :],
                                            y[:, u % 3, v * 128:(v + 1) * 128], start=True, stop=True)
                last.then_inc(s.r, 1)
            u = i - 2
            if 0 <= u < UNITS:
                p, q, m = unit(u)
                pe.wait_ge(s.r_ready, upto(u))
                pe.wait_ge(s.w_ready, upto(u - 1))
                for v in range(4):
                    last = nc.tensor.matmul(ps[0:PT, W, v * 128:(v + 1) * 128], k.tt[:, m + v, :],
                                            r[:, v * 128:(v + 1) * 128], start=True, stop=True)
                last.then_inc(s.w, 1)
            u = i - 3
            if 0 <= u < UNITS:
                p, q, m = unit(u)
                pe.wait_ge(s.w_ready, upto(u))
                pe.wait_ge(s.og, upto(u - 1))
                pe.wait_ge(s.osq, upto(u - 1))
                for v in range(4):
                    last = nc.tensor.matmul(ps[0:PT, O, v * 128:(v + 1) * 128], k.apt[:, 1, m + v, :],
                                            w[:, v * 128:(v + 1) * 128], start=True, stop=True)
                last.then_inc(s.o, 1)
            u = i - 5
            if 0 <= u < UNITS:
                pe.wait_ge(s.ogn, upto(u))
                pe.wait_ge(s.ogT, upto(u - 1))
                for v in range(4):
                    last = nc.tensor.transpose(ps[:, T, v * PT:(v + 1) * PT], ogn[:, v * 128:(v + 1) * 128],
                                               k.ident[0:PT, 0:PT])
                last.then_inc(s.turned, 1)
            u = i - 6
            if 0 <= u < UNITS:
                p, q, m = unit(u)
                pe.wait_ge(s.ogT, upto(u))
                if q == 0:
                    pe.wait_ge(s.added, grp * PAIRS + p)
                for v in range(4):
                    last = nc.tensor.matmul(ps[0:PT, OUT, 0:HID], ogT[:, u % 2, v * PT:(v + 1) * PT],
                                            k.wo[:, q * 4 + v, :], start=(q == 0 and v == 0),
                                            stop=(q == 1 and v == 3))
                last.then_inc(s.out, 1)

    @block.scalar
    def _(act):
        for i in range(UNITS + 6):
            u = i
            if u < UNITS:
                act.wait_ge(s.y, upto(u))
                if u >= 3:
                    act.wait_ge(s.w_ready, upto(u - 3))
                nc.scalar.copy(y[:, u % 3, :], ps[0:PT, Y[u % 2], :]).then_inc(s.y_ready, 1)
            u = i - 3
            if 0 <= u < UNITS:
                act.wait_ge(s.o, upto(u))
                act.wait_ge(s.ssq_o, upto(u - 1))
                nc.scalar.square(osq[:], ps[0:PT, O, :]).then_inc(s.osq, 1)
            u = i - 5
            if 0 <= u < UNITS:
                act.wait_ge(s.turned, upto(u))
                if u >= 2:
                    act.wait_ge(s.out, upto(u - 2))
                nc.scalar.copy(ogT[:, u % 2, :], ps[:, T, 0:4 * PT]).then_inc(s.ogT, 1)

    @block.vector
    def _(dve):
        nc.vector.tensor_copy(rq[:].rearrange("q p (h e) -> q p h e", e=VPK),
                              k.rnq[:].rearrange("q h p -> q p h").unsqueeze(3)
                              .broadcast_to([PT, PAIRS, GK, VPK])).then_inc(s.rq, 1)
        dve.wait_ge(s.rq, 2 * grp + 1)
        nc.vector.scalar_tensor_tensor(out=rq2[:], in0=rq[:], scalar=1.0 / 128, in1=rq[:],
                                       op0=ALU.mult, op1=ALU.mult).then_inc(s.rq, 1)
        for i in range(UNITS + 6):
            u = i
            if u < UNITS:
                p, q, m = unit(u)
                dve.wait_ge(s.y_ready, upto(u))
                if u >= 2:
                    dve.wait_ge(s.r_ready, upto(u - 2))
                nc.vector.tensor_tensor(quad(d[:, u % 2, :]), k.v[:, q * 4:q * 4 + 4, p, :], quad(ps[0:PT, Y[u % 2], :]),
                                        ALU.subtract).then_inc(s.d_ready, 1)
            u = i - 1
            if 0 <= u < UNITS:
                dve.wait_ge(s.r, upto(u))
                dve.wait_ge(s.d_ready, upto(u))
                dve.wait_ge(s.w, upto(u - 1))
                nc.vector.tensor_tensor(r[:], ps[0:PT, R[u % 2], :], d[:, u % 2, :], ALU.add).then_inc(s.r_ready, 1)
            u = i - 2
            if 0 <= u < UNITS:
                dve.wait_ge(s.w, upto(u))
                dve.wait_ge(s.o, upto(u - 1))
                nc.vector.tensor_tensor(w[:], ps[0:PT, W, :], y[:, u % 3, :], ALU.add).then_inc(s.w_ready, 1)
            u = i - 3
            if 0 <= u < UNITS:
                dve.wait_ge(s.osq, upto(u))
                dve.wait_ge(s.mean, upto(u - 1))
                nc.vector.tensor_reduce(ssq[:], quad(osq[:]), AX.X, ALU.add).then_inc(s.ssq_o, 1)
                dve.wait_ge(s.ogn, upto(u - 1))
                nc.vector.tensor_tensor(og[:], ps[0:PT, O, :], k.gate[:, u, :], ALU.mult).then_inc(s.og, 1)
            u = i - 6
            if 0 <= u < UNITS and u % 2:
                p = u // 2
                dve.wait_ge(s.out, upto(u))
                nc.vector.tensor_tensor(k.x[:, p, :], k.x[:, p, :], ps[0:PT, OUT, 0:HID], ALU.add)\
                    .then_inc(s.added, 1)

    @block.gpsimd
    def _(pool):
        pool.wait_ge(s.rq, 2 * grp + 2)
        for i in range(UNITS + 6):
            u = i - 3
            if 0 <= u < UNITS:
                p, q, m = unit(u)
                pool.wait_ge(s.ssq_o, upto(u))
                nc.gpsimd.tensor_tensor(mean[:], ssq[:], rq2[:, p, q * 4:q * 4 + 4], ALU.mult).then_inc(s.mean, 1)
                pool.wait_ge(s.mean, upto(u))
                nc.gpsimd.tensor_tensor(eps[:], mean[:], k.eps6[0:PT, 0:4], ALU.add).then_inc(s.eps, 1)
                pool.wait_ge(s.eps, upto(u))
                nc.gpsimd.tensor_tensor(root[:], eps[:], k.minus_half[0:PT, 0:4], ALU.pow).then_inc(s.root, 1)
                pool.wait_ge(s.root, upto(u))
                nc.gpsimd.tensor_tensor(fac[:], root[:], rq[:, p, q * 4:q * 4 + 4], ALU.mult).then_inc(s.fac, 1)
                pool.wait_ge(s.fac, upto(u))
                pool.wait_ge(s.og, upto(u))
                pool.wait_ge(s.turned, upto(u - 1))
                nc.gpsimd.tensor_tensor(quad(ogn[:]), quad(og[:]), fac[:].unsqueeze(2).broadcast_to([PT, 4, 128]),
                                        ALU.mult).then_inc(s.ogn, 1)


def gated_delta_rule(nc, k, t):
    with ExitStack() as ctx:
        k.beta = sb(nc, ctx, "beta", [PT, PAIRS, NV])
        k.logdecay = sb(nc, ctx, "logdecay", [PT, PAIRS, NV])
        k.after = sb(nc, ctx, "after", [PT, PT])
        k.upto = sb(nc, ctx, "upto", [PT, PT])
        k.kqmask = sb(nc, ctx, "kqmask", [PT, 2 * PT])
        k.normw = sb(nc, ctx, "normw", [PT, 128])
        gdn_gates(nc, k, t)
        k.v = sb(nc, ctx, "values", [PT, GV, PAIRS, 128])
        k.gmtt = sb(nc, ctx, "gmtt", [PT, GK * PAIRS * 2 * PT])
        k.tt = k.gmtt[:].rearrange("q (m w) -> q m w", w=PT)
        k.apt = sb(nc, ctx, "apt", [PT, 2, SYS, PT])
        k.rnk2 = sb(nc, ctx, "rnk2", [PT, GK, PAIRS])
        k.rnq = sb(nc, ctx, "rnq", [PT, GK, PAIRS])
        k.scratch_a = nc.dram_tensor("scratch_a", [2, 2, SYS, BLK, BLK], F32, kind="Internal").ap()
        k.scratch_t = nc.dram_tensor("scratch_t", [2, 2, SYS, BLK, BLK], F32, kind="Internal").ap()
        s = sems(nc, ctx, "gdn", "evac projected squared v_done ssq gm_done kq_done conv_done nsq_ready "
                 "conv_step padded roots rnk2 lead a_out a_in solved t_out t_in t_zero zeroed prod "
                 "wz_in wo_in silu z y_ready d_ready y r r_ready w w_ready o og osq ogn ogT turned out added "
                 "gate ssq_o mean eps root fac rq", pairs="w_in v_turned emm u_ready dec_ready apt")
        with nc.Fori(0, GROUPS) as grp:
            for part in (gdn_project, gdn_systems):
                with ExitStack() as inner:
                    part(nc, k, t, grp, s, inner)
            with ExitStack() as both:
                k.gate = sb(nc, both, "gates", [PT, UNITS, 512])
                k.wo = sb(nc, both, "gdn_wo", [128, GV, HID])
                for part in (gdn_solve, gdn_output):
                    with ExitStack() as inner:
                        part(nc, k, t, grp, s, inner)


def context_projections(nc, k, t):
    with ExitStack() as ctx:
        wq = sb(nc, ctx, "cp_wq", [128, CC, HID])
        wk = sb(nc, ctx, "cp_wk", [128, CC, HID])
        wv = sb(nc, ctx, "cp_wv", [128, CC, HID])
        layernorm(nc, k, "ln1", [(wq[:], t["c_wq"]), (wk[:], t["c_wk"]), (wv[:], t["c_wv"])])
        ps = pb(nc, ctx, "cp_ps", 8)
        s = sems(nc, ctx, "cp", "product even odd")
        block = ctx.enter_context(nc.Block())

        @block.tensor
        def _(pe):
            for n in range(16):
                if n >= 8:
                    pe.wait_ge((s.even, s.odd)[n % 2], (n - 8) // 2 + 1)
                if n < 8:
                    w, f, half = (wq, wk)[n // 4], n // 2 % 2, n % 2
                    for c in range(CC):
                        last = nc.tensor.matmul(ps[:, n, 0:HALF], w[:, c, f * 128:(f + 1) * 128],
                                                k.xnT[:, c, half * HALF:(half + 1) * HALF],
                                                start=(c == 0), stop=(c == CC - 1))
                else:
                    for e in range(2):
                        b = 2 * (n - 8) + e
                        for c in range(CC):
                            last = nc.tensor.matmul(ps[0:SEQ, n % 8, e * HID:(e + 1) * HID],
                                                    k.xnT[:, c, b * SEQ:(b + 1) * SEQ], wv[:, c, :],
                                                    start=(c == 0), stop=(c == CC - 1))
                last.then_inc(s.product, 1)

        def evacuate(eng, n, copy, scaled):
            eng.wait_ge(s.product, n + 1)
            done = (s.even, s.odd)[n % 2]
            if n < 8:
                dst = (k.qT, k.knT)[n // 4][:, n // 2 % 2, n % 2 * HALF:(n % 2 + 1) * HALF]
                if n < 4:
                    scaled(dst, ps[:, n, 0:HALF], 1 / 16).then_inc(done, 1)
                else:
                    copy(dst, ps[:, n, 0:HALF]).then_inc(done, 1)
            else:
                copy(k.vnew[:, 2 * (n - 8):2 * (n - 8) + 2, :].rearrange("q b d -> q (b d)"),
                     ps[0:SEQ, n % 8, :]).then_inc(done, 1)

        @block.scalar
        def _(act):
            for n in range(0, 16, 2):
                evacuate(act, n, nc.scalar.copy, nc.scalar.mul)

        @block.vector
        def _(dve):
            for n in range(1, 16, 2):
                evacuate(dve, n, nc.vector.tensor_copy, nc.vector.tensor_scalar_mul)


def context_softmax(nc, k, t):
    SLOTS = 4
    TURNS = BATCH // SLOTS
    KEYS = CTX + SEQ
    SPAN = KEYS // 4
    NT = NKT + 1
    LOW = 7
    with ExitStack() as ctx:
        kv = sb(nc, ctx, "cs_kv", [KT, SLOTS, NKT, HID])
        kvT = sb(nc, ctx, "cs_kvT", [128, 2, CC, CTX])
        qslot = sb(nc, ctx, "cs_qslot", [128, 2, CC, SEQ])
        vslot = sb(nc, ctx, "cs_vslot", [SEQ, 2, HID])
        prob = sb(nc, ctx, "cs_prob", [SEQ, KEYS])
        probn = sb(nc, ctx, "cs_probn", [SEQ, KEYS])
        pT = sb(nc, ctx, "cs_pT", [KT, NT, SEQ])
        negmax = sb(nc, ctx, "cs_negmax", [SEQ, 1])
        total = sb(nc, ctx, "cs_total", [SEQ, 1])
        rtotal = sb(nc, ctx, "cs_rtotal", [SEQ, 1])
        ps_s = pb(nc, ctx, "cs_ps_s", 4)
        ps_t = pb(nc, ctx, "cs_ps_t", 2)
        ps_o = pb(nc, ctx, "cs_ps_o", 1)
        s = sems(nc, ctx, "cs", "scored negmax exped rtotal probn stored q_staged v_staged wo_in")
        ctx_in = [sem(nc, ctx, f"cs_ctx_in{j}") for j in range(SLOTS)]
        pv_done = [sem(nc, ctx, f"cs_pv_done{j}") for j in range(SLOTS)]
        turned = [sem(nc, ctx, f"cs_turned{j}") for j in range(2)]
        copied = [sem(nc, ctx, f"cs_copied{j}") for j in range(2)]
        block = ctx.enter_context(nc.Block())
        ROUNDS = NKT // 4

        def uses(b):
            return ROUNDS if isinstance(b, int) and b == 0 else (ROUNDS + 1) * b + ROUNDS - 1

        def steps(body, eng):
            for j in range(SLOTS):
                body(0, j, j == 0, False)
            with eng.Fori(0, TURNS - 2) as it:
                for j in range(SLOTS):
                    body(it + 1, j, False, False)
            for j in range(SLOTS):
                body(TURNS - 1, j, False, j == SLOTS - 1)

        @block.sync
        def _(sp):
            sp.dma_start(k.wo[:], t["c_wo"]).then_inc(s.wo_in, 16)
            sp.wait_ge(s.wo_in, 16)
            with sp.Fori(0, TURNS) as it:
                for j in range(SLOTS):
                    sp.wait_ge(pv_done[j], it)
                    sp.dma_start(kv[:, j], t["context"][it * SLOTS + j].rearrange("(i q) d -> q i d", q=KT))\
                        .then_inc(ctx_in[j], 16)

        @block.tensor
        def _(pe):
            def turn_context(it, j, use, rounds):
                for r in rounds:
                    if r == 0:
                        pe.wait_ge(ctx_in[j], 16 * it + 16)
                    c, quad = r % 2, r // 2
                    pe.wait_ge(copied[c], use + quad)
                    for e in range(4):
                        last = nc.tensor.transpose(ps_t[:, c, e * KT:(e + 1) * KT],
                                                   kv[:, j, quad * 4 + e, c * 128:(c + 1) * 128],
                                                   k.ident[0:KT, 0:KT])
                    last.then_inc(turned[c], 1)

            def scores(b, j, spans):
                for i in spans:
                    lo, hi = i * SPAN, min((i + 1) * SPAN, CTX)
                    for c in range(CC):
                        nc.tensor.matmul(ps_s[0:SEQ, i, 0:hi - lo], qslot[:, j % 2, c, :],
                                         kvT[:, j % 2, c, lo:hi], start=(c == 0), stop=(c == CC - 1))
                if 3 in spans:
                    for c in range(CC):
                        last = nc.tensor.matmul(ps_s[0:SEQ, 3, SPAN - SEQ:SPAN], qslot[:, j % 2, c, :],
                                                k.knT[:, c, bass.ts(b, SEQ)], start=(c == 0), stop=(c == CC - 1))
                    last.then_inc(s.scored, 1)

            def turn_probs(b, use):
                pe.wait_ge(s.probn, b + 1)
                for bank in range(2):
                    pe.wait_ge(copied[bank], use)
                nc.tensor.nop(nofuse=True)
                for bank, tiles in ((0, range(LOW)), (1, range(LOW, NT))):
                    for i in tiles:
                        n = KT if i < NKT else SEQ
                        last = nc.tensor.transpose(ps_t[0:n, bank, (i - tiles[0]) * SEQ:(i - tiles[0] + 1) * SEQ],
                                                   probn[:, i * KT:i * KT + n], k.ident[0:SEQ, 0:SEQ])
                    last.then_inc(turned[bank], 1)

            def values(b, j, use, d):
                if d == 0:
                    for bank in range(2):
                        pe.wait_ge(copied[bank], use)
                    pe.wait_ge(s.stored, b)
                    pe.wait_ge(s.v_staged, b + 1)
                for i in range(NT):
                    n = KT if i < NKT else SEQ
                    v = kv[:, j, i, d * 128:(d + 1) * 128] if i < NKT else vslot[:, j % 2, d * 128:(d + 1) * 128]
                    last = nc.tensor.matmul(ps_o[:, 0, d * SEQ:(d + 1) * SEQ], v, pT[0:n, i, :],
                                            start=(i == 0), stop=(i == NT - 1))
                if d == CC - 1:
                    last.then_inc(pv_done[j], 1)

            def step(it, j, first, last_one):
                b = it * SLOTS + j
                use = uses(b)
                slot, nit, nslot = (j - 1) % SLOTS, it + (j + 1) // SLOTS, (j + 1) % SLOTS
                for c in range(2):
                    pe.wait_ge(copied[c], use - 1)
                pe.wait_ge(s.q_staged, b + 1)
                pe.wait_ge(s.exped, b)
                scores(b, j, (0, 1))
                if not first:
                    turn_probs(b - 1, use)
                for c in range(2):
                    pe.wait_ge(copied[c], use)
                scores(b, j, (2, 3))
                if not first:
                    use = use + 1
                    values(b - 1, slot, use, 0)
                if not last_one:
                    turn_context(nit, nslot, use, (0, 1))
                if not first:
                    values(b - 1, slot, use, 1)
                if not last_one:
                    turn_context(nit, nslot, use, range(2, 2 * ROUNDS))

            turn_context(0, 0, 0, range(2 * ROUNDS))
            steps(step, pe)
            use = uses(BATCH) - ROUNDS
            turn_probs(BATCH - 1, use)
            for d in range(CC):
                values(BATCH - 1, SLOTS - 1, use + 1, d)

        def copy_context(eng, copy, rounds, slot, use):
            for r in rounds:
                bank, quad = r % 2, r // 2
                eng.wait_ge(turned[bank], use + quad + 1)
                copy(kvT[:, slot, bank, quad * 500:(quad + 1) * 500], ps_t[:, bank, 0:500])\
                    .then_inc(copied[bank], 1)

        @block.scalar
        def _(act):
            def copy_probs(use):
                act.wait_ge(turned[0], use + 1)
                nc.scalar.copy(pT[:, 0:LOW, :], ps_t[0:KT, 0, 0:LOW * SEQ].rearrange("q (i n) -> q i n", n=SEQ))\
                    .then_inc(copied[0], 1)
                act.wait_ge(turned[1], use + 1)
                nc.scalar.copy(pT[:, LOW:NKT, :], ps_t[0:KT, 1, 0:(NKT - LOW) * SEQ]
                               .rearrange("q (i n) -> q i n", n=SEQ))
                nc.scalar.copy(pT[0:SEQ, NKT, :], ps_t[0:SEQ, 1, (NKT - LOW) * SEQ:(NT - LOW) * SEQ])\
                    .then_inc(copied[1], 1)

            def step(it, j, first, last_one):
                b = it * SLOTS + j
                use = uses(b)
                if not first:
                    copy_probs(use)
                    use = use + 1
                act.wait_ge(s.negmax, b + 1)
                nc.scalar.activation(prob[:].rearrange("q (i n) -> q i n", i=4), ps_s[0:SEQ, :, 0:SPAN], ACT.Exp,
                                     bias=negmax[:], accum_out=total[:]).then_inc(s.exped, 1)
                if not last_one:
                    copy_context(act, nc.scalar.copy, (2, 3, 5), (j + 1) % 2, use)

            copy_context(act, nc.scalar.copy, (0, 2, 4), 0, 0)
            steps(step, act)
            copy_probs(uses(BATCH) - ROUNDS)

        @block.vector
        def _(dve):
            def store(b, j, count):
                dve.wait_ge(pv_done[j], count)
                nc.vector.tensor_copy(k.oT[:, :, bass.ts(b, SEQ)],
                                      ps_o[:, 0, 0:CC * SEQ].rearrange("d (c n) -> d c n", c=CC)).then_inc(s.stored, 1)

            def step(it, j, first, last_one):
                b = it * SLOTS + j
                use = uses(b)
                dve.wait_ge(s.scored, b + 1)
                nc.vector.tensor_reduce(negmax[:], ps_s[0:SEQ, :, 0:SPAN], AX.XY, ALU.max, negate=True)\
                    .then_inc(s.negmax, 1)
                after = use if first else use + 1
                if not last_one:
                    copy_context(dve, nc.vector.tensor_copy, (0, 1), (j + 1) % 2, after)
                dve.wait_ge(s.exped, b + 1)
                nc.vector.reciprocal(rtotal[:], total[:]).then_inc(s.rtotal, 1)
                dve.wait_ge(s.rtotal, b + 1)
                if not first:
                    dve.wait_ge(turned[1], use + 1)
                nc.vector.tensor_scalar_mul(probn[:], prob[:], rtotal[:]).then_inc(s.probn, 1)
                if not first:
                    store(b - 1, (j - 1) % SLOTS, it + (1 if j else 0))
                if not last_one:
                    copy_context(dve, nc.vector.tensor_copy, (4,), (j + 1) % 2, after)

            copy_context(dve, nc.vector.tensor_copy, (1, 3, 5), 0, 0)
            steps(step, dve)
            store(BATCH - 1, SLOTS - 1, TURNS)

        @block.gpsimd
        def _(pool):
            def queries(b, j, used):
                if used:
                    pool.wait_ge(s.scored, b - 1)
                nc.gpsimd.tensor_copy(qslot[:, j % 2], k.qT[:, :, bass.ts(b, SEQ)]).then_inc(s.q_staged, 1)

            def values(b, j, count):
                if count is not None:
                    pool.wait_ge(pv_done[(j - 2) % SLOTS], count)
                nc.gpsimd.tensor_copy(vslot[:, j % 2, :], k.vnew[:, b, :]).then_inc(s.v_staged, 1)

            for b in range(SLOTS):
                queries(b, b, b >= 2)
                values(b, b, 1 if b >= 2 else None)
            with pool.Fori(0, TURNS - 1) as it:
                for j in range(SLOTS):
                    b = (it + 1) * SLOTS + j
                    queries(b, j, True)
                    values(b, j, it + (2 if j >= 2 else 1))


def add_projection(nc, k, tag, w, srcT, chunks, bias=None):
    with ExitStack() as ctx:
        ps = pb(nc, ctx, f"{tag}_ps", 8)
        s = sems(nc, ctx, tag, "product biased added")
        block = ctx.enter_context(nc.Block())

        @block.tensor
        def _(pe):
            for p in range(PAIRS):
                for c in range(chunks):
                    last = nc.tensor.matmul(ps[0:PT, p, 0:HID], srcT[:, c, p * PT:(p + 1) * PT], w[:, c, :],
                                            start=(c == 0), stop=(c == chunks - 1))
                last.then_inc(s.product, 1)

        @block.vector
        def _(dve):
            if bias is not None:
                nc.vector.tensor_tensor(k.x[:], k.x[:], bias.unsqueeze(1).broadcast_to([PT, PAIRS, HID]),
                                        ALU.add).then_inc(s.biased, 1)
                dve.wait_ge(s.biased, 1)
            for p in range(PAIRS):
                dve.wait_ge(s.product, p + 1)
                nc.vector.tensor_tensor(k.x[:, p, :], k.x[:, p, :], ps[0:PT, p, 0:HID], ALU.add)\
                    .then_inc(s.added, 1)


def context_attention(nc, k, t):
    with ExitStack() as ctx:
        k.qT = sb(nc, ctx, "ca_qT", [128, CC, TOK])
        k.knT = sb(nc, ctx, "ca_knT", [128, CC, TOK])
        k.vnew = sb(nc, ctx, "ca_vnew", [SEQ, BATCH, HID])
        k.oT = sb(nc, ctx, "ca_oT", [128, CC, TOK])
        k.wo = sb(nc, ctx, "ca_wo", [128, CC, HID])
        context_projections(nc, k, t)
        context_softmax(nc, k, t)
        add_projection(nc, k, "ca_out", k.wo, k.oT, CC)


def route(nc, k, tag, norm_tag, weight, bias, experts=8, loads=(), awaited=None,
          pool_work=None, act_work=None):
    N = PAIRS * experts
    with ExitStack() as ctx:
        w = sb(nc, ctx, f"{tag}_w", [128, CC, experts])
        earlier = sb(nc, ctx, f"{tag}_earlier", [PT, experts * experts])
        brow = sb(nc, ctx, f"{tag}_brow", [PT, experts]) if bias is not None else None
        logit = sb(nc, ctx, f"{tag}_logit", [PT, PAIRS, experts])
        top = sb(nc, ctx, f"{tag}_top", [PT, PAIRS])
        shifted = sb(nc, ctx, f"{tag}_shifted", [PT, PAIRS, experts])
        ex = sb(nc, ctx, f"{tag}_ex", [PT, PAIRS, experts])
        total = sb(nc, ctx, f"{tag}_total", [PT, PAIRS])
        rtotal = sb(nc, ctx, f"{tag}_rtotal", [PT, PAIRS])
        more = sb(nc, ctx, f"{tag}_more", [PT, N, experts])
        same = sb(nc, ctx, f"{tag}_same", [PT, N, experts])
        tie = sb(nc, ctx, f"{tag}_tie", [PT, N, experts])
        before = sb(nc, ctx, f"{tag}_before", [PT, N, experts])
        operands = [(w[:], weight), (earlier[:], k.t["earlier"])]
        if bias is not None:
            operands.append((brow[:], bias))
        layernorm(nc, k, norm_tag, operands)
        ps = pb(nc, ctx, f"{tag}_ps", 1)
        s = sems(nc, ctx, tag, "product ex chain")
        block = ctx.enter_context(nc.Block())
        over_j = lambda x: x[:].unsqueeze(3).broadcast_to([PT, PAIRS, experts, experts])
        over_e = lambda x: x[:].unsqueeze(2).broadcast_to([PT, PAIRS, experts, experts])
        cube = lambda x: x[:].rearrange("q (p e) j -> q p e j", p=PAIRS)

        @block.sync
        def _(sp):
            for dst, src, loaded in loads:
                sp.dma_start(dst, src).then_inc(loaded, 16)
            if awaited is not None:
                sp.wait_ge(*awaited)

        if pool_work is not None:
            block.gpsimd(pool_work)

        @block.tensor
        def _(pe):
            for p in range(PAIRS):
                for c in range(CC):
                    last = nc.tensor.matmul(ps[0:PT, 0, p * experts:(p + 1) * experts],
                                            k.xnT[:, c, p * PT:(p + 1) * PT], w[:, c, :],
                                            start=(c == 0), stop=(c == CC - 1))
            last.then_inc(s.product, 1)

        @block.scalar
        def _(act):
            if act_work is not None:
                act_work(act)
            act.wait_ge(s.chain, 3)
            nc.scalar.activation(ex[:], shifted[:], ACT.Exp).then_inc(s.ex, 1)

        @block.vector
        def _(dve):
            count = [0]

            def wait_all():
                dve.wait_ge(s.chain, count[0])

            def step(ins):
                ins.then_inc(s.chain, 1)
                count[0] += 1

            dve.wait_ge(s.product, 1)
            raw = ps[0:PT, 0, 0:N].rearrange("q (p e) -> q p e", p=PAIRS)
            if bias is None:
                step(nc.vector.tensor_copy(logit[:], raw))
            else:
                step(nc.vector.tensor_tensor(logit[:], raw, brow[:].unsqueeze(1)
                                             .broadcast_to([PT, PAIRS, experts]), ALU.add))
            wait_all()
            step(nc.vector.tensor_reduce(top[:], logit[:], AX.X, ALU.max))
            wait_all()
            step(nc.vector.tensor_tensor(shifted[:], logit[:], top[:].unsqueeze(2)
                                         .broadcast_to([PT, PAIRS, experts]), ALU.subtract))
            dve.wait_ge(s.ex, 1)
            step(nc.vector.tensor_reduce(total[:], ex[:], AX.X, ALU.add))
            wait_all()
            step(nc.vector.reciprocal(rtotal[:], total[:]))
            wait_all()
            step(nc.vector.tensor_tensor(k.prob[:], ex[:], rtotal[:].unsqueeze(2)
                                         .broadcast_to([PT, PAIRS, experts]), ALU.mult))
            wait_all()
            step(nc.vector.tensor_tensor(cube(more), over_e(k.prob), over_j(k.prob), ALU.is_gt))
            step(nc.vector.tensor_tensor(cube(same), over_e(k.prob), over_j(k.prob), ALU.is_equal))
            wait_all()
            step(nc.vector.tensor_tensor(cube(tie), cube(same), earlier[:]
                                         .rearrange("q (e j) -> q e j", e=experts).unsqueeze(1)
                                         .broadcast_to([PT, PAIRS, experts, experts]), ALU.mult))
            wait_all()
            step(nc.vector.tensor_tensor(before[:], more[:], tie[:], ALU.add))
            wait_all()
            step(nc.vector.tensor_reduce(k.rank[:].rearrange("q p e -> q (p e)"), before[:], AX.X, ALU.add))


def expert_weights(nc, k):
    with ExitStack() as ctx:
        picked = sb(nc, ctx, "ew_picked", [PT, PAIRS, E0])
        total = sb(nc, ctx, "ew_total", [PT, PAIRS])
        rtotal = sb(nc, ctx, "ew_rtotal", [PT, PAIRS])
        s = sems(nc, ctx, "ew", "picked total rtotal done")
        block = ctx.enter_context(nc.Block())

        @block.vector
        def _(dve):
            nc.vector.scalar_tensor_tensor(out=picked[:], in0=k.rank[:], scalar=1.5, in1=k.prob[:],
                                           op0=ALU.is_lt, op1=ALU.mult).then_inc(s.picked, 1)
            dve.wait_ge(s.picked, 1)
            nc.vector.tensor_reduce(total[:], picked[:], AX.X, ALU.add).then_inc(s.total, 1)
            dve.wait_ge(s.total, 1)
            nc.vector.reciprocal(rtotal[:], total[:]).then_inc(s.rtotal, 1)
            dve.wait_ge(s.rtotal, 1)
            nc.vector.tensor_tensor(k.wfull[:], picked[:], rtotal[:].unsqueeze(2)
                                    .broadcast_to([PT, PAIRS, E0]), ALU.mult).then_inc(s.done, 1)


def swiglu_split(nc, k, s, pool, e, j, step):
    SPLITS = 4
    cols = (slice(0, 2 * CC * F0), slice(2 * CC * F0, None))[step // 2]
    if step == 0:
        pool.wait_ge(s.raw_in, 16 * e + 16)
    high, low = k.ws[:, j, 0, cols], k.ws[:, j, 1, cols]
    if step % 2 == 0:
        nc.gpsimd.tensor_tensor(high, k.raw[:, cols], k.ones[:, 0:1].broadcast_to([128, high.shape[1]]),
                                ALU.mult).then_inc(s.split, 1)
    else:
        pool.wait_ge(s.split, SPLITS * e + step)
        nc.gpsimd.tensor_tensor(low, k.raw[:, cols], high, ALU.subtract).then_inc(s.split, 1)


def swiglu_experts(nc, k, t, s):
    FT = F0 // 128
    W13 = CC * F0
    with ExitStack() as ctx:
        gate = sb(nc, ctx, "sw_gate", [128, 2, HALF])
        hid = sb(nc, ctx, "sw_hid", [128, 2, HALF])
        hs = sb(nc, ctx, "sw_hs", [128, 2, 2, FT, TOK], F32R)
        up = pb(nc, ctx, "sw_up", 4)
        down = pb(nc, ctx, "sw_down", 4)
        block = ctx.enter_context(nc.Block())
        w13 = [[[k.ws[:, j, a, m * W13:(m + 1) * W13].rearrange("c (k n) -> c k n", k=CC) for m in range(2)]
                for a in range(2)] for j in range(2)]
        w2 = [[k.ws[:, j, a, 2 * W13:].rearrange("c (k n) -> c k n", k=FT) for a in range(2)] for j in range(2)]
        Q = 2 * FT
        SPLITS = 4

        def tile(x, q):
            return x[:, q % FT, (q // FT) * HALF:(q // FT + 1) * HALF]

        @block.sync
        def _(sp):
            for e in range(1, E0):
                sp.wait_ge(s.split, SPLITS * e)
                sp.dma_start(k.raw[:], t["s_w"][e]).then_inc(s.raw_in, 16)

        @block.tensor
        def _(pe):
            with pe.Fori(0, E0 // 2) as i:
                for j in range(2):
                    e = i * 2 + j
                    pe.wait_ge(s.split, SPLITS * e + 2)
                    for q in range(Q):
                        f, half = q % FT, q // FT
                        pe.wait_ge(s.hidden, Q * e + max(q - 1, 0))
                        for m in range(2):
                            terms = [(c, a, b) for c in range(CC) for a, b in SPLIT_TERMS]
                            for c, a, b in terms:
                                last = nc.tensor.matmul(up[:, (q % 2) * 2 + m, 0:HALF],
                                                        w13[j][a][m][:, c, f * 128:(f + 1) * 128],
                                                        k.xs[:, b, c, half * HALF:(half + 1) * HALF],
                                                        start=((c, a, b) == terms[0]), stop=((c, a, b) == terms[-1]))
                        last.then_inc(s.upped, 1)
                    pe.wait_ge(s.split, SPLITS * e + 4)
                    for p in range(PAIRS):
                        if p % HPAIRS == 0:
                            pe.wait_ge(s.high, Q * e + (p // HPAIRS + 1) * FT)
                            pe.wait_ge(s.low, Q * e + (p // HPAIRS + 1) * FT)
                        pe.wait_ge(s.added, PAIRS * e + max(p - 3, 0))
                        terms = [(f, a, b) for f in range(FT) for a, b in SPLIT_TERMS]
                        for f, a, b in terms:
                            last = nc.tensor.matmul(down[0:PT, p % 4, 0:HID], hs[:, j, a, f, p * PT:(p + 1) * PT],
                                                    w2[j][b][:, f, :], start=((f, a, b) == terms[0]),
                                                    stop=((f, a, b) == terms[-1]))
                        last.then_inc(s.used[j], 1)

        @block.scalar
        def _(act):
            with act.Fori(0, E0 // 2) as i:
                for j in range(2):
                    e = i * 2 + j
                    for q in range(Q + 1):
                        if q < Q:
                            act.wait_ge(s.upped, Q * e + q + 1)
                            act.wait_ge(s.hidden, Q * e + max(q - 1, 0))
                            nc.scalar.activation(gate[:, q % 2, :], up[:, (q % 2) * 2, 0:HALF], ACT.Silu)\
                                .then_inc(s.gated, 1)
                        if q == 1:
                            act.wait_ge(s.used[j], PAIRS * i)
                        if q:
                            act.wait_ge(s.hidden, Q * e + q)
                            nc.scalar.copy(tile(hs[:, j, 0], q - 1), hid[:, (q - 1) % 2, :]).then_inc(s.high, 1)

        @block.vector
        def _(dve):
            with dve.Fori(0, E0 // 2) as i:
                for j in range(2):
                    e = i * 2 + j
                    for q in range(Q + 1):
                        if q < Q:
                            dve.wait_ge(s.gated, Q * e + q + 1)
                            dve.wait_ge(s.high, Q * e + max(q - 1, 0))
                            dve.wait_ge(s.low, Q * e + max(q - 1, 0))
                            nc.vector.tensor_tensor(hid[:, q % 2, :], gate[:, q % 2, :],
                                                    up[:, (q % 2) * 2 + 1, 0:HALF], ALU.mult).then_inc(s.hidden, 1)
                        if q:
                            dve.wait_ge(s.high, Q * e + q)
                            nc.vector.tensor_tensor(tile(hs[:, j, 1], q - 1), hid[:, (q - 1) % 2, :],
                                                    tile(hs[:, j, 0], q - 1), ALU.subtract).then_inc(s.low, 1)
                    for p in range(PAIRS):
                        dve.wait_ge(s.used[j], PAIRS * i + p + 1)
                        nc.vector.scalar_tensor_tensor(out=k.x[:, p, :], in0=down[0:PT, p % 4, 0:HID],
                                                       scalar=k.wfull[:, p, bass.ds(e, 1)], in1=k.x[:, p, :],
                                                       op0=ALU.mult, op1=ALU.add).then_inc(s.added, 1)

        @block.gpsimd
        def _(pool):
            def turn(i, last):
                for j in range(2):
                    e = i * 2 + j
                    if not (last and j == 1):
                        pool.wait_ge(s.used[1 - j], PAIRS * (i + j))
                        for step in range(4):
                            swiglu_split(nc, k, s, pool, e + 1, 1 - j, step)

            with pool.Fori(0, E0 // 2 - 1) as i:
                turn(i, False)
            turn(E0 // 2 - 1, True)


def routed_swiglu(nc, k, t):
    with ExitStack() as ctx:
        k.t = t
        k.prob = sb(nc, ctx, "rs_prob", [PT, PAIRS, E0])
        k.rank = sb(nc, ctx, "rs_rank", [PT, PAIRS, E0])
        k.wfull = sb(nc, ctx, "rs_wfull", [PT, PAIRS, E0])
        W = 2 * CC * F0 + F0 // 128 * HID
        k.raw = sb(nc, ctx, "rs_raw", [128, W])
        k.ws = sb(nc, ctx, "rs_ws", [128, 2, 2, W], F32R)
        k.xs = sb(nc, ctx, "rs_xs", [128, 2, CC, TOK], F32R)
        s = sems(nc, ctx, "sw", "raw_in split first_high x_split upped gated hidden high low added", pairs="used")

        W13 = 2 * CC * F0
        first = ((k.xs[:, 0], k.xs[:, 1], k.xnT[:]), (k.ws[:, 0, 0, 0:W13], k.ws[:, 0, 1, 0:W13], k.raw[:, 0:W13]),
                 (k.ws[:, 0, 0, W13:], k.ws[:, 0, 1, W13:], k.raw[:, W13:]))

        def high_parts(act):
            for high, low, src in first:
                if src is first[1][2]:
                    act.wait_ge(s.raw_in, 16)
                nc.scalar.copy(high, src).then_inc(s.first_high, 1)

        def low_parts(pool):
            for n, (high, low, src) in enumerate(first):
                pool.wait_ge(s.first_high, n + 1)
                done, by = (s.x_split, 1) if n == 0 else (s.split, 2)
                nc.gpsimd.tensor_tensor(low, src, high, ALU.subtract).then_inc(done, by)
            pool.wait_ge(s.x_split, 1)

        route(nc, k, "r0", "ln2", t["r0_w"], None, loads=[(k.raw[:], t["s_w"][0], s.raw_in)],
              pool_work=low_parts, act_work=high_parts)
        expert_weights(nc, k)
        swiglu_experts(nc, k, t, s)


def feature_products(nc, k, t):
    NH = PAIRS * QKH
    MAGIC = 1.5 * 2.0 ** 23
    PI = float(np.float32(np.pi))
    TWO_PI_HI = 6.28125
    TWO_PI_LO = 2 * np.pi - TWO_PI_HI
    with ExitStack() as ctx:
        w = sb(nc, ctx, "fp_w", [128, CC, 512])
        brow = sb(nc, ctx, "fp_brow", [PT, 512])
        cos = sb(nc, ctx, "fp_cos", [PT, AD])
        sin = sb(nc, ctx, "fp_sin", [PT, AD])
        rdiag = sb(nc, ctx, "fp_rdiag", [128, 64])
        qk = sb(nc, ctx, "fp_qk", [PT, NH, AD])
        turned_by = sb(nc, ctx, "fp_turned", [PT, NH, AD])
        crossed = sb(nc, ctx, "fp_crossed", [PT, NH, AD])
        rot = sb(nc, ctx, "fp_rot", [PT, NH, AD])
        sq = sb(nc, ctx, "fp_sq", [PT, NH, AD])
        ssq = sb(nc, ctx, "fp_ssq", [PT, NH])
        ssqm = sb(nc, ctx, "fp_ssqm", [PT, NH])
        rnorm = sb(nc, ctx, "fp_rnorm", [PT, NH])
        norm = sb(nc, ctx, "fp_norm", [PT, NH])
        rotn = sb(nc, ctx, "fp_rotn", [PT, NH, AD])
        rotT = sb(nc, ctx, "fp_rotT", [128, 2, 3 * PT])
        arg = sb(nc, ctx, "fp_arg", [PT, NH, AD])
        near = sb(nc, ctx, "fp_near", [PT, NH, AD])
        layernorm(nc, k, "ln3", [(dst[:], t[name]) for dst, name in (
            (w, "f_w"), (brow, "f_b"), (cos, "f_cos"), (sin, "f_sin"), (rdiag, "f_r"))])
        ps = pb(nc, ctx, "fp_ps", 8)
        s = sems(nc, ctx, "fp", "loaded product biased chain ssqm norm rnorm turned copied feat argued ready sined")
        block = ctx.enter_context(nc.Block())
        by_pair = lambda x, p: x[:, p * QKH:(p + 1) * QKH, :].rearrange("q h d -> q (h d)")

        @block.sync
        def _(sp):
            for dst, name in ((k.wo, "f_wo"), (k.bo, "f_bo")):
                sp.dma_start(dst[:], t[name]).then_inc(s.loaded, 16)
            sp.wait_ge(s.loaded, 32)

        @block.tensor
        def _(pe):
            for p in range(PAIRS):
                for c in range(CC):
                    last = nc.tensor.matmul(ps[0:PT, p, :], k.xnT[:, c, p * PT:(p + 1) * PT], w[:, c, :],
                                            start=(c == 0), stop=(c == CC - 1))
                last.then_inc(s.product, 1)
            pe.wait_ge(s.biased, 2 * PAIRS)
            pe.wait_ge(s.ready, 1)
            for turn in range(PAIRS + 1):
                if turn < PAIRS:
                    if turn >= 2:
                        pe.wait_ge(s.copied, turn - 1)
                    for i in range(3):
                        last = nc.tensor.transpose(ps[:, turn % 2, i * PT:(i + 1) * PT],
                                                   by_pair(rotn, turn)[:, i * 128:(i + 1) * 128],
                                                   k.ident[0:PT, 0:PT])
                    last.then_inc(s.turned, 1)
                p = turn - 1
                if p < 0:
                    continue
                pe.wait_ge(s.copied, p + 1)
                if p >= 4:
                    pe.wait_ge(s.argued, 2 * (p - 3))
                for i in range(3):
                    last = nc.tensor.matmul(ps[0:PT, 4 + p % 4, i * 64:(i + 1) * 64],
                                            rotT[:, p % 2, i * PT:(i + 1) * PT], rdiag[:], start=True, stop=True)
                last.then_inc(s.feat, 1)

        @block.scalar
        def _(act):
            act.wait_ge(s.ssqm, 1)
            nc.scalar.activation(norm[:], ssqm[:], ACT.Sqrt).then_inc(s.norm, 1)
            for p in range(PAIRS):
                act.wait_ge(s.turned, p + 1)
                if p >= 2:
                    act.wait_ge(s.feat, p - 1)
                nc.scalar.copy(rotT[:, p % 2, :], ps[:, p % 2, 0:3 * PT]).then_inc(s.copied, 1)
            act.wait_ge(s.ready, 2)
            nc.scalar.activation(k.feat[:], near[:], ACT.Sin).then_inc(s.sined, 1)

        @block.vector
        def _(dve):
            count = [0]

            def step(ins):
                ins.then_inc(s.chain, 1)
                count[0] += 1
                dve.wait_ge(s.chain, count[0])

            heads = lambda x: x[:].unsqueeze(1).broadcast_to([PT, NH, AD])
            for p in range(PAIRS):
                dve.wait_ge(s.product, p + 1)
                nc.vector.tensor_tensor(by_pair(qk, p), ps[0:PT, p, 0:QKH * AD], brow[:, 0:QKH * AD], ALU.add)\
                    .then_inc(s.biased, 1)
                nc.vector.tensor_tensor(k.vals[:, p, :], ps[0:PT, p, QKH * AD:], brow[:, QKH * AD:], ALU.add)\
                    .then_inc(s.biased, 1)
            dve.wait_ge(s.biased, 2 * PAIRS)
            step(nc.vector.tensor_tensor(turned_by[:], qk[:], heads(cos), ALU.mult))
            step(nc.vector.tensor_tensor(crossed[:, :, 0:AF], qk[:, :, AF:], sin[:, 0:AF].unsqueeze(1)
                                         .broadcast_to([PT, NH, AF]), ALU.mult))
            step(nc.vector.tensor_tensor(crossed[:, :, AF:], qk[:, :, 0:AF], sin[:, AF:].unsqueeze(1)
                                         .broadcast_to([PT, NH, AF]), ALU.mult))
            step(nc.vector.tensor_tensor(rot[:], turned_by[:], crossed[:], ALU.add))
            step(nc.vector.tensor_tensor(sq[:], rot[:], rot[:], ALU.mult))
            step(nc.vector.tensor_reduce(ssq[:], sq[:], AX.X, ALU.add))
            nc.vector.tensor_scalar_max(ssqm[:], ssq[:], 1e-12).then_inc(s.ssqm, 1)
            dve.wait_ge(s.norm, 1)
            nc.vector.reciprocal(rnorm[:], norm[:]).then_inc(s.rnorm, 1)
            dve.wait_ge(s.rnorm, 1)
            nc.vector.tensor_tensor(rotn[:], rot[:], rnorm[:].unsqueeze(2).broadcast_to([PT, NH, AD]), ALU.mult)\
                .then_inc(s.ready, 1)
            for p in range(PAIRS):
                dve.wait_ge(s.feat, p + 1)
                prod = ps[0:PT, 4 + p % 4, 0:QKH * AF].rearrange("q (h f) -> q h f", f=AF)
                at = arg[:, p * QKH:(p + 1) * QKH, :]
                nc.vector.tensor_copy(at[:, :, 0:AF], prod).then_inc(s.argued, 1)
                nc.vector.tensor_scalar_add(at[:, :, AF:], prod, float(np.pi / 2)).then_inc(s.argued, 1)
            dve.wait_ge(s.argued, 2 * PAIRS)
            step(nc.vector.tensor_scalar(near[:], arg[:], float(1 / (2 * np.pi)), MAGIC, ALU.mult, ALU.add))
            step(nc.vector.tensor_scalar(sq[:], near[:], -MAGIC, None, ALU.add))
            step(nc.vector.scalar_tensor_tensor(out=rot[:], in0=sq[:], scalar=-TWO_PI_HI, in1=arg[:],
                                                op0=ALU.mult, op1=ALU.add))
            step(nc.vector.scalar_tensor_tensor(out=crossed[:], in0=sq[:], scalar=-TWO_PI_LO, in1=rot[:],
                                                op0=ALU.mult, op1=ALU.add))
            nc.vector.tensor_scalar(near[:], crossed[:], PI, -PI, ALU.min, ALU.max).then_inc(s.ready, 1)


def feature_mix(nc, k, t):
    QN, KN = AH * AD, AHKV * AD
    with ExitStack() as ctx:
        prod = sb(nc, ctx, "fm_prod", [PT, 2, AH, AHKV, AD])
        score = sb(nc, ctx, "fm_score", [PT, 2, AH, AHKV])
        prod2 = sb(nc, ctx, "fm_prod2", [PT, AH, AD, AHKV])
        mixed = sb(nc, ctx, "fm_mixed", [PT, PAIRS, AH, AD])
        again = sb(nc, ctx, "fm_again", [PT, PAIRS, HID])
        ps = pb(nc, ctx, "fm_ps", 4)
        s = sems(nc, ctx, "fm", "prod scored prod2 mixed out back turned copied")
        block = ctx.enter_context(nc.Block())

        @block.gpsimd
        def _(pool):
            for p in range(PAIRS):
                if p >= 2:
                    pool.wait_ge(s.scored, p - 1)
                feat = k.feat[:, p * QKH:(p + 1) * QKH, :]
                nc.gpsimd.tensor_tensor(prod[:, p % 2], feat[:, 0:AH, :].unsqueeze(2)
                                        .broadcast_to([PT, AH, AHKV, AD]),
                                        feat[:, AH:, :].unsqueeze(1).broadcast_to([PT, AH, AHKV, AD]),
                                        ALU.mult).then_inc(s.prod, 1)

        @block.vector
        def _(dve):
            for p in range(PAIRS):
                dve.wait_ge(s.prod, p + 1)
                nc.vector.tensor_reduce(score[:, p % 2], prod[:, p % 2], AX.X, ALU.add).then_inc(s.scored, 1)
                dve.wait_ge(s.scored, p + 1)
                dve.wait_ge(s.mixed, p)
                nc.vector.tensor_tensor(prod2[:], score[:, p % 2].unsqueeze(2).broadcast_to([PT, AH, AD, AHKV]),
                                        k.vals[:, p, :].rearrange("q (h d) -> q d h", d=AD).unsqueeze(1)
                                        .broadcast_to([PT, AH, AD, AHKV]), ALU.mult).then_inc(s.prod2, 1)
                dve.wait_ge(s.prod2, p + 1)
                nc.vector.tensor_reduce(mixed[:, p], prod2[:], AX.X, ALU.add).then_inc(s.mixed, 1)

        @block.sync
        def _(sp):
            for p in range(PAIRS):
                sp.wait_ge(s.mixed, p + 1)
                for e in range(2):
                    sp.dma_start(k.scratch_f[2 * p + e].rearrange("h t d -> t h d"),
                                 mixed[e * SEQ:(e + 1) * SEQ, p]).then_inc(s.out, 16)
            sp.wait_ge(s.out, 16 * BATCH)
            flat = k.scratch_f.rearrange("b h t d -> (b h t d)").rearrange("(p q n) -> q p n", q=PT, n=HID)
            sp.dma_start(again[:], flat).then_inc(s.back, 16)

        @block.tensor
        def _(pe):
            pe.wait_ge(s.back, 16)
            for b in range(4):
                for e in range(HPAIRS):
                    last = nc.tensor.transpose(ps[:, b, e * PT:(e + 1) * PT],
                                               again[:, (b // CC) * HPAIRS + e, (b % CC) * 128:(b % CC + 1) * 128],
                                               k.ident[0:PT, 0:PT])
                last.then_inc(s.turned, 1)

        @block.scalar
        def _(act):
            for b in range(4):
                act.wait_ge(s.turned, b + 1)
                nc.scalar.mul(k.oT[:, b % CC, (b // CC) * HALF:(b // CC + 1) * HALF], ps[:, b, 0:HALF],
                              2.0 / AD).then_inc(s.copied, 1)


def feature_attention(nc, k, t):
    with ExitStack() as ctx:
        k.vals = sb(nc, ctx, "fa_vals", [PT, PAIRS, AHKV * AD])
        k.feat = sb(nc, ctx, "fa_feat", [PT, PAIRS * QKH, AD])
        k.oT = sb(nc, ctx, "fa_oT", [128, CC, TOK])
        k.bo = sb(nc, ctx, "fa_bo", [PT, HID])
        k.wo = sb(nc, ctx, "fa_wo", [128, CC, HID])
        k.scratch_f = nc.dram_tensor("scratch_f", [BATCH, AH, SEQ, AD], F32, kind="Internal").ap()
        feature_products(nc, k, t)
        feature_mix(nc, k, t)
        add_projection(nc, k, "fa_out", k.wo, k.oT, CC, bias=k.bo[:])




def split_piece(nc, k, pool, pre, n, slot):
    pool.wait_ge(pre.raw_in, 16 * n + 16)
    nc.gpsimd.tensor_tensor(k.piece[:, slot, 0], k.raw[:], k.ones[:, 0:1].unsqueeze(2)
                            .broadcast_to([128, CC, KS]), ALU.mult).then_inc(pre.split, 1)
    pool.wait_ge(pre.split, 2 * n + 1)
    nc.gpsimd.tensor_tensor(k.piece[:, slot, 1], k.raw[:], k.piece[:, slot, 0], ALU.subtract)\
        .then_inc(pre.split, 1)


def grouped_queries(nc, k, t, pre):
    QUADS = PAIRS * XKV
    with ExitStack() as ctx:
        w = sb(nc, ctx, "gq_w", [128, CC, XH * XD])
        nw = sb(nc, ctx, "gq_nw", [128, 2])
        wraw = sb(nc, ctx, "gq_wraw", [128, CC, 2 * XKV * XD])
        nws = sb(nc, ctx, "gq_nws", [128, 1])
        sq = sb(nc, ctx, "gq_sq", [PT, 512])
        ssq = sb(nc, ctx, "gq_ssq", [PT, 2, 4])
        mean = sb(nc, ctx, "gq_mean", [PT, 2, 4])
        rms = sb(nc, ctx, "gq_rms", [PT, 2, 4])
        qn = sb(nc, ctx, "gq_qn", [PT, 2, 512])
        qT = sb(nc, ctx, "gq_qT", [128, 2, 2, XH, SEQ])
        layernorm(nc, k, "ln4", [(w[:], t["x_wq"]), (nw[:], t["x_nw"])])
        ps = pb(nc, ctx, "gq_ps", 4)
        pt = pb(nc, ctx, "gq_pt", 2)
        s = sems(nc, ctx, "gq", "product squared ssq mean rms normed turned weight copied")
        out = [sem(nc, ctx, f"gq_out{j}") for j in range(2)]
        block = ctx.enter_context(nc.Block())
        quad = lambda x: x.rearrange("q (v n) -> q v n", v=4)

        @block.sync
        def _(sp):
            sp.dma_start(k.raw[:], t["x_ctxT"][0]).then_inc(pre.raw_in, 16)
            sp.dma_start(wraw[:], t["x_wkv"]).then_inc(pre.w_in, 16)
            sp.wait_ge(pre.split, 2)
            sp.dma_start(k.raw[:], t["x_ctxT"][1]).then_inc(pre.raw_in, 16)
            for p in range(PAIRS):
                sp.wait_ge(s.copied, XKV * (p + 1))
                sp.dma_start(k.scratch_q[p], qT[:, p % 2]).then_inc(out[p % 2], 16)
            for j in range(2):
                sp.wait_ge(out[j], 16 * (PAIRS // 2))

        @block.tensor
        def _(pe):
            for u in range(QUADS + 2):
                if u < QUADS:
                    p, g = u // XKV, u % XKV
                    if u >= 4:
                        pe.wait_ge(s.normed, u - 3)
                    for c in range(CC):
                        last = nc.tensor.matmul(ps[0:PT, u % 4, :], k.xnT[:, c, p * PT:(p + 1) * PT],
                                                w[:, c, g * 512:(g + 1) * 512], start=(c == 0), stop=(c == CC - 1))
                    last.then_inc(s.product, 1)
                v = u - 2
                if v >= 0:
                    pe.wait_ge(s.normed, v + 1)
                    if v >= 2:
                        pe.wait_ge(s.copied, v - 1)
                    for h in range(4):
                        last = nc.tensor.transpose(pt[:, v % 2, h * PT:(h + 1) * PT],
                                                   qn[:, v % 2, h * 128:(h + 1) * 128], k.ident[0:PT, 0:PT])
                    last.then_inc(s.turned, 1)

        @block.scalar
        def _(act):
            act.wait_ge(s.weight, 1)
            for u in range(QUADS + 2):
                if u == QUADS // 4:
                    act.wait_ge(pre.w_in, 16)
                    nc.scalar.copy(k.wkv[:, 0], wraw[:]).then_inc(pre.w_high, 1)
                if u < QUADS:
                    act.wait_ge(s.product, u + 1)
                    if u >= 1:
                        act.wait_ge(s.ssq, u)
                    nc.scalar.square(sq[:], ps[0:PT, u % 4, :]).then_inc(s.squared, 1)
                v = u - 2
                if v >= 0:
                    p, g = v // XKV, v % XKV
                    act.wait_ge(s.turned, v + 1)
                    if p >= 2:
                        act.wait_ge(out[p % 2], 16 * (p // 2))
                    nc.scalar.mul(qT[:, p % 2, :, g * 4:(g + 1) * 4, :].rearrange("d j h n -> d h j n"),
                                  pt[:, v % 2, 0:4 * PT].rearrange("d (h j n) -> d h j n", h=4, j=2), nws[:]).then_inc(s.copied, 1)

        @block.gpsimd
        def _(pool):
            split_piece(nc, k, pool, pre, 0, 0)
            for u in range(QUADS):
                if u == QUADS // 2:
                    split_piece(nc, k, pool, pre, 1, 1)
                pool.wait_ge(s.mean, u + 1)
                if u >= 2:
                    pool.wait_ge(s.normed, u - 1)
                nc.gpsimd.tensor_tensor(rms[:, u % 2, :], mean[:, u % 2, :], k.minus_half[0:PT, 0:4], ALU.pow)\
                    .then_inc(s.rms, 1)

        @block.vector
        def _(dve):
            nc.vector.scalar_tensor_tensor(out=nws[:], in0=nw[:, 0:1], scalar=float(XD) ** -0.5, in1=nw[:, 1:2],
                                           op0=ALU.mult, op1=ALU.mult).then_inc(s.weight, 1)
            for u in range(QUADS):
                if u == QUADS // 2:
                    dve.wait_ge(pre.w_high, 1)
                    nc.vector.tensor_tensor(k.wkv[:, 1], wraw[:], k.wkv[:, 0], ALU.subtract).then_inc(pre.w_split, 1)
                dve.wait_ge(s.squared, u + 1)
                if u >= 2:
                    dve.wait_ge(s.mean, u - 1)
                nc.vector.tensor_reduce(ssq[:, u % 2, :], quad(sq[:]), AX.X, ALU.add).then_inc(s.ssq, 1)
                dve.wait_ge(s.ssq, u + 1)
                if u >= 2:
                    dve.wait_ge(s.rms, u - 1)
                nc.vector.tensor_scalar(mean[:, u % 2, :], ssq[:, u % 2, :], 1.0 / XD, 1e-6, ALU.mult, ALU.add)\
                    .then_inc(s.mean, 1)
                dve.wait_ge(s.rms, u + 1)
                if u >= 2:
                    dve.wait_ge(s.turned, u - 1)
                nc.vector.tensor_tensor(quad(qn[:, u % 2, :]), quad(ps[0:PT, u % 4, :]),
                                        rms[:, u % 2, :].unsqueeze(2).broadcast_to([PT, 4, 128]), ALU.mult)\
                    .then_inc(s.normed, 1)


def grouped_softmax(nc, k, t, pre):
    HP = XH // 2
    TILES = [2, 1] * (HP // 2)
    FIRST = [sum(TILES[:h]) for h in range(HP + 1)]
    QT = 4
    PIECES = NKT // QT
    ROUNDS = NKT // QT
    with ExitStack() as ctx:
        wo = sb(nc, ctx, "gx_wo", [128, XH, HID])
        wkv, piece = k.wkv, k.piece
        kT = sb(nc, ctx, "gx_kT", [128, 2, XKV, CTX])
        val = sb(nc, ctx, "gx_val", [KT, 2, NKT, XKV * XD])
        qT = sb(nc, ctx, "gx_qT", [128, 2, XH, SEQ])
        oT = sb(nc, ctx, "gx_oT", [128, XH, PT])
        ksq = sb(nc, ctx, "gx_ksq", [KT, 512])
        kssq = sb(nc, ctx, "gx_kssq", [KT, 4])
        kmean = sb(nc, ctx, "gx_kmean", [KT, 4])
        krms = sb(nc, ctx, "gx_krms", [KT, 4])
        kn = sb(nc, ctx, "gx_kn", [KT, 2, 512])
        prob = sb(nc, ctx, "gx_prob", [PT, 2, CTX])
        pT = sb(nc, ctx, "gx_pT", [KT, NKT, PT])
        negmax = sb(nc, ctx, "gx_negmax", [PT, 2])
        total = sb(nc, ctx, "gx_total", [PT, 2])
        rtotal = sb(nc, ctx, "gx_rtotal", [PT, 2])
        ps_s = pb(nc, ctx, "gx_ps_s", 3)
        ps_t = pb(nc, ctx, "gx_ps_t", 2)
        ps_k = pb(nc, ctx, "gx_ps_k", 1)
        ps_v = pb(nc, ctx, "gx_ps_v", 1)
        ps_o = pb(nc, ctx, "gx_ps_o", 1)
        s = sems(nc, ctx, "gx", "scored negmax exped rtotal probn pv stored projected added "
                 "k_ps v_ps k_sq k_ssq k_mean k_rms k_normed v_copied wo_in", pairs="q_in")
        turned = [sem(nc, ctx, f"gx_turned{j}") for j in range(2)]
        copied = [sem(nc, ctx, f"gx_copied{j}") for j in range(2)]
        block = ctx.enter_context(nc.Block())
        quad = lambda x: x.rearrange("q (v n) -> q v n", v=4)

        TURNS = 2 * NKT + 2 * HP * ROUNDS
        LACKING = ((ROUNDS + 1) // 2, ROUNDS // 2)


        def plan(first, last):
            tasks, n = [], 0

            def turn(kind, e, x):
                nonlocal n
                tasks.append((kind, e, x, n % 2, n // 2))
                n += 1

            def values(e):
                tasks.append(("values", e, 0, (n - 1) % 2, ((n + 1) // 2, n // 2)))

            def make_values(e, tile):
                tasks.append(("make_values", e, tile, None, None))
                if tile % QT == QT - 1 and not (last and tile // QT > 0):
                    splits.append(("split", e, tile // QT, None, None))

            if first:
                n = ROUNDS
            for e in range(2 * HP):
                j, h = e // HP % 2, e % HP
                splits = []
                tiles = [] if last and j == 1 else list(range(FIRST[h], FIRST[h + 1]))
                tasks.append(("scores", e, 0, None, ((n + 1) // 2, n // 2)))
                if tiles and h:
                    for tile in range(FIRST[h - 1], FIRST[h]):
                        turn("turn_keys", e, tile)
                if e or not first:
                    for r in range(ROUNDS - 1):
                        turn("turn_probs", e - 1, r)
                tasks.append(("exp", e, 0, None, None))
                if tiles:
                    tasks.append(("make_keys", e, tiles[0], None, None))
                    tasks.append(("square_keys", e, tiles[0], None, None))
                if e or not first:
                    turn("turn_probs", e - 1, ROUNDS - 1)
                if tiles:
                    tasks.append(("sum_keys", e, tiles[0], None, None))
                tasks.append(("norm", e, 0, None, None))
                if tiles:
                    tasks.append(("scale_keys", e, tiles[0], None, None))
                if tiles and h:
                    make_values(e, tiles[0])
                if e or not first:
                    values(e - 1)
                if tiles and not h:
                    make_values(e, tiles[0])
                if e == 0 and not first:
                    tasks.append(("project", -1, 0, None, None))
                for tile in tiles[1:]:
                    for kind in ("make_keys", "square_keys", "sum_keys", "scale_keys"):
                        tasks.append((kind, e, tile, None, None))
                    make_values(e, tile)
                tasks += splits
                if tiles and h == HP - 1:
                    for tile in tiles:
                        turn("turn_keys", e, tile)
            return tasks

        def ending():
            tasks = [("turn_probs", -1, r, r % 2, r // 2) for r in range(ROUNDS)]
            return tasks + [("values", -1, 0, (ROUNDS - 1) % 2, ((ROUNDS + 1) // 2, ROUNDS // 2)), ("project", -1, 0, None, None)]

        def pairs(eng, task):
            def run(i, tasks, lacking=LACKING):
                before = [TURNS // 2 * i + (NKT // 2 - x) for x in lacking]
                for kind, e, n, bank, uses in tasks:
                    if isinstance(uses, tuple):
                        uses = [before[b] + uses[b] for b in range(2)]
                    elif uses is not None:
                        uses = before[bank] + uses
                    task(i, kind, e, n, bank, uses)

            run(0, plan(True, False))
            with eng.Fori(0, PAIRS - 2) as i:
                run(i + 1, plan(False, False))
            run(PAIRS - 1, plan(False, True))
            run(PAIRS, ending(), [x + NKT // 2 for x in LACKING])

        def dve_copies(r):
            return r == ROUNDS - 1

        def key_tile(i, e, tile):
            j = e // HP
            return (j + 1) % 2, NKT * (2 * i + j + 1) + tile

        @block.sync
        def _(sp):
            def load(n):
                sp.wait_ge(pre.split, 2 * n)
                sp.dma_start(k.raw[:], t["x_ctxT"][n]).then_inc(pre.raw_in, 16)

            def load_q(i, j, used):
                if used is not None:
                    sp.wait_ge(s.scored, used)
                sp.dma_start(qT[:, j], k.scratch_q[i, :, j]).then_inc(s.q_in[j], 16)

            load(2)
            load_q(0, 0, None)
            sp.dma_start(wo[:], t["x_wo"]).then_inc(s.wo_in, 16)
            for n in range(3, PIECES + 2):
                load(n)

            def pair(i, first, last):
                load_q(i, 1, None if first else 2 * HP * i)
                for q in range(PIECES + 2, PIECES + 3 if last else 3 * PIECES + 2):
                    load(2 * PIECES * i + q)
                    if q == 2 * PIECES + 2:
                        load_q(i + 1, 0, 2 * HP * i + HP)

            pair(0, True, False)
            with sp.Fori(0, PAIRS - 2) as i:
                pair(i + 1, False, False)
            pair(PAIRS - 1, False, True)

        @block.tensor
        def _(pe):
            def make_keys(slot, count, tile, pieces):
                if tile % QT == 0:
                    pe.wait_ge(pre.split, 2 * pieces)
                pe.wait_ge(s.k_normed, count)
                product(ps_k, slot, tile, 0).then_inc(s.k_ps, 1)

            def make_values(slot, count, tile):
                pe.wait_ge(s.v_copied, count)
                product(ps_v, slot, tile, XKV * XD).then_inc(s.v_ps, 1)

            def product(psum, slot, tile, w0):
                lo = tile % QT * KT
                terms = [(c, a, b) for c in range(CC) for a, b in SPLIT_TERMS]
                for c, a, b in terms:
                    last = nc.tensor.matmul(psum[0:KT, 0, :], piece[:, slot, a, c, lo:lo + KT],
                                            wkv[:, b, c, w0:w0 + 512], start=((c, a, b) == terms[0]),
                                            stop=((c, a, b) == terms[-1]))
                return last

            def turn_keys(tile, count, bank, use):
                pe.wait_ge(s.k_normed, count + 1)
                pe.wait_ge(copied[bank], use)
                for g in range(XKV):
                    last = nc.tensor.transpose(ps_t[:, bank, g * KT:(g + 1) * KT],
                                               kn[:, tile % 2, g * 128:(g + 1) * 128], k.ident[0:KT, 0:KT])
                last.then_inc(turned[bank], 1)

            def task(i, kind, e, n, bank, use):
                j, h = e // HP % 2, e % HP
                step = 2 * HP * i + e
                if kind == "scores":
                    if h == 0:
                        pe.wait_ge(s.q_in[j], 16 * i + 16)
                        pe.wait_ge(s.v_copied, NKT * (2 * i + j + 1))
                        for b in range(2):
                            pe.wait_ge(copied[b], use[b])
                    pe.wait_ge(s.exped, step)
                    for b in range(NKS):
                        last = nc.tensor.matmul(ps_s[0:PT, b, 0:KS], qT[:, j, 2 * h:2 * h + 2, :],
                                                kT[:, j, h // 2, b * KS:(b + 1) * KS], start=True, stop=True)
                    last.then_inc(s.scored, 1)
                elif kind == "turn_keys":
                    slot, count = key_tile(i, e, n)
                    turn_keys(n, count, bank, use)
                elif kind == "make_keys":
                    slot, count = key_tile(i, e, n)
                    pn = PIECES * (j + 1) + n // QT
                    make_keys(pn % 2, count, n, 2 * PIECES * i + pn + 1)
                elif kind == "make_values":
                    slot, count = key_tile(i, e, n)
                    make_values((PIECES * (j + 1) + n // QT) % 2, count, n)
                elif kind == "turn_probs":
                    if n == 0:
                        pe.wait_ge(s.probn, step + 1)
                    pe.wait_ge(copied[bank], use)
                    for x in range(QT):
                        last = nc.tensor.transpose(ps_t[0:KT, bank, x * PT:(x + 1) * PT],
                                                   prob[:, e % 2, (n * QT + x) * KT:(n * QT + x + 1) * KT],
                                                   k.ident[0:PT, 0:PT])
                    last.then_inc(turned[bank], 1)
                elif kind == "values":
                    pe.wait_ge(s.stored, step)
                    if e == 0:
                        pe.wait_ge(s.added, i)
                    for x in range(NKT):
                        if x == 0:
                            pe.wait_ge(copied[bank], use[bank] - 1)
                            pe.wait_ge(copied[1 - bank], use[1 - bank])
                        if x == (ROUNDS - 1) * QT:
                            pe.wait_ge(copied[bank], use[bank])
                        last = nc.tensor.matmul(ps_o[:, 0, 0:PT], val[:, j, x, h // 2 * 128:(h // 2 + 1) * 128],
                                                pT[:, x, :], start=(x == 0), stop=(x == NKT - 1))
                    last.then_inc(s.pv, 1)
                elif kind == "project":
                    pe.wait_ge(s.wo_in, 16)
                    pe.wait_ge(s.stored, 2 * HP * i)
                    for x in range(XH):
                        last = nc.tensor.matmul(ps_o[0:PT, 0, 0:HID], oT[:, x, :], wo[:, x, :],
                                                start=(x == 0), stop=(x == XH - 1))
                    last.then_inc(s.projected, 1)

            for tile in range(NKT):
                make_keys(tile // QT % 2, tile, tile, tile // QT + 1)
                make_values(tile // QT % 2, tile, tile)
                if tile:
                    turn_keys(tile - 1, tile - 1, (tile - 1) % 2, (tile - 1) // 2)
            turn_keys(NKT - 1, NKT - 1, (NKT - 1) % 2, (NKT - 1) // 2)
            pairs(pe, task)

        def copy_keys(eng, copy, slot, tile, bank, use):
            eng.wait_ge(turned[bank], use + 1)
            copy(kT[:, slot, :, tile * KT:(tile + 1) * KT],
                 ps_t[:, bank, 0:XKV * KT].rearrange("d (g n) -> d g n", g=XKV)).then_inc(copied[bank], 1)

        def copy_probs(eng, copy, r, bank, use):
            eng.wait_ge(turned[bank], use + 1)
            copy(pT[:, r * QT:(r + 1) * QT, :].rearrange("q x n -> q (x n)"), ps_t[0:KT, bank, 0:QT * PT])\
                .then_inc(copied[bank], 1)

        @block.scalar
        def _(act):
            def square(count):
                act.wait_ge(s.k_ps, count + 1)
                act.wait_ge(s.k_ssq, count)
                nc.scalar.square(ksq[:], ps_k[0:KT, 0, :]).then_inc(s.k_sq, 1)

            def copy_values(slot, tile, count):
                act.wait_ge(s.v_ps, count + 1)
                nc.scalar.copy(val[:, slot, tile, :], ps_v[0:KT, 0, :]).then_inc(s.v_copied, 1)

            def task(i, kind, e, n, bank, use):
                j, h = e // HP % 2, e % HP
                step = 2 * HP * i + e
                if kind == "exp":
                    act.wait_ge(s.negmax, step + 1)
                    nc.scalar.activation(prob[:, e % 2, :].rearrange("q (b n) -> q b n", b=NKS), ps_s[0:PT, :, 0:KS],
                                         ACT.Exp, bias=negmax[:, e % 2:e % 2 + 1],
                                         accum_out=total[:, e % 2:e % 2 + 1]).then_inc(s.exped, 1)
                elif kind == "square_keys":
                    square(key_tile(i, e, n)[1])
                elif kind == "make_values":
                    slot, count = key_tile(i, e, n)
                    copy_values(slot, n, count)
                elif kind == "turn_keys":
                    copy_keys(act, nc.scalar.copy, key_tile(i, e, n)[0], n, bank, use)
                elif kind == "turn_probs" and not dve_copies(n):
                    copy_probs(act, nc.scalar.copy, n, bank, use)
                elif kind == "values":
                    act.wait_ge(s.pv, step + 1)
                    if e == 0:
                        act.wait_ge(s.projected, i)
                    nc.scalar.copy(oT[:, 2 * h:2 * h + 2, j * SEQ:(j + 1) * SEQ],
                                   ps_o[:, 0, 0:PT].rearrange("d (h n) -> d h n", h=2)).then_inc(s.stored, 1)

            for tile in range(NKT):
                square(tile)
                copy_values(0, tile, tile)
                if tile and (tile - 1) % 2 == 0:
                    copy_keys(act, nc.scalar.copy, 0, tile - 1, 0, (tile - 1) // 2)
            pairs(act, task)

        @block.gpsimd
        def _(pool):
            def root(count):
                pool.wait_ge(s.k_mean, count + 1)
                nc.gpsimd.tensor_tensor(krms[:], kmean[:], k.minus_half[0:KT, 0:4], ALU.pow).then_inc(s.k_rms, 1)

            def task(i, kind, e, n, bank, use):
                if kind == "scale_keys":
                    root(key_tile(i, e, n)[1])
                elif kind == "split":
                    split(2 * PIECES * i + PIECES * (e // HP + 1) + n + 2, (e // HP + 1 + n) % 2)

            def split(n, slot):
                pool.wait_ge(s.v_ps, QT * (n - 1))
                split_piece(nc, k, pool, pre, n, slot)

            for tile in range(NKT):
                root(tile)
                if tile % QT == QT - 1:
                    split(tile // QT + 2, tile // QT % 2)
            pairs(pool, task)

        @block.vector
        def _(dve):
            def sum_keys(count):
                dve.wait_ge(s.k_sq, count + 1)
                nc.vector.tensor_reduce(kssq[:], quad(ksq[:]), AX.X, ALU.add).then_inc(s.k_ssq, 1)
                dve.wait_ge(s.k_ssq, count + 1)
                nc.vector.tensor_scalar(kmean[:], kssq[:], 1.0 / XD, 1e-6, ALU.mult, ALU.add).then_inc(s.k_mean, 1)

            def scale_keys(count, tile):
                dve.wait_ge(s.k_rms, count + 1)
                nc.vector.tensor_tensor(quad(kn[:, tile % 2, :]), quad(ps_k[0:KT, 0, :]),
                                        krms[:].unsqueeze(2).broadcast_to([KT, 4, 128]), ALU.mult)\
                    .then_inc(s.k_normed, 1)

            def task(i, kind, e, n, bank, use):
                j, h = e // HP % 2, e % HP
                step = 2 * HP * i + e
                if kind == "scores":
                    dve.wait_ge(s.scored, step + 1)
                    nc.vector.tensor_reduce(negmax[:, e % 2:e % 2 + 1], ps_s[0:PT, :, 0:KS], AX.XY, ALU.max,
                                            negate=True).then_inc(s.negmax, 1)
                elif kind == "sum_keys":
                    sum_keys(key_tile(i, e, n)[1])
                elif kind == "scale_keys":
                    scale_keys(key_tile(i, e, n)[1], n)
                elif kind == "norm":
                    dve.wait_ge(s.exped, step + 1)
                    nc.vector.reciprocal(rtotal[:, e % 2:e % 2 + 1], total[:, e % 2:e % 2 + 1]).then_inc(s.rtotal, 1)
                    dve.wait_ge(s.rtotal, step + 1)
                    nc.vector.tensor_scalar_mul(prob[:, e % 2, :], prob[:, e % 2, :],
                                                rtotal[:, e % 2:e % 2 + 1]).then_inc(s.probn, 1)
                elif kind == "turn_probs" and dve_copies(n):
                    copy_probs(dve, nc.vector.tensor_copy, n, bank, use)
                elif kind == "project":
                    dve.wait_ge(s.projected, i)
                    nc.vector.tensor_tensor(k.x[:, i - 1, :], k.x[:, i - 1, :], ps_o[0:PT, 0, 0:HID], ALU.add)\
                        .then_inc(s.added, 1)

            for tile in range(NKT):
                sum_keys(tile)
                scale_keys(tile, tile)
                if tile and (tile - 1) % 2 == 1:
                    copy_keys(dve, nc.vector.tensor_copy, 0, tile - 1, 1, (tile - 1) // 2)
            copy_keys(dve, nc.vector.tensor_copy, 0, NKT - 1, 1, (NKT - 1) // 2)
            pairs(dve, task)


def grouped_attention(nc, k, t):
    k.scratch_q = nc.dram_tensor("scratch_q", [PAIRS, 128, 2, XH, SEQ], F32, kind="Internal").ap()
    with ExitStack() as ctx:
        k.wkv = sb(nc, ctx, "ga_wkv", [128, 2, CC, 2 * XKV * XD], F32R)
        k.raw = sb(nc, ctx, "ga_raw", [128, CC, KS])
        k.piece = sb(nc, ctx, "ga_piece", [128, 2, 2, CC, KS], F32R)
        pre = sems(nc, ctx, "ga", "raw_in split w_in w_high w_split")
        grouped_queries(nc, k, t, pre)
        grouped_softmax(nc, k, t, pre)


def lora_slots(nc, k, a1):
    ER = E1 * R1
    with ExitStack() as ctx:
        chosen = sb(nc, ctx, "ls_chosen", [PT, 2, PAIRS, E1])
        z = sb(nc, ctx, "ls_z", [PT, 2, PAIRS, 128])
        ps = pb(nc, ctx, "ls_ps", 1)
        pt = pb(nc, ctx, "ls_pt", 4)
        s = sems(nc, ctx, "ls", "product onehot chosen weight scaled zeroed masked turned copied low summed")
        block = ctx.enter_context(nc.Block())
        psv = ps[0:PT, 0, :].rearrange("q (p n) -> q p n", p=PAIRS)

        @block.gpsimd
        def _(pool):
            nc.gpsimd.memset(z[:], 0.0).then_inc(s.zeroed, 1)

        @block.tensor
        def _(pe):
            for p in range(PAIRS):
                for c in range(CC):
                    last = nc.tensor.matmul(psv[:, p, :], k.xnT[:, c, p * PT:(p + 1) * PT], a1[:, c, :],
                                            start=(c == 0), stop=(c == CC - 1))
            last.then_inc(s.product, 1)
            for m in range(2):
                for half in range(2):
                    pe.wait_ge(s.masked, (m + 1) * PAIRS)
                    for e in range(HPAIRS):
                        last = nc.tensor.transpose(pt[:, 2 * m + half, e * PT:(e + 1) * PT],
                                                   z[:, m, half * HPAIRS + e, :], k.ident[0:PT, 0:PT])
                    last.then_inc(s.turned, 1)

        @block.scalar
        def _(act):
            for n in range(4):
                act.wait_ge(s.turned, n + 1)
                nc.scalar.copy(k.zs[:, 0, n // 2, (n % 2) * HALF:(n % 2 + 1) * HALF], pt[:, n, 0:HALF])\
                    .then_inc(s.copied, 1)

        @block.vector
        def _(dve):
            for m in range(2):
                nc.vector.tensor_scalar(k.onehot[:, m], k.rank[:], float(m), None, ALU.is_equal).then_inc(s.onehot, 1)
                dve.wait_ge(s.onehot, m + 1)
                nc.vector.tensor_tensor(chosen[:, m], k.onehot[:, m], k.prob[:], ALU.mult).then_inc(s.chosen, 1)
                dve.wait_ge(s.chosen, m + 1)
                nc.vector.tensor_reduce(k.wchoice[:, m, :], chosen[:, m], AX.X, ALU.add).then_inc(s.weight, 1)
                nc.vector.tensor_scalar_mul(k.onehotw[:, m], chosen[:, m], LSCALE).then_inc(s.scaled, 1)
            dve.wait_ge(s.weight, 2)
            nc.vector.tensor_tensor(k.wsum[:], k.wchoice[:, 0, :], k.wchoice[:, 1, :], ALU.add).then_inc(s.summed, 1)
            dve.wait_ge(s.product, 1)
            dve.wait_ge(s.zeroed, 1)
            for m in range(2):
                for p in range(PAIRS):
                    nc.vector.scalar_tensor_tensor(out=z[:, m, p, 0:ER].rearrange("q (e r) -> q e r", r=R1),
                                                   in0=psv[:, p, :].rearrange("q (e r) -> q e r", r=R1), scalar=LSCALE,
                                                   in1=k.onehot[:, m, p, :].unsqueeze(2).broadcast_to([PT, E1, R1]),
                                                   op0=ALU.mult, op1=ALU.mult).then_inc(s.masked, 1)
            for n in range(4):
                dve.wait_ge(s.copied, n + 1)
                cols = slice((n % 2) * HALF, (n % 2 + 1) * HALF)
                nc.vector.tensor_tensor(k.zs[:, 1, n // 2, cols], pt[:, n, 0:HALF], k.zs[:, 0, n // 2, cols],
                                        ALU.subtract).then_inc(s.low, 1)


def lora_mlp(nc, k, w1s, b1xs, b1, w2a2, b2x, b2):
    FT = F1 // 128
    ER = E1 * R1
    with ExitStack() as ctx:
        hT = sb(nc, ctx, "lm_hT", [128, 2, FT, TOK])
        z2 = sb(nc, ctx, "lm_z2", [PT, PAIRS, 128])
        part = sb(nc, ctx, "lm_part", [PT, 2, ER])
        z2T = sb(nc, ctx, "lm_z2T", [128, TOK])
        up = pb(nc, ctx, "lm_up", 4)
        down = pb(nc, ctx, "lm_down", 2)
        pt = pb(nc, ctx, "lm_pt", 2)
        s = sems(nc, ctx, "lm", "upped gelued downed weighed parted zeroed summed turned copied last added")
        block = ctx.enter_context(nc.Block())
        N = 4 * FT

        @block.gpsimd
        def _(pool):
            nc.gpsimd.memset(z2[:], 0.0).then_inc(s.zeroed, 1)

        @block.tensor
        def _(pe):
            for n in range(N):
                f, m, half = n // 4, n // 2 % 2, n % 2
                if n >= 4:
                    pe.wait_ge(s.gelued, n - 3)
                cols = slice(half * HALF, (half + 1) * HALF)
                terms = [(w1s[:, a, c, f * 128:(f + 1) * 128], k.xs[:, b, c, cols])
                         for c in range(CC) for a, b in SPLIT_TERMS]
                terms += [(b1xs[:, a, f * 128:(f + 1) * 128], k.zs[:, b, m, cols]) for a, b in SPLIT_TERMS]
                for x, (weight, values) in enumerate(terms):
                    last = nc.tensor.matmul(up[:, n % 4, 0:HALF], weight, values, start=(x == 0),
                                            stop=(x == len(terms) - 1))
                last.then_inc(s.upped, 1)
            pe.wait_ge(s.gelued, N)
            for n in range(2 * PAIRS):
                p, m = n // 2, n % 2
                if n >= 2:
                    pe.wait_ge(s.parted, n - 1)
                for f in range(FT):
                    last = nc.tensor.matmul(down[0:PT, m, 0:HID + ER], hT[:, m, f, p * PT:(p + 1) * PT],
                                            w2a2[:, f, :], start=(f == 0), stop=(f == FT - 1))
                last.then_inc(s.downed, 1)
            for half in range(2):
                pe.wait_ge(s.summed, (half + 1) * HPAIRS)
                for e in range(HPAIRS):
                    last = nc.tensor.transpose(pt[:, half, e * PT:(e + 1) * PT], z2[:, half * HPAIRS + e, :],
                                               k.ident[0:PT, 0:PT])
                last.then_inc(s.turned, 1)
            for p in range(PAIRS):
                pe.wait_ge(s.copied, p // HPAIRS + 1)
                if p >= 4:
                    pe.wait_ge(s.added, p - 3)
                nc.tensor.matmul(up[0:PT, p % 4, 0:HID], z2T[:, p * PT:(p + 1) * PT], b2x[:],
                                 start=True, stop=True).then_inc(s.last, 1)

        @block.scalar
        def _(act):
            for n in range(N):
                f, m, half = n // 4, n // 2 % 2, n % 2
                act.wait_ge(s.upped, n + 1)
                nc.scalar.activation(hT[:, m, f, half * HALF:(half + 1) * HALF], up[:, n % 4, 0:HALF],
                                     ACT.Gelu_apprx_tanh, bias=b1[:, f:f + 1]).then_inc(s.gelued, 1)
            for half in range(2):
                act.wait_ge(s.turned, half + 1)
                nc.scalar.copy(z2T[:, half * HALF:(half + 1) * HALF], pt[:, half, 0:HALF]).then_inc(s.copied, 1)

        @block.vector
        def _(dve):
            for p in range(PAIRS):
                nc.vector.scalar_tensor_tensor(out=k.x[:, p, :], in0=b2[:], scalar=k.wsum[:, p:p + 1],
                                               in1=k.x[:, p, :], op0=ALU.mult, op1=ALU.add).then_inc(s.weighed, 1)
            dve.wait_ge(s.zeroed, 1)
            for n in range(2 * PAIRS):
                p, m = n // 2, n % 2
                dve.wait_ge(s.downed, n + 1)
                dve.wait_ge(s.weighed, PAIRS + n if m else p + 1)
                nc.vector.scalar_tensor_tensor(out=k.x[:, p, :], in0=down[0:PT, m, 0:HID],
                                               scalar=k.wchoice[:, m, p:p + 1], in1=k.x[:, p, :],
                                               op0=ALU.mult, op1=ALU.add).then_inc(s.weighed, 1)
                if n >= 2:
                    dve.wait_ge(s.summed, n // 2)
                nc.vector.tensor_tensor(part[:, m, :].rearrange("q (e r) -> q e r", r=R1),
                                        down[0:PT, m, HID:HID + ER].rearrange("q (e r) -> q e r", r=R1),
                                        k.onehotw[:, m, p, :].unsqueeze(2).broadcast_to([PT, E1, R1]), ALU.mult)\
                    .then_inc(s.parted, 1)
                if m:
                    dve.wait_ge(s.parted, n + 1)
                    nc.vector.tensor_tensor(z2[:, p, 0:ER], part[:, 0, :], part[:, 1, :], ALU.add).then_inc(s.summed, 1)
            dve.wait_ge(s.weighed, 3 * PAIRS)
            for p in range(PAIRS):
                dve.wait_ge(s.last, p + 1)
                nc.vector.tensor_tensor(k.x[:, p, :], k.x[:, p, :], up[0:PT, p % 4, 0:HID], ALU.add)\
                    .then_inc(s.added, 1)


def routed_lora(nc, k, t):
    with ExitStack() as ctx:
        k.t = t
        k.prob = sb(nc, ctx, "rl_prob", [PT, PAIRS, E1])
        k.rank = sb(nc, ctx, "rl_rank", [PT, PAIRS, E1])
        k.onehot = sb(nc, ctx, "rl_onehot", [PT, 2, PAIRS, E1])
        k.onehotw = sb(nc, ctx, "rl_onehotw", [PT, 2, PAIRS, E1])
        k.wchoice = sb(nc, ctx, "rl_wchoice", [PT, 2, PAIRS])
        k.wsum = sb(nc, ctx, "rl_wsum", [PT, PAIRS])
        k.zs = sb(nc, ctx, "rl_zs", [128, 2, 2, TOK], F32R)
        k.xs = sb(nc, ctx, "rl_xs", [128, 2, CC, TOK], F32R)
        ER, FT = E1 * R1, F1 // 128
        a1 = sb(nc, ctx, "rl_a1", [128, CC, ER])
        w1 = sb(nc, ctx, "rl_w1", [128, CC, F1])
        w1s = sb(nc, ctx, "rl_w1s", [128, 2, CC, F1], F32R)
        b1x = sb(nc, ctx, "rl_b1x", [128, F1])
        b1xs = sb(nc, ctx, "rl_b1xs", [128, 2, F1], F32R)
        b1 = sb(nc, ctx, "rl_b1", [128, FT])
        w2a2 = sb(nc, ctx, "rl_w2a2", [128, FT, HID + ER])
        b2x = sb(nc, ctx, "rl_b2x", [128, HID])
        b2 = sb(nc, ctx, "rl_b2", [PT, HID])
        s = sems(nc, ctx, "rl", "loaded high low")
        operands = ((a1, "l_a1"), (w1, "l_w1"), (b1x, "l_b1x"), (b1, "l_b1"), (w2a2, "l_w2a2"), (b2x, "l_b2x"),
                    (b2, "l_b2"))

        to_split = ((k.xs, k.xnT), (w1s, w1), (b1xs, b1x))

        def high_parts(act):
            for parts, src in to_split:
                if src is w1:
                    act.wait_ge(s.loaded, 16 * len(operands))
                nc.scalar.copy(parts[:, 0], src[:]).then_inc(s.high, 1)

        def low_parts(pool):
            for n, (parts, src) in enumerate(to_split):
                pool.wait_ge(s.high, n + 1)
                nc.gpsimd.tensor_tensor(parts[:, 1], src[:], parts[:, 0], ALU.subtract).then_inc(s.low, 1)
            pool.wait_ge(s.low, len(to_split))

        route(nc, k, "r1", "ln5", t["r1_w"], t["r1_b"], loads=[(dst[:], t[name], s.loaded) for dst, name in operands],
              awaited=(s.loaded, 16 * len(operands)), pool_work=low_parts,
              act_work=high_parts)
        lora_slots(nc, k, a1)
        lora_mlp(nc, k, w1s, b1xs, b1, w2a2, b2x, b2)


def decoder(nc, t, out, stages=range(6)):
    with ExitStack() as ctx:
        k = Shared()
        k.x = sb(nc, ctx, "x", [PT, PAIRS, HID])
        k.xnT = sb(nc, ctx, "xnT", [128, CC, TOK])
        k.ident = sb(nc, ctx, "ident", [128, 128])
        k.ones = sb(nc, ctx, "ones", [128, 128])
        k.minus_half = sb(nc, ctx, "minus_half", [128, 48])
        k.eps6 = sb(nc, ctx, "eps6", [128, 32])
        k.half = sb(nc, ctx, "half", [128, 8])
        load_constants(nc, k, t)
        sublayers = [gated_delta_rule, context_attention, routed_swiglu, feature_attention,
                     grouped_attention, routed_lora]
        for i in stages:
            sublayers[i](nc, k, t)
        store_result(nc, k, out)


def lay_out(**inputs):
    a = {n: np.asarray(v) for n, v in inputs.items()}
    f = np.ascontiguousarray

    def chunked(w):
        return f(w.T.reshape(-1, 128, w.shape[0]).transpose(1, 0, 2))

    def rows(v, n):
        return f(np.broadcast_to(v, (n, v.size)))

    o = {"x": f(a["x"].reshape(TOK, HID)), "ident": np.eye(128, dtype=np.float32)}

    w = a["L0_attn_W_qkv"]
    cw = a["L0_attn_conv_w"]
    qd = NK * DK
    per_head = []
    for h in range(NK):
        r0 = [qd + h * DK, h * DK, 2 * qd + 2 * h * DK, 2 * qd + (2 * h + 1) * DK]
        mats = np.stack([chunked(w[r:r + DK]) for r in r0], axis=1)
        taps = np.stack([cw[r:r + DK] for r in r0], axis=1)
        per_head.append(np.concatenate([mats.reshape(128, -1), taps.reshape(128, -1)], axis=1))
    o["gdn_w"] = f(np.stack(per_head))
    o["gdn_wba"] = chunked(np.concatenate([a["L0_attn_W_b"], a["L0_attn_W_a"]]))
    o["gdn_rows"] = rows(np.concatenate([a["L0_attn_dt_bias"], a["L0_attn_A_log"]]), PT)
    o["gdn_normw"] = rows(a["L0_attn_norm_w"], PT)
    o["gdn_wz"] = f(np.stack([chunked(a["L0_attn_W_z"][g * GV * 128:(g + 1) * GV * 128]) for g in range(GROUPS)]))
    o["gdn_wo"] = f(a["L0_attn_W_out"].T.reshape(GROUPS, GV, 128, HID).transpose(0, 2, 1, 3))
    r, c = np.arange(PT)[:, None], np.arange(PT)[None, :]
    same = (r // SEQ) == (c // SEQ)
    o["gdn_after"] = (same & (c < r)).astype(np.float32)
    o["gdn_upto"] = (same & (r <= c)).astype(np.float32)
    o["gdn_kqmask"] = f(np.concatenate([-(same & (r < c)).astype(np.float32),
                                        (same & (r <= c)).astype(np.float32)], axis=1))

    o["context"] = a["ctx_2048"]
    for n in "qkvo":
        o[f"c_w{n}"] = chunked(a[f"L0_xattn_w{n}"])

    o["r0_w"] = chunked(a["L0_ffn_gate_w"])
    e = np.arange(E0)
    o["earlier"] = rows((e[None, :] < e[:, None]).astype(np.float32).reshape(-1), PT)
    w1, w2, w3 = a["L0_ffn_w1"], a["L0_ffn_w2"], a["L0_ffn_w3"]
    o["s_w"] = f(np.stack([np.concatenate([chunked(w1[i]).reshape(128, -1), chunked(w3[i]).reshape(128, -1),
                                           chunked(w2[i]).reshape(128, -1)], axis=1) for i in range(E0)]))

    o["f_w"] = chunked(np.concatenate([a["L1_attn_Wq"], a["L1_attn_Wk"], a["L1_attn_Wv"]]))
    o["f_b"] = rows(np.concatenate([a["L1_attn_bq"], a["L1_attn_bk"], a["L1_attn_bv"]]), PT)
    o["f_wo"] = chunked(a["L1_attn_Wo"])
    o["f_bo"] = rows(a["L1_attn_bo"], PT)
    inv = (1.0 / np.float32(10000.0) ** (np.arange(0, AD, 2, dtype=np.float32) / AD)).astype(np.float32)
    ang = np.arange(SEQ, dtype=np.float32)[:, None] * inv[None, :]
    ang = np.concatenate([ang, ang], axis=1)
    sign = np.where(np.arange(AD) < AF, -1.0, 1.0).astype(np.float32)
    o["f_cos"] = f(np.tile(np.cos(ang), (2, 1)))
    o["f_sin"] = f(np.tile(np.sin(ang) * sign, (2, 1)))
    diag = np.zeros((128 // AD, AD, 128 // AD, AF), np.float32)
    for i in range(128 // AD):
        diag[i, :, i, :] = a["L1_attn_rand_matrix"].T
    o["f_r"] = f(diag.reshape(128, -1))

    o["x_wq"] = chunked(a["L1_xattn_Wq"].T)
    o["x_nw"] = f(np.stack([a["L1_xattn_q_norm_w"], a["L1_xattn_k_norm_w"]], axis=1))
    o["x_wkv"] = chunked(np.concatenate([a["L1_xattn_Wk"], a["L1_xattn_Wv"]], axis=1).T)
    o["x_wo"] = chunked(a["L1_xattn_Wo"].T)
    o["x_ctxT"] = f(a["ctx_2048"].reshape(BATCH * NKS, KS, CC, 128).transpose(0, 3, 2, 1))

    o["r1_w"] = chunked(a["L1_ffn_W_r"])
    o["r1_b"] = rows(a["L1_ffn_b_r"], PT)
    o["l_a1"] = chunked(a["L1_ffn_A1"].reshape(E1 * R1, HID))
    o["l_w1"] = chunked(a["L1_ffn_W1"])
    pad = np.zeros((128 - E1 * R1, F1), np.float32)
    o["l_b1x"] = f(np.concatenate([a["L1_ffn_B1"].transpose(0, 2, 1).reshape(E1 * R1, F1), pad]))
    o["l_b1"] = f(a["L1_ffn_b1"].reshape(F1 // 128, 128).T)
    o["l_w2a2"] = chunked(np.concatenate([a["L1_ffn_W2"], a["L1_ffn_A2"].reshape(E1 * R1, F1)]))
    o["l_b2x"] = f(np.concatenate([a["L1_ffn_B2"].transpose(0, 2, 1).reshape(E1 * R1, HID), pad[:, 0:HID]]))
    o["l_b2"] = rows(a["L1_ffn_b2"], PT)
    return o


def kernel(**inputs):
    import concourse.bacc as _bacc
    from concourse.bass_utils import run_bass_kernel_spmd as _run

    arrays = lay_out(**inputs)
    nc = _bacc.Bacc("TRN2", target_bir_lowering=False, num_devices=1)
    t = {n: nc.dram_tensor(n, v.shape, mybir.dt.from_np(v.dtype), kind="ExternalInput").ap()
         for n, v in arrays.items()}
    out = nc.dram_tensor("out", (TOK, HID), F32, kind="ExternalOutput").ap()
    decoder(nc, t, out)
    r = _run(nc, [arrays], core_ids=[0])
    return r.results[0]["out"].reshape(BATCH, SEQ, HID)
```
